# Optimizing a Trainium2 kernel written in Bass

```python
import numpy as np
import jax
import jax.numpy as jnp

def _softmax(x, axis=-1):
    return jax.nn.softmax(x, axis=axis)

def _gelu(x):
    return jax.nn.gelu(x, approximate=True)

def _silu(x):
    return jax.nn.silu(x)

def _sigmoid(x):
    return jax.nn.sigmoid(x)

def _layernorm(x, axis=-1, eps=1e-05):
    m = jnp.mean(x, axis=axis, keepdims=True)
    v = jnp.var(x, axis=axis, keepdims=True)
    return (x - m) / jnp.sqrt(v + eps)

def _scatter_add(tgt, idx, src, axis=0):
    return tgt.at[idx].add(src)

def _segment_sum(src, seg, n):
    return jax.ops.segment_sum(src, seg, n)
kernel_name = 'mk_hybrid_d1_jaxref_r8_01a65c'

def setup_inputs(seed: int=0):
    np.random.seed(seed)
    _w = jnp.asarray

    def _L0_attn_a_setup():
        import jax, jax.numpy as jnp
        import numpy as np
        key = jax.random.key(seed)
        x = jax.random.normal(key, (8, 256, 128), dtype=jnp.float32)
        return {'x': x}
    _L0_attn_a_in = _L0_attn_a_setup()

    def _L0_attn_b_setup():
        import jax, jax.numpy as jnp
        import numpy as np
        from jax import lax
        B, N, C, RED = (8, 256, 128, 4)
        GN_EPS = 1e-05

        def _conv1d(x, w):
            return lax.conv_general_dilated(x, w, (1,), [(1, 1)], dimension_numbers=('NCH', 'OIH', 'NCH'))

        def _ode_func(A, conv1_w, gn_g, gn_b, conv2_w, conv2_b):
            h = _conv1d(A[:, None, :], conv1_w)
            b, _, n = h.shape
            hg = h.reshape(b, 2, 2, n)
            mu = hg.mean((2, 3), keepdims=True)
            var = hg.var((2, 3), keepdims=True)
            h = ((hg - mu) * lax.rsqrt(var + GN_EPS)).reshape(b, 4, n)
            h = jax.nn.relu(h * gn_g[None, :, None] + gn_b[None, :, None])
            y = _conv1d(h, conv2_w) + conv2_b[None, :, None]
            return y[:, 0, :]
        key = jax.random.key(seed)
        ks = jax.random.split(key, 8)
        s = lambda k, shp, sc: jax.random.normal(k, shp, jnp.float32) * sc
        return dict(x=jax.random.normal(ks[0], (B, N, C), jnp.float32), qkv_w=s(ks[1], (C, 3 * C), 0.02), c1=jnp.float32(0.01 ** 2), c2=jnp.float32(0.03 ** 2), conv1_w=s(ks[2], (4, 1, 3), 0.3), gn_g=jnp.ones(4, jnp.float32), gn_b=jnp.zeros(4, jnp.float32), conv2_w=s(ks[3], (1, 4, 3), 0.3), conv2_b=jnp.zeros(1, jnp.float32), ch_w1=s(ks[4], (C, C // RED), 0.02), ch_b1=jnp.zeros(C // RED, jnp.float32), ch_w2=s(ks[5], (C // RED, C), 0.02), ch_b2=jnp.zeros(C, jnp.float32), proj_w=s(ks[6], (C, C), 0.02), proj_b=jnp.zeros(C, jnp.float32))
    _L0_attn_b_in = _L0_attn_b_setup()

    def _L0_ffn_setup():
        import jax, jax.numpy as jnp
        import numpy as np
        DIM = 128
        DEPTH = 2
        HEADS = 8
        DIM_HEAD = 64
        WINDOW = 64
        INNER = HEADS * DIM_HEAD
        HID = int(DIM * 4 * 2 / 3)
        B, N = (2, 1024)
        QK_SCALE = 8.0

        def shift_token(t):
            t1, t2 = jnp.split(t, 2, axis=-1)
            t2 = jnp.pad(t2, ((0, 0), (1, 0), (0, 0)))[:, :-1]
            return jnp.concatenate([t1, t2], axis=-1)

        def l2norm(t):
            return t / jnp.clip(jnp.linalg.norm(t, axis=-1, keepdims=True), 1e-12)

        def rotate_half(x):
            x1, x2 = jnp.split(x, 2, axis=-1)
            return jnp.concatenate([-x2, x1], axis=-1)

        def rotary_xpos(q, k):
            n = q.shape[-2]
            half_idx = jnp.arange(0, DIM_HEAD, 2, dtype=jnp.float32)
            inv_freq = 1.0 / 10000.0 ** (half_idx / DIM_HEAD)
            t = jnp.arange(n, dtype=jnp.float32)
            freqs = t[:, None] * inv_freq[None, :]
            freqs = jnp.concatenate([freqs, freqs], axis=-1)
            base = (half_idx + 0.4 * DIM_HEAD) / (1.4 * DIM_HEAD)
            power = (t - n // 2) / float(WINDOW // 2)
            scale = base[None, :] ** power[:, None]
            scale = jnp.concatenate([scale, scale], axis=-1)
            cos, sin = (jnp.cos(freqs), jnp.sin(freqs))
            q = q * cos * scale + rotate_half(q) * sin * scale
            k = k * cos / scale + rotate_half(k) * sin / scale
            return (q, k)

        def local_attention(q, k, v):
            b, h, n, d = q.shape
            w = n // WINDOW
            bq = q.reshape(b, h, w, WINDOW, d) * QK_SCALE
            bk = k.reshape(b, h, w, WINDOW, d)
            bv = v.reshape(b, h, w, WINDOW, d)

            def look_around(t):
                p = jnp.pad(t, ((0, 0), (0, 0), (1, 0), (0, 0), (0, 0)))
                return jnp.concatenate([p[:, :, :w], p[:, :, 1:]], axis=3)
            bk, bv = (look_around(bk), look_around(bv))
            bt = jnp.arange(n).reshape(w, WINDOW)
            btp = jnp.pad(bt, ((1, 0), (0, 0)), constant_values=-1)
            btk = jnp.concatenate([btp[:w], btp[1:]], axis=1)
            sim = jnp.einsum('bhwid,bhwjd->bhwij', bq, bk)
            i = bt[:, :, None]
            j = btk[:, None, :]
            mask = (i < j) | (i > j + WINDOW) | (j == -1)
            sim = jnp.where(mask, -jnp.finfo(sim.dtype).max, sim)
            attn = jax.nn.softmax(sim, axis=-1)
            out = jnp.einsum('bhwij,bhwjd->bhwid', attn, bv)
            return out.reshape(b, h, n, d)

        def _layer(x, wqkv, qs, ksc, wo, lg, lb, w1, b1, w2, b2):
            b, n, _ = x.shape
            h = shift_token(x)
            qkv = h @ wqkv
            q, k, v = jnp.split(qkv, 3, axis=-1)
            to_heads = lambda t: t.reshape(b, n, HEADS, DIM_HEAD).transpose(0, 2, 1, 3)
            q, k, v = (to_heads(q), to_heads(k), to_heads(v))
            q = l2norm(q) * qs
            k = l2norm(k) * ksc
            q, k = rotary_xpos(q, k)
            o = local_attention(q, k, v)
            o = o.transpose(0, 2, 1, 3).reshape(b, n, INNER)
            x = x + o @ wo
            h = shift_token(x)
            mu = h.mean(-1, keepdims=True)
            var = h.var(-1, keepdims=True)
            h = (h - mu) / jnp.sqrt(var + 1e-05) * lg + lb
            h = h @ w1 + b1
            a, g = jnp.split(h, 2, axis=-1)
            h = a * jax.nn.gelu(g, approximate=False)
            x = x + h @ w2 + b2
            return x
        key = jax.random.key(seed)
        ks = jax.random.split(key, 6)
        return {'x': jax.random.normal(ks[0], (B, N, DIM), jnp.float32), 'wqkv': jax.random.normal(ks[1], (DEPTH, DIM, 3 * INNER), jnp.float32) * 0.02, 'q_scale': jnp.ones((DEPTH, DIM_HEAD), jnp.float32), 'k_scale': jnp.ones((DEPTH, DIM_HEAD), jnp.float32), 'wo': jax.random.normal(ks[2], (DEPTH, INNER, DIM), jnp.float32) * 0.02, 'ln_g': jnp.ones((DEPTH, DIM), jnp.float32), 'ln_b': jnp.zeros((DEPTH, DIM), jnp.float32), 'w1': jax.random.normal(ks[3], (DEPTH, DIM, 2 * HID), jnp.float32) * 0.02, 'b1': jnp.zeros((DEPTH, 2 * HID), jnp.float32), 'w2': jax.random.normal(ks[4], (DEPTH, HID, DIM), jnp.float32) * 0.02, 'b2': jnp.zeros((DEPTH, DIM), jnp.float32)}
    _L0_ffn_in = _L0_ffn_setup()
    _d = {'L0_attn_a_x': _L0_attn_a_in['x'], 'L0_attn_b_qkv_w': _L0_attn_b_in['qkv_w'], 'L0_attn_b_c1': _L0_attn_b_in['c1'], 'L0_attn_b_c2': _L0_attn_b_in['c2'], 'L0_attn_b_conv1_w': _L0_attn_b_in['conv1_w'], 'L0_attn_b_gn_g': _L0_attn_b_in['gn_g'], 'L0_attn_b_gn_b': _L0_attn_b_in['gn_b'], 'L0_attn_b_conv2_w': _L0_attn_b_in['conv2_w'], 'L0_attn_b_conv2_b': _L0_attn_b_in['conv2_b'], 'L0_attn_b_ch_w1': _L0_attn_b_in['ch_w1'], 'L0_attn_b_ch_b1': _L0_attn_b_in['ch_b1'], 'L0_attn_b_ch_w2': _L0_attn_b_in['ch_w2'], 'L0_attn_b_ch_b2': _L0_attn_b_in['ch_b2'], 'L0_attn_b_proj_w': _L0_attn_b_in['proj_w'], 'L0_attn_b_proj_b': _L0_attn_b_in['proj_b'], 'L0_ffn_wqkv': _L0_ffn_in['wqkv'], 'L0_ffn_q_scale': _L0_ffn_in['q_scale'], 'L0_ffn_k_scale': _L0_ffn_in['k_scale'], 'L0_ffn_wo': _L0_ffn_in['wo'], 'L0_ffn_ln_g': _L0_ffn_in['ln_g'], 'L0_ffn_ln_b': _L0_ffn_in['ln_b'], 'L0_ffn_w1': _L0_ffn_in['w1'], 'L0_ffn_b1': _L0_ffn_in['b1'], 'L0_ffn_w2': _L0_ffn_in['w2'], 'L0_ffn_b2': _L0_ffn_in['b2']}
    _x0 = _d['L0_attn_a_x']
    _d['L0_attn_a_x'] = jax.random.normal(jax.random.fold_in(jax.random.key(seed), 1), (2, 2048, 128), dtype=_x0.dtype)
    del _x0
    return _d

def reference(L0_attn_a_x, L0_attn_b_qkv_w, L0_attn_b_c1, L0_attn_b_c2, L0_attn_b_conv1_w, L0_attn_b_gn_g, L0_attn_b_gn_b, L0_attn_b_conv2_w, L0_attn_b_conv2_b, L0_attn_b_ch_w1, L0_attn_b_ch_b1, L0_attn_b_ch_w2, L0_attn_b_ch_b2, L0_attn_b_proj_w, L0_attn_b_proj_b, L0_ffn_wqkv, L0_ffn_q_scale, L0_ffn_k_scale, L0_ffn_wo, L0_ffn_ln_g, L0_ffn_ln_b, L0_ffn_w1, L0_ffn_b1, L0_ffn_w2, L0_ffn_b2):

    def _L0_attn_a_ref(x):
        import jax, jax.numpy as jnp
        import numpy as np
        scores = jnp.einsum('bld,bmd->blm', x, x)
        scores = jax.nn.softmax(scores, axis=1)
        return jnp.einsum('blm,bmd->bld', scores, x)

    def _L0_attn_b_ref(x, qkv_w, c1, c2, conv1_w, gn_g, gn_b, conv2_w, conv2_b, ch_w1, ch_b1, ch_w2, ch_b2, proj_w, proj_b):
        import jax, jax.numpy as jnp
        import numpy as np
        from jax import lax
        B, N, C, RED = (8, 256, 128, 4)
        GN_EPS = 1e-05

        def _conv1d(x, w):
            return lax.conv_general_dilated(x, w, (1,), [(1, 1)], dimension_numbers=('NCH', 'OIH', 'NCH'))

        def _ode_func(A, conv1_w, gn_g, gn_b, conv2_w, conv2_b):
            h = _conv1d(A[:, None, :], conv1_w)
            b, _, n = h.shape
            hg = h.reshape(b, 2, 2, n)
            mu = hg.mean((2, 3), keepdims=True)
            var = hg.var((2, 3), keepdims=True)
            h = ((hg - mu) * lax.rsqrt(var + GN_EPS)).reshape(b, 4, n)
            h = jax.nn.relu(h * gn_g[None, :, None] + gn_b[None, :, None])
            y = _conv1d(h, conv2_w) + conv2_b[None, :, None]
            return y[:, 0, :]
        Bx, Nx, Cx = x.shape
        qkv = (x @ qkv_w).reshape(Bx, Nx, 3, Cx)
        q, k, v = (qkv[..., 0, :], qkv[..., 1, :], qkv[..., 2, :])
        mu_q = q.mean(-1, keepdims=True)
        mu_k = k.mean(-1, keepdims=True)
        dq, dk = (q - mu_q, k - mu_k)
        inv_cm1 = 1.0 / (Cx - 1)
        sigma_qk = (dq * dk).sum(-1, keepdims=True) * inv_cm1
        sigma_q2 = (dq * dq).sum(-1, keepdims=True) * inv_cm1
        sigma_k2 = (dk * dk).sum(-1, keepdims=True) * inv_cm1
        num = (2 * mu_q * mu_k + c1) * (2 * sigma_qk + c2)
        den = (mu_q ** 2 + mu_k ** 2 + c1) * (sigma_q2 + sigma_k2 + c2)
        attn_base = ((num / (den + 1e-07)) ** 2)[..., 0]
        steps = 2
        ts = jnp.linspace(0.0, 1.0, steps)
        dts = ts[1:] - ts[:-1]

        def step(A, dt):
            return (A + dt * _ode_func(A, conv1_w, gn_g, gn_b, conv2_w, conv2_b), None)
        A, _ = lax.scan(step, attn_base, dts)
        final_a = jax.nn.sigmoid(A)
        weights = jax.nn.softmax(final_a, axis=1)
        m = x.mean(axis=1, keepdims=True)
        ch_w = jax.nn.sigmoid(jax.nn.relu(m @ ch_w1 + ch_b1) @ ch_w2 + ch_b2)
        out_low = weights[..., None] * v * ch_w
        return out_low @ proj_w + proj_b

    def _L0_ffn_ref(x, wqkv, q_scale, k_scale, wo, ln_g, ln_b, w1, b1, w2, b2):
        import jax, jax.numpy as jnp
        import numpy as np
        DIM = 128
        DEPTH = 2
        HEADS = 8
        DIM_HEAD = 64
        WINDOW = 64
        INNER = HEADS * DIM_HEAD
        HID = int(DIM * 4 * 2 / 3)
        B, N = (2, 1024)
        QK_SCALE = 8.0

        def shift_token(t):
            t1, t2 = jnp.split(t, 2, axis=-1)
            t2 = jnp.pad(t2, ((0, 0), (1, 0), (0, 0)))[:, :-1]
            return jnp.concatenate([t1, t2], axis=-1)

        def l2norm(t):
            return t / jnp.clip(jnp.linalg.norm(t, axis=-1, keepdims=True), 1e-12)

        def rotate_half(x):
            x1, x2 = jnp.split(x, 2, axis=-1)
            return jnp.concatenate([-x2, x1], axis=-1)

        def rotary_xpos(q, k):
            n = q.shape[-2]
            half_idx = jnp.arange(0, DIM_HEAD, 2, dtype=jnp.float32)
            inv_freq = 1.0 / 10000.0 ** (half_idx / DIM_HEAD)
            t = jnp.arange(n, dtype=jnp.float32)
            freqs = t[:, None] * inv_freq[None, :]
            freqs = jnp.concatenate([freqs, freqs], axis=-1)
            base = (half_idx + 0.4 * DIM_HEAD) / (1.4 * DIM_HEAD)
            power = (t - n // 2) / float(WINDOW // 2)
            scale = base[None, :] ** power[:, None]
            scale = jnp.concatenate([scale, scale], axis=-1)
            cos, sin = (jnp.cos(freqs), jnp.sin(freqs))
            q = q * cos * scale + rotate_half(q) * sin * scale
            k = k * cos / scale + rotate_half(k) * sin / scale
            return (q, k)

        def local_attention(q, k, v):
            b, h, n, d = q.shape
            w = n // WINDOW
            bq = q.reshape(b, h, w, WINDOW, d) * QK_SCALE
            bk = k.reshape(b, h, w, WINDOW, d)
            bv = v.reshape(b, h, w, WINDOW, d)

            def look_around(t):
                p = jnp.pad(t, ((0, 0), (0, 0), (1, 0), (0, 0), (0, 0)))
                return jnp.concatenate([p[:, :, :w], p[:, :, 1:]], axis=3)
            bk, bv = (look_around(bk), look_around(bv))
            bt = jnp.arange(n).reshape(w, WINDOW)
            btp = jnp.pad(bt, ((1, 0), (0, 0)), constant_values=-1)
            btk = jnp.concatenate([btp[:w], btp[1:]], axis=1)
            sim = jnp.einsum('bhwid,bhwjd->bhwij', bq, bk)
            i = bt[:, :, None]
            j = btk[:, None, :]
            mask = (i < j) | (i > j + WINDOW) | (j == -1)
            sim = jnp.where(mask, -jnp.finfo(sim.dtype).max, sim)
            attn = jax.nn.softmax(sim, axis=-1)
            out = jnp.einsum('bhwij,bhwjd->bhwid', attn, bv)
            return out.reshape(b, h, n, d)

        def _layer(x, wqkv, qs, ksc, wo, lg, lb, w1, b1, w2, b2):
            b, n, _ = x.shape
            h = shift_token(x)
            qkv = h @ wqkv
            q, k, v = jnp.split(qkv, 3, axis=-1)
            to_heads = lambda t: t.reshape(b, n, HEADS, DIM_HEAD).transpose(0, 2, 1, 3)
            q, k, v = (to_heads(q), to_heads(k), to_heads(v))
            q = l2norm(q) * qs
            k = l2norm(k) * ksc
            q, k = rotary_xpos(q, k)
            o = local_attention(q, k, v)
            o = o.transpose(0, 2, 1, 3).reshape(b, n, INNER)
            x = x + o @ wo
            h = shift_token(x)
            mu = h.mean(-1, keepdims=True)
            var = h.var(-1, keepdims=True)
            h = (h - mu) / jnp.sqrt(var + 1e-05) * lg + lb
            h = h @ w1 + b1
            a, g = jnp.split(h, 2, axis=-1)
            h = a * jax.nn.gelu(g, approximate=False)
            x = x + h @ w2 + b2
            return x
        for l in range(DEPTH):
            x = _layer(x, wqkv[l], q_scale[l], k_scale[l], wo[l], ln_g[l], ln_b[l], w1[l], b1[l], w2[l], b2[l])
        return x
    x = L0_attn_a_x
    x = x + _L0_attn_a_ref(_layernorm(x, axis=-1))
    x = x + _L0_ffn_ref(_layernorm(x, axis=-1), L0_ffn_wqkv, L0_ffn_q_scale, L0_ffn_k_scale, L0_ffn_wo, L0_ffn_ln_g, L0_ffn_ln_b, L0_ffn_w1, L0_ffn_b1, L0_ffn_w2, L0_ffn_b2)
    x = x + _L0_attn_b_ref(_layernorm(x, axis=-1), L0_attn_b_qkv_w, L0_attn_b_c1, L0_attn_b_c2, L0_attn_b_conv1_w, L0_attn_b_gn_g, L0_attn_b_gn_b, L0_attn_b_conv2_w, L0_attn_b_conv2_b, L0_attn_b_ch_w1, L0_attn_b_ch_b1, L0_attn_b_ch_w2, L0_attn_b_ch_b2, L0_attn_b_proj_w, L0_attn_b_proj_b)
    x = x + _L0_ffn_ref(_layernorm(x, axis=-1), L0_ffn_wqkv, L0_ffn_q_scale, L0_ffn_k_scale, L0_ffn_wo, L0_ffn_ln_g, L0_ffn_ln_b, L0_ffn_w1, L0_ffn_b1, L0_ffn_w2, L0_ffn_b2)
    return x

_drawn_inputs = setup_inputs


def setup_inputs(seed=0):
    import zlib

    import numpy as np

    out = dict(_drawn_inputs(seed))
    spreads = {'L0_attn_b_gn_g': (1.0, 0.6),
     'L0_attn_b_gn_b': (0.0, 2.0),
     'L0_attn_b_ch_b1': (0.0, 2.0),
     'L0_attn_b_ch_b2': (0.0, 2.0),
     'L0_attn_b_proj_b': (0.0, 0.505),
     'L0_ffn_q_scale': (1.0, 0.6),
     'L0_ffn_k_scale': (1.0, 0.6),
     'L0_ffn_ln_g': (1.0, 0.6),
     'L0_ffn_ln_b': (0.0, 0.8),
     'L0_ffn_b1': (0.0, 0.8),
     'L0_ffn_b2': (0.0, 0.1)}
    factors = {'L0_attn_b_qkv_w': 200.0,
     'L0_attn_b_conv1_w': 200.0,
     'L0_attn_b_conv2_w': 200.0,
     'L0_attn_b_ch_w1': 200.0,
     'L0_attn_b_ch_w2': 200.0,
     'L0_attn_b_proj_w': 200.0,
     'L0_ffn_wqkv': 3.478,
     'L0_ffn_wo': 3.427,
     'L0_ffn_w1': 5.299,
     'L0_ffn_w2': 5.219}
    for name, (base, spread) in spreads.items():
        noise = np.random.default_rng([zlib.crc32(name.encode()), seed]).standard_normal(out[name].shape)
        drawn = base * np.exp(spread * noise) if base else spread * noise
        out[name] = jnp.asarray(drawn.astype(out[name].dtype))
    for name, factor in factors.items():
        out[name] = (out[name] * factor).astype(out[name].dtype)
    return out
```

```python
from contextlib import ExitStack

import numpy as np

import concourse.bass as bass
from concourse import mybir

F32 = mybir.dt.float32
BF16 = mybir.dt.bfloat16
ALU = mybir.AluOpType
ACT = mybir.ActivationFunctionType
AX = mybir.AxisListType

NB, N, D = 2, 2048, 128
NT = N // 128
NH, DH, W = 8, 64, 64
HID = 341
CW = [114, 114, 113]
C0 = [0, 114, 228]
CH = 512
NCH = NB * N // CH
EPS = 1e-5
NEG = -1e30


class Op:

    def __init__(self, eng, fn, waits):
        self.eng, self.fn, self.waits, self.mark, self.table = eng, fn, waits, None, False


class Load:

    def __init__(self, sem, value):
        self.sem, self.value = sem, value


class Queues:

    def __init__(self):
        self.q = {e: [] for e in ("sync", "tensor", "vector", "scalar", "gpsimd")}
        self.dma_sems = 0

    def op(self, eng, fn, *waits):
        flat = []
        todo = list(waits)
        while todo:
            w = todo.pop()
            if w is None:
                continue
            if isinstance(w, (list, tuple)):
                todo += w
            else:
                flat.append(w)
        o = Op(eng, fn, flat)
        self.q[eng].append(o)
        return o

    def last(self):
        return [[o for o in q if not o.table][-1:] for e, q in self.q.items() if e != "sync"]

    def emit(self, block, sems):
        for q in self.q.values():
            for o in q:
                for w in o.waits:
                    if isinstance(w, Op):
                        w.mark = 0
        for e, q in self.q.items():
            n = 0
            for o in q:
                if o.mark is not None and not isinstance(o.fn, Load):
                    n += 1
                    o.mark = n

        def run(eng, name):
            seen = {}
            for o in self.q[name]:
                for w in o.waits:
                    key, value = (w.eng, w.mark) if isinstance(w, Op) else (id(w.sem), w.value)
                    if seen.get(key, 0) >= value:
                        continue
                    seen[key] = value
                    eng.wait_ge(sems[w.eng] if isinstance(w, Op) else w.sem, value)
                ins = o.fn(eng)
                if o.mark is not None:
                    ins.then_inc(sems[name], 1)

        block.sync(lambda eng: run(eng, "sync"))
        block.tensor(lambda eng: run(eng, "tensor"))
        block.vector(lambda eng: run(eng, "vector"))
        block.scalar(lambda eng: run(eng, "scalar"))
        block.gpsimd(lambda eng: run(eng, "gpsimd"))


class Ring:

    def __init__(self, n, start=None):
        self.n, self.i, self.held = n, 0, [start] * n

    def take(self):
        k = self.i % self.n
        self.i += 1
        return k, self.held[k]

    def free(self, k, *ops):
        self.held[k] = list(ops)


def build(nc, a, out):
    ctx = ExitStack()
    with ctx:
        def sb(name, shape, dt=F32):
            return ctx.enter_context(nc.sbuf_tensor(name, shape, dt))

        def sem(name):
            return ctx.enter_context(nc.semaphore(name))

        sems = {e: sem("c_" + e) for e in ("sync", "tensor", "vector", "scalar", "gpsimd")}
        Q = Queues()

        def T(fn, *w):
            return Q.op("tensor", fn, *w)

        def V(fn, *w):
            return Q.op("vector", fn, *w)

        def A(fn, *w):
            return Q.op("scalar", fn, *w)

        def G(fn, *w):
            return Q.op("gpsimd", fn, *w)

        def tables():
            A(lambda e: e.preload_act_table_set("natural_log_exp_and_others")).table = True

        n_loads = [0]

        def load(pairs, *w):
            s = sem(f"d{n_loads[0]}")
            n_loads[0] += 1
            for dst, src in pairs:
                Q.op("sync", lambda e, dst=dst, src=src: e.dma_start(dst, src).then_inc(s, 16), *w)
                w = ()
            return Load(s, 16 * len(pairs))

        xT = sb("xT", [128, NB, N])
        yT = sb("yT", [128, NB, N])
        HT = sb("HT", [128, NB, N + 4])
        TB = sb("TB", [128, 2, 2, NT, 2, DH])
        wqkv = sb("wqkv", [128, 3 * NH * DH])
        wo = sb("wo", [128, 4, D])
        w1 = sb("w1", [128, 2 * HID])
        w1g = sb("w1g", [128, 2 * HID])
        w2 = sb("w2", [114, 3, D])
        wb = sb("wb", [128, 3 * D])
        wp = sb("wp", [128, D])
        cw1 = sb("cw1", [128, 32])
        cw2 = sb("cw2", [32, D])
        cst = sb("cst", [128, 7, 128])
        mk = sb("mk", [128, 3, 384], BF16)
        idb = sb("idb", [128, 128], BF16)
        sel = sb("sel", [8, 8, 128], BF16)
        qks = sb("qks", [128, 2, 2, DH])
        b1c = sb("b1c", [114, 2, 6])
        b1r = sb("b1r", [114, 6])
        vec = sb("vec", [128, 64])
        tiny = sb("tiny", [128, 1])
        cstv = sb("cstv", [128, 4])
        AR = sb("AR", [128, 24700])
        ident, cen, avg, sdn, sup, edn, eup = (cst[:, i, :] for i in range(7))
        PS = ctx.enter_context(nc.psum_tensor("PS", [128, 8, 512], F32))

        at = [0]

        def arena(n, shape, dt=F32, parts=128):
            ap = AR[0:parts, at[0]:at[0] + n]
            at[0] += n
            assert at[0] <= 24700, at[0]
            if dt is not F32:
                ap = ap.bitcast(dt)
            if len(shape) == 2:
                ap = ap.rearrange("p (a b) -> p a b", b=shape[1])
            elif len(shape) == 3:
                ap = ap.rearrange("p (a b c) -> p a b c", b=shape[1], c=shape[2])
            elif len(shape) == 4:
                ap = ap.rearrange("p (a b c d) -> p a b c d", b=shape[1], c=shape[2], d=shape[3])
            return ap

        xtok = HT[:, :, :].rearrange("p b n -> p (b n)")[:, 0:NB * N].rearrange("p (t d) -> p t d", d=D)
        xd = a["L0_attn_a_x"].rearrange("b (t p) d -> p (b t) d", p=128)
        ld_cst = load([(cst[:, :, :], a["c_f32"])])
        ld_x = [load([(xtok[:, 8 * i:8 * i + 8, :], xd[:, 8 * i:8 * i + 8, :])]) for i in range(4)]
        mkf = AR[:, 0:1152]
        idf = AR[:, 1152:1280]
        self32 = AR[0:8, 1280:2304]
        ld_mk = load([(mkf, a["c_mask"]), (self32, a["c_sel"])])
        bc = lambda ap, n: ap.rearrange("(o n) -> o n", o=1).to_broadcast([128, n])
        ld_tb = load([(TB[:, 1, :, :, :, :].rearrange("p a b c d -> p (a b c d)"), a["c_rope"]),
                      (qks[:, :, 0, :], a["L0_ffn_q_scale"].rearrange("(o l) d -> o l d", o=1).to_broadcast([128, 2, DH])),
                      (qks[:, :, 1, :], a["L0_ffn_k_scale"].rearrange("(o l) d -> o l d", o=1).to_broadcast([128, 2, DH]))])
        col = lambda ap: ap.rearrange("(p o) -> p o", o=1)
        small = []
        for l in range(2):
            small += [(vec[:, l:l + 1], col(a["L0_ffn_ln_g"][l])), (vec[:, 2 + l:3 + l], col(a["L0_ffn_ln_b"][l])),
                      (vec[:, 4 + l:5 + l], col(a["L0_ffn_b2"][l]))]
            for g in range(2):
                for i in range(3):
                    s0 = HID * g + C0[i]
                    small.append((b1c[0:CW[i], l, 3 * g + i:3 * g + i + 1], col(a["L0_ffn_b1"][l, s0:s0 + CW[i]])))
        small += [(vec[:, 6:7], col(a["L0_attn_b_proj_b"])), (vec[:, 7:8], col(a["L0_attn_b_ch_b2"])),
                  (vec[0:32, 8:9], col(a["L0_attn_b_ch_b1"])),
                  (vec[:, 9:10], bc(a["L0_attn_b_c1"], 1)), (vec[:, 10:11], bc(a["L0_attn_b_c2"], 1)),
                  (vec[:, 12:24], bc(a["L0_attn_b_conv1_w"].rearrange("a b c -> (a b c)"), 12)),
                  (vec[:, 24:28], bc(a["L0_attn_b_gn_g"], 4)), (vec[:, 28:32], bc(a["L0_attn_b_gn_b"], 4)),
                  (vec[:, 32:44], bc(a["L0_attn_b_conv2_w"].rearrange("a b c -> (a b c)"), 12)),
                  (vec[:, 44:45], bc(a["L0_attn_b_conv2_b"], 1)),
                  (wb[:, :], a["L0_attn_b_qkv_w"]), (wp[:, :], a["L0_attn_b_proj_w"]),
                  (cw1[:, :], a["L0_attn_b_ch_w1"]), (cw2[:, :], a["L0_attn_b_ch_w2"])]
        ld_small = load(small)
        wait_attn_w = [None]
        wait_ffn_w = [None]

        def load_attn_w(l, *w):
            wait_attn_w[0] = load([(wqkv[:, :], a["L0_ffn_wqkv"][l]),
                                   (wo[:, :, :], a["L0_ffn_wo"][l].rearrange("(c p) d -> p c d", p=128))], *w)

        def load_ffn_w(l, *w):
            wait_ffn_w[0] = load([(w1[:, :], a["L0_ffn_w1"][l])] +
                                 [(w2[0:CW[i], i, :], a["L0_ffn_w2"][l, C0[i]:C0[i] + CW[i], :]) for i in range(3)], *w)

        load_attn_w(0)
        load_ffn_w(0)

        tables()
        t0 = V(lambda e: e.tensor_copy(mk[:, :, :].rearrange("p a b -> p (a b)"), mkf), ld_mk)
        t1 = V(lambda e: e.tensor_copy(idb[:, :], ident), ld_cst)
        t2 = V(lambda e: e.tensor_copy(sel[:, :, :].rearrange("p a b -> p (a b)"), self32), ld_mk)
        t3 = V(lambda e: e.memset(cstv[:, 0:1], EPS))
        t4 = V(lambda e: e.memset(cstv[:, 1:2], -64.0))
        k_consts = [t0, t1, t2, t3, t4]
        tb_ready = []
        for l in range(2):
            for c in range(2):
                dst = TB[:, l, c, :, :, :]
                src = TB[:, 1, c, :, :, :]
                sc = qks[:, l, :, :].rearrange("p a b -> p (a b)")[:, None, :].to_broadcast([128, NT, 2 * DH])
                d2 = dst.rearrange("p t a b -> p t (a b)")
                s2 = src.rearrange("p t a b -> p t (a b)")
                tb_ready.append(G(lambda e, d2=d2, s2=s2, sc=sc: e.tensor_tensor(d2, s2, sc, ALU.mult),
                                  ld_tb, tb_ready[-2:]))
        eps_ap = cstv[:, 0:1]

        def barrier():
            return Q.last()

        ring = Ring(8)
        x_parts = []
        for g in range(8):
            k, held = ring.take()
            for j in range(4):
                mm = T(lambda e, g=g, j=j, k=k: e.transpose(PS[:, k, j * 128:(j + 1) * 128], xtok[:, 4 * g + j, :], ident),
                       ld_cst, ld_x[g // 2], held)
            dst = xT[:, g // 4, (g % 4) * 512:(g % 4 + 1) * 512]
            x_parts.append(V(lambda e, k=k, dst=dst: e.tensor_copy(dst, PS[:, k, :]), mm))

        def chunk(t, c):
            return t[:, c // 4, (c % 4) * CH:(c % 4 + 1) * CH]

        def layernorm(src, dst, ready, free):
            sq = [arena(CH, [CH]) for _ in range(3)]
            rs = [arena(CH, [CH]) for _ in range(3)]
            ps, rsq, rrs = Ring(8, free), Ring(3, free), Ring(3, free)
            done = []
            held = []
            for c in range(NCH + 1):
                if c < NCH:
                    kc, h = ps.take()
                    m1 = T(lambda e, c=c, kc=kc: e.matmul(PS[:, kc, :], cen, chunk(src, c), start=True, stop=True),
                           ready[c], h)
                    ks, h = rsq.take()
                    s1 = A(lambda e, kc=kc, ks=ks: e.activation(sq[ks], PS[:, kc, :], ACT.Square), m1, h)
                    held.append((c, kc, ks, s1))
                if c >= 1:
                    cc, kc, ks, s1 = held[c - 1]
                    kv, h = ps.take()
                    m2 = T(lambda e, kv=kv, ks=ks: e.matmul(PS[:, kv, :], avg, sq[ks], start=True, stop=True), s1, h)
                    rsq.free(ks, m2)
                    kr, h = rrs.take()
                    s2 = A(lambda e, kv=kv, kr=kr: e.activation(rs[kr], PS[:, kv, :], ACT.Ln, bias=eps_ap), m2, h, t3)
                    ps.free(kv, s2)
                    s3 = A(lambda e, kr=kr: e.activation(rs[kr], rs[kr], ACT.Exp, scale=-0.5), s2)
                    v = V(lambda e, cc=cc, kc=kc, kr=kr: e.tensor_tensor(chunk(dst, cc), PS[:, kc, :], rs[kr], ALU.mult), s3)
                    ps.free(kc, v)
                    rrs.free(kr, v)
                    done.append(v)
            return done

        def self_attention(ready):
            at[0] = 0
            bar = barrier()
            ntok = arena(NT * 128, [NT, 128])
            nsc = [arena(128, [128]) for _ in range(2)]
            E = [arena(N, [N]) for _ in range(2)]
            zz = arena(8, [8])
            out_ops = []
            def sequence(b):
                tr = []
                for g in range(4):
                    for j in range(4):
                        t = 4 * g + j
                        mm = T(lambda e, g=g, j=j, t=t: e.transpose(PS[:, 4 + g, j * 128:(j + 1) * 128],
                                                                 yT[:, b, t * 128:(t + 1) * 128], ident),
                               bar, ready, out_ops[-4:])
                    tr.append(V(lambda e, g=g: e.tensor_copy(ntok[:, 4 * g:4 * g + 4, :].rearrange("p a b -> p (a b)"),
                                                            PS[:, 4 + g, :]), mm, bar))
                ex = {}
                pv = {}
                scl = {}

                def scores(m):
                    for h in range(2):
                        for j in range(2):
                            mm = T(lambda e, h=h, j=j: e.matmul(PS[:, 2 * h + j, :], yT[:, b, m * 128:(m + 1) * 128],
                                                                yT[:, b, (2 * h + j) * 512:(2 * h + j + 1) * 512],
                                                                start=True, stop=True), ex.get((m - 1, h)), bar)
                        ex[m, h] = A(lambda e, h=h: e.activation(
                            E[m % 2][:, h * 1024:(h + 1) * 1024], PS[:, 2 * h:2 * h + 2, :].rearrange("p a b -> p (a b)"),
                            ACT.Exp, bias=cstv[:, 1:2], accum_out=zz[:, 2 * (m % 2) + h:2 * (m % 2) + h + 1]),
                            mm, pv.get(m - 2), scl.get(m - 2), t4, bar, out_ops[-4:])
                    q = m % 2
                    s = V(lambda e: e.tensor_tensor(zz[:, 4 + q:5 + q], zz[:, 2 * q:2 * q + 1], zz[:, 2 * q + 1:2 * q + 2],
                                                    ALU.add), ex[m, 0], ex[m, 1], scl.get(m - 2))
                    r = V(lambda e: e.reciprocal(zz[:, 6 + q:7 + q], zz[:, 4 + q:5 + q]), s)
                    scl[m] = V(lambda e: e.tensor_scalar(nsc[q], ntok[:, m, :], zz[:, 6 + q:7 + q], None, ALU.mult),
                               r, tr[m // 4], pv.get(m - 2), bar)

                def weighted(m):
                    for j in range(4):
                        mm = T(lambda e, j=j: e.matmul(PS[:, 4 + j, :], nsc[m % 2], E[m % 2][:, j * 512:(j + 1) * 512],
                                                       start=(m == 0), stop=(m == NT - 1)), scl[m], tr, bar)
                    pv[m] = mm

                for m in range(NT + 1):
                    if m < NT:
                        scores(m)
                    if m >= 1:
                        weighted(m - 1)
                for j in range(4):
                    dst = xT[:, b, j * 512:(j + 1) * 512]
                    out_ops.append(V(lambda e, j=j, dst=dst: e.tensor_tensor(dst, PS[:, 4 + j, :], dst, ALU.add),
                                     pv[NT - 1]))
            for b in range(NB):
                sequence(b)
            return out_ops

        def shift(ready, free):
            done = []
            z = V(lambda e: e.memset(HT[64:128, :, 0:1], 0.0), free)
            for c in range(NCH):
                b, n0 = c // 4, (c % 4) * CH
                v1 = V(lambda e, b=b, n0=n0: e.tensor_copy(HT[0:64, b, n0:n0 + CH], yT[0:64, b, n0:n0 + CH]), ready[c], free)
                v2 = V(lambda e, b=b, n0=n0: e.tensor_copy(HT[64:128, b, n0 + 1:n0 + 1 + CH], yT[64:128, b, n0:n0 + CH]),
                       ready[c], free)
                done.append([v1, v2, z] + ([done[-1][1]] if c % 4 else []))
            return done

        def local_attention(l, h_ready):
            at[0] = 0
            bar = barrier()
            sq = arena(1024, [NH * 2, DH])
            qn = arena(1024, [NH * 2, DH])
            ta = [arena(1024, [NH * 2, DH]) for _ in range(2)]
            tc = arena(1024, [NH * 2, DH])
            ss = arena(64, [2, 32])
            RQ = 8
            qT = arena(4 * (RQ * 128 + 64), [4, RQ * 128 + 64])
            kT = [arena(512, [4, 128]) for _ in range(4)]
            kB = arena(2 * (N + 64), [4, N + 64], BF16)
            qB = [arena(256, [4, 128], BF16) for _ in range(2)]
            va = [arena(1024, [4, 256]) for _ in range(2)]
            PT = [arena(384, [2, 192]) for _ in range(3)]
            ND = [[arena(768, [2, 2, 192]) for _ in range(2)] for _ in range(2)]
            mx = [arena(8, [8]) for _ in range(2)]
            mT = arena((RQ * 128 + 64) // 2, [RQ * 128 + 64], BF16, 8)
            lnd = [arena(256, [2, 128]) for _ in range(2)]
            ot = [arena(512, [4, 128]) for _ in range(2)]
            ones = [V(lambda e, i=i: e.memset(va[i][:, :, 64:192], 1.0), bar) for i in range(2)]
            zk = V(lambda e: e.memset(kB[:, :, 0:64], 0.0), bar)
            ra, rm, rs, rv = Ring(2, bar), Ring(2, bar), Ring(2, bar), Ring(2, bar)
            rqn, rta, rtc, rsq, rss = Ring(1, bar), Ring(2, bar), Ring(1, bar), Ring(1, bar), Ring(2, bar)
            rkT, rqB, rva, rPT, rmx, rlnd, rot = (Ring(4, bar), Ring(2, bar), Ring(2, bar), Ring(3, bar), Ring(2, bar),
                                                  Ring(2, bar), Ring(2, bar))
            R = {}
            tiles = [(b, t) for b in range(NB) for t in range(NT)]
            nt = len(tiles)

            def project(i):
                b, t = tiles[i]
                ops = []
                banks = []
                for x in range(2):
                    k, h = ra.take()
                    ops.append(T(lambda e, x=x, k=k: e.matmul(PS[:, k, :], HT[:, b, t * 128:(t + 1) * 128],
                                                              wqkv[:, x * 512:(x + 1) * 512], start=True, stop=True),
                                 h, h_ready[i // 4], wait_attn_w[0], bar))
                    banks.append(k)
                R["p", i] = (ops, banks)
                ks, h = rsq.take()
                kss, h2 = rss.take()
                a1 = [A(lambda e, x=x: e.activation(sq[:, 8 * x:8 * x + 8, :].rearrange("p a b -> p (a b)"),
                                                    PS[:, banks[x], :], ACT.Square), ops[x], h) for x in range(2)]
                v1 = V(lambda e: e.tensor_reduce(ss[:, kss, 0:16], sq, AX.X, ALU.add), a1, h2)
                rsq.free(ks, v1)
                v2 = V(lambda e: e.tensor_scalar(ss[:, kss, 0:16], ss[:, kss, 0:16], 1e-24, None, ALU.max), v1)
                a2 = A(lambda e: e.activation(ss[:, kss, 16:32], ss[:, kss, 0:16], ACT.Ln), v2)
                a3 = A(lambda e: e.activation(ss[:, kss, 16:32], ss[:, kss, 16:32], ACT.Exp, scale=-0.5), a2)
                R["ss", i] = (kss, a3)

            def rope(i):
                b, t = tiles[i]
                ops, banks = R.pop(("p", i))
                kss, a3 = R.pop(("ss", i))
                _, h = rqn.take()
                v3 = [V(lambda e, x=x: e.tensor_tensor(
                    qn[:, 8 * x:8 * x + 8, :], PS[:, banks[x], :].rearrange("p (a b) -> p a b", b=DH),
                    ss[:, kss, 16 + 8 * x:24 + 8 * x].rearrange("p (a o) -> p a o", o=1).to_broadcast([128, NH, DH]), ALU.mult),
                    a3, h) for x in range(2)]
                ra.free(banks[0], v3[0])
                ra.free(banks[1], v3[1])
                rss.free(kss, v3)
                ka, h = rta.take()
                kc, h2 = rtc.take()
                qv = qn.rearrange("p (x h) d -> p x h d", x=2)
                tab = lambda c: TB[:, l, c, t, :, :].rearrange("p x (o d) -> p x o d", o=1).to_broadcast([128, 2, NH, DH])
                v4 = V(lambda e: e.tensor_tensor(ta[ka].rearrange("p (x h) d -> p x h d", x=2), qv, tab(0), ALU.mult),
                       v3, h, tb_ready)
                g1 = G(lambda e: e.tensor_tensor(tc.rearrange("p (x h) d -> p x h d", x=2), qv, tab(1), ALU.mult),
                       v3, h2, tb_ready)
                rqn.free(0, v4, g1)
                tv = ta[ka]
                g2 = [G(lambda e, s=s: e.tensor_tensor(tv[:, :, 32 * s:32 * s + 32], tv[:, :, 32 * s:32 * s + 32],
                                                       tc[:, :, 32 * (1 - s):32 * (1 - s) + 32], ALU.add), v4, g1)
                      for s in range(2)]
                rtc.free(kc, g2)
                R["r", i] = (ka, g2)

            def turn(i, x):
                b, t = tiles[i]
                ka, g2 = R["r", i]
                k, h = ra.take()
                for j in range(4):
                    mm = T(lambda e, j=j: e.transpose(
                        PS[:, k, j * 128:(j + 1) * 128],
                        ta[ka][:, 8 * x + 2 * j:8 * x + 2 * j + 2, :].rearrange("p a b -> p (a b)"), ident), h, g2)
                src = PS[:, k, :].rearrange("p (a b) -> p a b", b=128)
                if x == 0:
                    c0 = (i % RQ) * 128
                    w = [bar, R.get(("S", i - RQ)), R.get(("S", i - RQ - 1))]
                    o = [A(lambda e: e.copy(qT[:, :, c0:c0 + 128], src), mm, w)]
                    if i % RQ == 0 and i > 0:
                        o.append(A(lambda e: e.copy(qT[:, :, RQ * 128:RQ * 128 + 64], src[:, :, 0:64]), mm, w))
                    kb, h = rqB.take()
                    o2 = V(lambda e: e.tensor_copy(qB[kb], src), mm, h, o)
                    R["q", i] = (o, kb, o2)
                    ra.free(k, o, o2)
                else:
                    kk, h = rkT.take()
                    o = V(lambda e: e.tensor_copy(kT[kk], src), mm, h)
                    o2 = A(lambda e: e.copy(kB[:, :, 64 + t * 128:192 + t * 128], src), mm, o, R.get(("Mw", i - NT)),
                           R.get(("Mw", i - NT + 1)), bar)
                    R["k", i] = (kk, o, o2)
                    ra.free(k, o, o2)
                    rta.free(ka, mm)
                    del R["r", i]

            def maxima(i, n):
                g, s = divmod(n, 2)
                b, t = tiles[i]
                oq, kb, oqb = R["q", i]
                kk, _, okb = R["k", i]
                k, h = rm.take()
                prev = R["k", i - 1][2] if t else zk
                T(lambda e: e.matmul(PS[:, 2 + k, 0:384], idb[:, :], mk[:, 0 if t else 1, :], start=True, stop=False,
                                     skip_group_check=True), h, k_consts)
                for c in range(2):
                    mm = T(lambda e, c=c: e.matmul(PS[:, 2 + k, 192 * c:192 * c + 192],
                                                   qB[kb][64 * s:64 * s + 64, 2 * g + c, :],
                                                   kB[64 * s:64 * s + 64, 2 * g + c, t * 128:t * 128 + 192],
                                                   start=False, stop=True, skip_group_check=True), oqb, okb, prev)
                if n == 0:
                    R["mx", i] = [rmx.take(), []]
                (km, h), lst = R["mx", i]
                v = V(lambda e: e.tensor_reduce(mx[km][:, 4 * g + s:4 * g + s + 3:2],
                                                PS[:, 2 + k, 0:384].rearrange("p (a b) -> p a b", b=192), AX.X, ALU.max,
                                                negate=True), mm, h)
                rm.free(k, v)
                lst.append(v)
                if n == 3:
                    rqB.free(kb, mm)
                    R["Mw", i] = mm

            def turn_maxima(i):
                (km, _), lst = R.pop(("mx", i))
                k, h = ra.take()
                mm = T(lambda e: e.transpose(PS[0:8, k, 0:128], mx[km], ident), lst, h)
                rmx.free(km, mm)
                c0 = (i % RQ) * 128
                w = [bar, R.get(("S", i - RQ)), R.get(("S", i - RQ - 1))]
                o = [A(lambda e: e.copy(mT[:, c0:c0 + 128], PS[0:8, k, 0:128]), mm, w)]
                if i % RQ == 0 and i > 0:
                    o.append(A(lambda e: e.copy(mT[:, RQ * 128:RQ * 128 + 64], PS[0:8, k, 0:64]), mm, w))
                ra.free(k, o)
                R["m", i] = o

            def values(i):
                b, t = tiles[i]
                k, h = ra.take()
                mm = T(lambda e: e.matmul(PS[:, k, :], HT[:, b, t * 128:(t + 1) * 128], wqkv[:, 1024:1536],
                                          start=True, stop=True), h, h_ready[i // 4], wait_attn_w[0], bar)
                kv, h = rva.take()
                src = PS[:, k, :].rearrange("p (a s d) -> p a s d", s=2, d=DH)
                o = [A(lambda e, s=s: e.copy(va[kv][:, :, 192 * s:192 * s + 64], src[:, :, s, :]), mm, h, ones)
                     for s in range(2)]
                ra.free(k, o)
                R["v", i] = (kv, o)

            def scores(i, n):
                g, s = divmod(n, 2)
                b, t = tiles[i]
                nq = 192 if t < NT - 1 else 128
                c0 = (i % RQ) * 128
                kk, okt, _ = R["k", i]
                need = [R["q", i][0], R["m", i], okt]
                if nq == 192:
                    need += [R["q", i + 1][0], R["m", i + 1]]
                k, h = rs.take()
                T(lambda e: e.matmul(PS[:, 4 + k, 0:384], idb[:, :], mk[:, 2, :], start=True, stop=False,
                                     skip_group_check=True), h, k_consts)
                for c in range(2):
                    T(lambda e, c=c: e.matmul(PS[:, 4 + k, 192 * c:192 * c + nq], sel[:, 4 * g + 2 * c + s, :],
                                              mT[:, c0:c0 + nq], start=False, stop=False, skip_group_check=True), need)
                for c in range(2):
                    mm = T(lambda e, c=c: e.matmul(PS[:, 4 + k, 192 * c:192 * c + nq],
                                                   kT[kk][64 * s:64 * s + 64, 2 * g + c, :],
                                                   qT[64 * s:64 * s + 64, 2 * g + c, c0:c0 + nq],
                                                   start=False, stop=True, skip_group_check=True), need)
                kp, h = rPT.take()
                src = PS[:, 4 + k, 0:384].rearrange("p (a b) -> p a b", b=192)[:, :, 0:nq]
                ae = A(lambda e: e.activation(PT[kp][:, :, 0:nq], src, ACT.Exp), mm, h)
                rs.free(k, ae)
                R["e", i, n] = (kp, ae)
                if n == 3:
                    rkT.free(kk, mm)
                    R["S", i] = mm

            def gather(i, n):
                g, s = divmod(n, 2)
                b, t = tiles[i]
                nq = 192 if t < NT - 1 else 128
                kv, ov = R["v", i]
                kp, ae = R.pop(("e", i, n))
                k, h = rv.take()
                for c in range(2):
                    mm = T(lambda e, c=c: e.matmul(PS[:, 6 + k, 192 * c:192 * c + nq],
                                                   va[kv][:, 2 * g + c, 128 * s:128 * s + 128],
                                                   PT[kp][:, c, 0:nq],
                                                   start=True, stop=True, skip_group_check=True), h, ae, ov)
                rPT.free(kp, mm)
                if n == 3:
                    rva.free(kv, mm)
                nd, old = ND[g][i % 2], ND[g][(i + 1) % 2]
                w = R.get(("nd", i - 1, g)), R.get(("nd", i - 2, g)), bar
                lo, hi = slice(64 * s, 64 * s + 64), slice(64 - 64 * s, 128 - 64 * s)
                src = PS[:, 6 + k, 0:384].rearrange("p (a b) -> p a b", b=192)[:, :, 0:nq]
                cp = [A(lambda e: e.copy(nd[lo, 0, :, 0:nq], src[lo, :, :]), mm, w),
                      A(lambda e: e.copy(nd[lo, 1, :, 0:nq], src[hi, :, :]), mm, w)]
                rv.free(k, cp)
                if s == 0:
                    R["cp", i, g] = cp
                    return
                cp = cp + R.pop(("cp", i, g))
                if t:
                    cp = [V(lambda e: e.tensor_tensor(nd[:, :, :, 0:64], nd[:, :, :, 0:64], old[:, :, :, 128:192], ALU.add),
                            cp)]
                kl, h = rlnd.take()
                a1 = A(lambda e: e.activation(lnd[kl], nd[:, 1, :, 0:128], ACT.Ln), cp, h)
                a2 = A(lambda e: e.activation(lnd[kl], lnd[kl], ACT.Exp, scale=-1.0), a1)
                if g == 0:
                    R["ot", i] = [rot.take(), []]
                (ko, h), lst = R["ot", i]
                o = G(lambda e: e.tensor_tensor(ot[ko][:, 2 * g:2 * g + 2, :], nd[:, 0, :, 0:128], lnd[kl], ALU.mult),
                      a2, cp, h)
                rlnd.free(kl, o)
                R["nd", i, g] = [o, cp]
                lst.append(o)

            def project_out(i):
                b, t = tiles[i]
                (ko, _), lst = R.pop(("ot", i))
                k, h = ra.take()
                for j in range(4):
                    mm = T(lambda e, j=j: e.matmul(PS[:, k, 0:128], wo[:, j, :], ot[ko][:, j, :],
                                                   start=(j == 0), stop=(j == 3)), h, lst, wait_attn_w[0])
                rot.free(ko, mm)
                dst = yT[:, b, t * 128:(t + 1) * 128]
                o = V(lambda e: e.tensor_tensor(dst, PS[:, k, 0:128], dst, ALU.add), mm, bar)
                ra.free(k, o)
                R["out", i] = o

            for s in range(nt + 7):
                def on(lag):
                    return 0 <= s - lag < nt
                if on(3):
                    turn_maxima(s - 3)
                if on(0):
                    project(s)
                for n in range(4):
                    if on(4):
                        scores(s - 4, n)
                    if n == 0:
                        if on(0):
                            rope(s)
                        if on(5):
                            gather(s - 5, 3)
                            project_out(s - 5)
                        if on(3):
                            values(s - 3)
                    if on(4) and n >= 1:
                        gather(s - 4, n - 1)
                    if on(2):
                        maxima(s - 2, n)
                    if n == 2 and on(1):
                        turn(s - 1, 0)
                        turn(s - 1, 1)
            return [[R["out", 4 * c + j] for j in range(4)] for c in range(NCH)], T_last(Q)

        def T_last(Q):
            return Q.q["tensor"][-1]

        def feed_forward(l, ready):
            at[0] = 0
            bar = barrier()
            h_ready = shift(ready, bar)
            hn = layernorm(HT[:, :, 0:N], HT[:, :, 0:N], h_ready, bar)
            bar2 = barrier()
            gl = [arena(CH, [CH]) for _ in range(3)]
            hm = [arena(CH, [CH]) for _ in range(6)]
            fold = V(lambda e: e.tensor_scalar(w1g[:, :], w1[:, :], vec[:, l:l + 1], None, ALU.mult), wait_ffn_w[0],
                     ld_small, bar)
            for i in range(6):
                s0 = HID * (i // 3) + C0[i % 3]
                wd = CW[i % 3]
                mm = T(lambda e, i=i, s0=s0, wd=wd: e.matmul(PS[0:wd, 0, i:i + 1], w1[:, s0:s0 + wd], vec[:, 2 + l:3 + l],
                                                            start=True, stop=True), wait_ffn_w[0], ld_small, bar2)
            bb = [V(lambda e, i=i: e.tensor_tensor(b1r[0:CW[i % 3], i:i + 1], PS[0:CW[i % 3], 0, i:i + 1],
                                                   b1c[0:CW[i % 3], l, i:i + 1], ALU.add), mm, bar) for i in range(6)]
            r6, r2, rg, rh = Ring(6, [bb]), Ring(2, bar2), Ring(3, bar2), Ring(6, bar2)
            done = []
            pend = []

            def second(c, items):
                k, h = r2.take()
                for i, (kh, v) in enumerate(items):
                    mm = T(lambda e, i=i, kh=kh: e.matmul(PS[:, 6 + k, :], w2[0:CW[i], i, :], hm[kh][0:CW[i], :],
                                                          start=(i == 0), stop=(i == 2)), h, v, bar2)
                    rh.free(kh, mm)
                dst = chunk(yT, c)
                o = V(lambda e: e.scalar_tensor_tensor(dst, PS[:, 6 + k, :], vec[:, 4 + l:5 + l], dst, ALU.add, ALU.add),
                      mm, bar2)
                r2.free(k, o)
                done.append(o)
                return mm

            lastT = None
            for c in range(NCH + 1):
                if c < NCH:
                    items = []
                    for i in range(3):
                        wd = CW[i]
                        kg, h = r6.take()
                        m1 = T(lambda e, i=i, kg=kg, wd=wd, c=c: e.matmul(PS[0:wd, kg, :], w1g[:, HID + C0[i]:HID + C0[i] + wd],
                                                                     HT[:, c // 4, (c % 4) * CH:(c % 4 + 1) * CH],
                                                                     start=True, stop=True), h, hn[c], fold, bar2)
                        ka, h = r6.take()
                        m2 = T(lambda e, i=i, ka=ka, wd=wd, c=c: e.matmul(PS[0:wd, ka, :], w1g[:, C0[i]:C0[i] + wd],
                                                                     HT[:, c // 4, (c % 4) * CH:(c % 4 + 1) * CH],
                                                                     start=True, stop=True), h, bar2)
                        q, h = rg.take()
                        g1 = A(lambda e, i=i, kg=kg, wd=wd, q=q: e.activation(gl[q][0:wd, :], PS[0:wd, kg, :], ACT.Gelu,
                                                                              bias=b1r[0:wd, 3 + i:4 + i]), m1, h, bb)
                        r6.free(kg, g1)
                        kh, h = rh.take()
                        v = V(lambda e, i=i, ka=ka, wd=wd, q=q, kh=kh: e.scalar_tensor_tensor(
                            hm[kh][0:wd, :], PS[0:wd, ka, :], b1r[0:wd, i:i + 1], gl[q][0:wd, :], ALU.add, ALU.mult),
                            m2, g1, h, bb)
                        r6.free(ka, v)
                        rg.free(q, v)
                        items.append((kh, v))
                    pend.append(items)
                if c >= 1:
                    lastT = second(c - 1, pend[c - 1])
            return done, lastT

        def ffn(ready, last):
            for l in range(2):
                h_ready = shift(ready, barrier())
                ready, lt = local_attention(l, h_ready)
                if not (last and l == 1):
                    load_attn_w(1 - l, lt)
                ready, lt = feed_forward(l, ready)
                if not (last and l == 1):
                    load_ffn_w(1 - l, lt)
                tables()
            res = []
            for c in range(NCH):
                res.append(V(lambda e, c=c: e.tensor_tensor(chunk(xT, c), chunk(xT, c), chunk(yT, c), ALU.add), ready[c]))
            return res

        def weighted_values(ready):
            at[0] = 0
            bar = barrier()
            TT = NB * NT
            st = arena(5 * TT, [5, TT])
            dd = [arena(512, [4, 128]) for _ in range(2)]
            d2 = [arena(512, [4, 128]) for _ in range(2)]
            dm = [arena(256, [2, 128]) for _ in range(2)]
            w = arena(16 * TT, [16, TT])
            h4 = arena(4 * TT, [4, TT])
            h5 = arena(4 * TT, [4, TT])
            sm = arena(32, [32])
            wbr = [arena(128, [128]) for _ in range(4)]
            wbs = [arena(512, [512]) for _ in range(2)]
            vs = [arena(512, [512]) for _ in range(2)]
            rp, rd = Ring(3, bar), Ring(2, bar)
            seq = []
            for j in range(TT // 2):
                b = j // (NT // 2)
                k, h = rp.take()
                for s in range(2):
                    n0 = (2 * j + s) % NT * 128
                    mm = T(lambda e, s=s, n0=n0, b=b, k=k: e.matmul(PS[:, k, 256 * s:256 * s + 256], yT[:, b, n0:n0 + 128],
                                                                    wb[:, 0:256], start=True, stop=True,
                                                                    skip_group_check=True), h, ready, bar, ld_small)
                q, h = rd.take()
                p4 = PS[:, k, :].rearrange("p (a b) -> p a b", b=128)
                mu = st[:, 0:2, 2 * j:2 * j + 2].rearrange("p a b -> p b a")
                v1 = V(lambda e, p4=p4, mu=mu: e.tensor_reduce(mu, p4.rearrange("p (a c) b -> p a c b", c=2), AX.X, ALU.add),
                       mm, bar)
                v2 = V(lambda e, mu=mu: e.tensor_scalar(mu, mu, 1.0 / 128, None, ALU.mult), v1)
                v3 = V(lambda e, p4=p4, mu=mu, q=q: e.tensor_tensor(
                    dd[q].rearrange("p (a c) b -> p a c b", c=2), p4.rearrange("p (a c) b -> p a c b", c=2),
                    mu.rearrange("p a (c o) -> p a c o", o=1).to_broadcast([128, 2, 2, 128]), ALU.subtract), v2, h)
                rp.free(k, v3)
                a1 = A(lambda e, q=q: e.activation(d2[q], dd[q], ACT.Square), v3, h)
                dv = dd[q].rearrange("p (a c) b -> p a c b", c=2)
                g1 = G(lambda e, q=q, dv=dv: e.tensor_tensor(dm[q], dv[:, :, 0, :], dv[:, :, 1, :], ALU.mult), v3, h)
                sg = st[:, 2:4, 2 * j:2 * j + 2].rearrange("p a b -> p b a")
                v4 = V(lambda e, q=q, sg=sg: e.tensor_reduce(sg, d2[q].rearrange("p (a c) b -> p a c b", c=2), AX.X, ALU.add), a1)
                v5 = V(lambda e, q=q, j=j: e.tensor_reduce(st[:, 4, 2 * j:2 * j + 2], dm[q], AX.X, ALU.add), g1)
                rd.free(q, v4, v5)
                seq += [v4, v5]
            c1, c2 = vec[:, 9:10], vec[:, 10:11]
            prev = [seq + [bar]]

            def V1(fn, *more):
                prev[0] = V(fn, prev[0], *more)
                return prev[0]

            mq, mkk, sq2, sk2, sqk = (st[:, i, :] for i in range(5))
            i127 = 1.0 / 127
            V1(lambda e: e.tensor_tensor(w[:, 0, :], mq, mkk, ALU.mult))
            V1(lambda e: e.tensor_scalar(w[:, 0, :], w[:, 0, :], 2.0, c1, ALU.mult, ALU.add))
            V1(lambda e: e.tensor_scalar(w[:, 1, :], sqk, 2.0 * i127, c2, ALU.mult, ALU.add))
            V1(lambda e: e.tensor_tensor(w[:, 0, :], w[:, 0, :], w[:, 1, :], ALU.mult))
            V1(lambda e: e.tensor_tensor(w[:, 1, :], mq, mq, ALU.mult))
            V1(lambda e: e.tensor_tensor(w[:, 2, :], mkk, mkk, ALU.mult))
            V1(lambda e: e.scalar_tensor_tensor(w[:, 1, :], w[:, 1, :], c1, w[:, 2, :], ALU.add, ALU.add))
            V1(lambda e: e.tensor_tensor(w[:, 2, :], sq2, sk2, ALU.add))
            V1(lambda e: e.tensor_scalar(w[:, 2, :], w[:, 2, :], i127, c2, ALU.mult, ALU.add))
            V1(lambda e: e.tensor_tensor(w[:, 1, :], w[:, 1, :], w[:, 2, :], ALU.mult))
            V1(lambda e: e.tensor_scalar(w[:, 1, :], w[:, 1, :], 1e-7, None, ALU.add))
            V1(lambda e: e.reciprocal(w[:, 2, :], w[:, 1, :]))
            V1(lambda e: e.tensor_tensor(w[:, 0, :], w[:, 0, :], w[:, 2, :], ALU.mult))
            va_ = V1(lambda e: e.tensor_tensor(w[:, 3, :], w[:, 0, :], w[:, 0, :], ALU.mult))

            def neighbours(src, nch, bank, *wait):
                view = lambda ap: ap.rearrange("p (c b t) -> p c b t", b=NB, t=NT)
                s = view(src)
                ops = []
                for d, (m, ed) in enumerate(((sdn, edn), (sup, eup))):
                    o = PS[:, bank + d, 0:nch * TT]
                    ov = view(o)
                    T(lambda e, o=o, m=m: e.matmul(o, m, src, start=True, stop=False, skip_group_check=True), wait)
                    for c in range(nch):
                        for b in range(NB):
                            do = ov[:, c, b, 1:NT] if d == 0 else ov[:, c, b, 0:NT - 1]
                            di = s[:, c, b, 0:NT - 1] if d == 0 else s[:, c, b, 1:NT]
                            mm = T(lambda e, do=do, di=di, ed=ed: e.matmul(do, ed, di, start=False, stop=True,
                                                                          skip_group_check=True))
                    ops.append(mm)
                return ops

            nb = neighbours(w[:, 3, :], 1, 3, va_, bar)
            for c in range(4):
                wc = lambda k: vec[:, 12 + 3 * c + k:13 + 3 * c + k]
                V1(lambda e, c=c: e.tensor_scalar(h4[:, c, :], w[:, 3, :], vec[:, 13 + 3 * c:14 + 3 * c], None, ALU.mult))
                for k, d in ((0, 0), (2, 1)):
                    V1(lambda e, c=c, k=k, d=d: e.scalar_tensor_tensor(
                        h4[:, c, :], PS[:, 3 + d, 0:TT], vec[:, 12 + 3 * c + k:13 + 3 * c + k], h4[:, c, :],
                        ALU.mult, ALU.add), nb)
            g5 = lambda ap: ap.rearrange("p (g c) (b t) -> p g c b t", g=2, b=NB)

            def group_mean(src, bank, *more):
                for g in range(2):
                    for b in range(NB):
                        V1(lambda e, g=g, b=b: e.tensor_reduce(sm[:, 2 * g + b:2 * g + b + 1], g5(src)[:, g, :, b, :],
                                                               AX.XY, ALU.add), *more)
                m = T(lambda e: e.matmul(PS[:, bank, 0:4], avg, sm[:, 0:4], start=True, stop=True), prev[0])
                return V1(lambda e: e.tensor_scalar(sm[:, 4:8], PS[:, bank, 0:4], 1.0 / 32, None, ALU.mult), m)

            group_mean(h4, 5)
            for g in range(2):
                for b in range(NB):
                    hv = g5(h4)[:, g, :, b, :]
                    V1(lambda e, g=g, b=b, hv=hv: e.tensor_scalar(hv, hv, sm[:, 4 + 2 * g + b:5 + 2 * g + b], None,
                                                                  ALU.subtract))
            V1(lambda e: e.tensor_tensor(h5, h4, h4, ALU.mult))
            v = group_mean(h5, 6)
            a1 = A(lambda e: e.activation(sm[:, 8:12], sm[:, 4:8], ACT.Ln, bias=eps_ap), v)
            a2 = A(lambda e: e.activation(sm[:, 12:16], sm[:, 8:12], ACT.Exp, scale=-0.5), a1)
            for g in range(2):
                for b in range(NB):
                    hv = g5(h4)[:, g, :, b, :]
                    V1(lambda e, g=g, b=b, hv=hv: e.tensor_scalar(hv, hv, sm[:, 12 + 2 * g + b:13 + 2 * g + b], None,
                                                                  ALU.mult), a2)
            for c in range(4):
                V1(lambda e, c=c: e.tensor_scalar(h4[:, c, :], h4[:, c, :], vec[:, 24 + c:25 + c], vec[:, 28 + c:29 + c],
                                                  ALU.mult, ALU.add))
            vh = V1(lambda e: e.tensor_scalar(h4, h4, 0.0, None, ALU.max))
            nb = neighbours(h4.rearrange("p a b -> p (a b)"), 4, 3, vh)
            for c in range(4):
                V1(lambda e, c=c: e.scalar_tensor_tensor(w[:, 3, :], h4[:, c, :], vec[:, 33 + 3 * c:34 + 3 * c], w[:, 3, :],
                                                         ALU.mult, ALU.add))
                for k, d in ((0, 0), (2, 1)):
                    V1(lambda e, c=c, k=k, d=d: e.scalar_tensor_tensor(
                        w[:, 3, :], PS[:, 3 + d, c * TT:(c + 1) * TT], vec[:, 32 + 3 * c + k:33 + 3 * c + k], w[:, 3, :],
                        ALU.mult, ALU.add), nb)
            v = V1(lambda e: e.tensor_reduce(sm[:, 16:18], yT[:, :, :], AX.X, ALU.add))
            v = V1(lambda e: e.tensor_scalar(sm[:, 16:18], sm[:, 16:18], 1.0 / N, None, ALU.mult))
            m = T(lambda e: e.matmul(PS[0:32, 5, 0:2], cw1[:, :], sm[:, 16:18], start=True, stop=True), v)
            v = V1(lambda e: e.tensor_scalar(sm[0:32, 18:20], PS[0:32, 5, 0:2], vec[0:32, 8:9], 0.0, ALU.add, ALU.max), m)
            m = T(lambda e: e.matmul(PS[:, 6, 0:2], cw2[:, :], sm[0:32, 18:20], start=True, stop=True), v)
            a0 = A(lambda e: e.activation(sm[:, 20:22], PS[:, 6, 0:2], ACT.Sigmoid, bias=vec[:, 7:8]), m)
            a1 = A(lambda e: e.activation(w[:, 4, :], w[:, 3, :], ACT.Sigmoid, bias=vec[:, 44:45]), prev[0])
            tables()
            a2 = A(lambda e: e.activation(w[:, 5, :], w[:, 4, :], ACT.Exp), a1)
            v = V1(lambda e: e.tensor_reduce(sm[:, 22:24], w[:, 5, :].rearrange("p (b t) -> p b t", b=NB), AX.X, ALU.add), a2)
            m = T(lambda e: e.matmul(PS[:, 5, 0:2], avg, sm[:, 22:24], start=True, stop=True), v)
            v = V1(lambda e: e.tensor_scalar(sm[:, 24:26], PS[:, 5, 0:2], 128.0, None, ALU.mult), m)
            v = V1(lambda e: e.reciprocal(sm[:, 26:28], sm[:, 24:26]))
            for b in range(NB):
                v = V1(lambda e, b=b: e.tensor_scalar(w[:, 6, NT * b:NT * (b + 1)], w[:, 5, NT * b:NT * (b + 1)],
                                                      sm[:, 26 + b:27 + b], None, ALU.mult))
            bar2 = [barrier()]
            rb, rwb, rv3, rws, rvs, ro = Ring(2, bar2), Ring(4, bar2), Ring(2, bar2), Ring(2, bar2), Ring(2, bar2), Ring(2, bar2)
            done = []
            for c in range(NCH):
                b = c // 4
                kv, h = rv3.take()
                mv = T(lambda e, c=c, kv=kv: e.matmul(PS[:, kv, :], wb[:, 256:384], chunk(yT, c), start=True, stop=True), h)
                kb, h = rb.take()
                for j in range(4):
                    t = 4 * c + j
                    kw, h2 = rwb.take()
                    v1 = V(lambda e, t=t, kw=kw: e.tensor_copy(wbr[kw], w[:, 6, t:t + 1].to_broadcast([128, 128])), v, h2)
                    mm = T(lambda e, j=j, kw=kw, kb=kb: e.matmul(PS[:, 2 + kb, 128 * j:128 * j + 128], wbr[kw], ident,
                                                                start=True, stop=True, skip_group_check=True), v1, h)
                    rwb.free(kw, mm)
                ks, h = rws.take()
                a1 = A(lambda e, kb=kb, ks=ks: e.copy(wbs[ks], PS[:, 2 + kb, :]), mm, h)
                rb.free(kb, a1)
                kz, h = rvs.take()
                v2 = V(lambda e, kv=kv, ks=ks, kz=kz, b=b: e.scalar_tensor_tensor(
                    vs[kz], PS[:, kv, :], sm[:, 20 + b:21 + b], wbs[ks], ALU.mult, ALU.mult), mv, a1, a0, h)
                rv3.free(kv, v2)
                rws.free(ks, v2)
                ko, h = ro.take()
                mo = T(lambda e, ko=ko, kz=kz: e.matmul(PS[:, 4 + ko, :], wp[:, :], vs[kz], start=True, stop=True), v2, h)
                rvs.free(kz, mo)
                o = V(lambda e, c=c, ko=ko: e.scalar_tensor_tensor(chunk(xT, c), PS[:, 4 + ko, :], vec[:, 6:7], chunk(xT, c),
                                                                   ALU.add, ALU.add), mo)
                ro.free(ko, o)
                done.append(o)
            return done

        def normed(ready):
            at[0] = 0
            bar = barrier()
            return layernorm(xT, yT, ready, bar)

        r = normed(x_parts)
        r = self_attention(r)
        r = ffn(normed(r), False)
        r = weighted_values(normed(r))
        r = ffn(normed(r), True)

        bar = barrier()
        at[0] = 0
        ob = [arena(512, [4, 128]) for _ in range(8)]
        od = out.rearrange("b (t p) d -> p (b t) d", p=128)
        s_out = sem("s_out")
        for g in range(8):
            for j in range(4):
                mm = T(lambda e, g=g, j=j: e.transpose(PS[:, g, j * 128:(j + 1) * 128],
                                                       chunk(xT, g)[:, j * 128:(j + 1) * 128], ident), r[g], bar)
            o = (V if g % 2 else A)(lambda e, g=g: (e.tensor_copy if g % 2 else e.copy)(
                ob[g].rearrange("p a b -> p (a b)"), PS[:, g, :]), mm, bar)
            Q.op("sync", lambda e, g=g: e.dma_start(od[:, 4 * g:4 * g + 4, :], ob[g]).then_inc(s_out, 16), o)
        Q.op("sync", lambda e: e.wait_ge(s_out, 128))

        block = ctx.enter_context(nc.Block())
        Q.emit(block, sems)


def rope_tables():
    f = np.float32
    half = np.arange(0, DH, 2, dtype=f)
    inv = (f(1.0) / np.power(f(10000.0), half / f(DH))).astype(f)
    t = np.arange(N, dtype=f)
    fr = (t[:, None] * inv[None, :]).astype(f).astype(np.float64)
    base = ((half + f(0.4 * DH)) / f(1.4 * DH)).astype(f).astype(np.float64)
    sc = base[None, :] ** ((t.astype(np.float64) - N // 2) / (W // 2))[:, None]
    c, s = np.cos(fr), np.sin(fr)
    dup = lambda x: np.concatenate([x, x], -1)
    sgn = lambda x: np.concatenate([x, -x], -1)
    C = np.stack([dup(8 * c * sc), dup(c / sc)], 1)
    S = np.stack([sgn(8 * s * sc), sgn(s / sc)], 1)
    tab = np.stack([C, S], 0).astype(f).reshape(2, NT, 128, 2, DH)
    return np.ascontiguousarray(tab.transpose(2, 0, 1, 3, 4)).reshape(128, -1)


def constants():
    f = np.float32
    I = np.eye(128, dtype=f)
    sdn = np.zeros((128, 128), f)
    sdn[np.arange(127), np.arange(1, 128)] = 1
    edn = np.zeros((128, 128), f)
    edn[127, 0] = 1
    cst = np.stack([I, I - f(1 / 128), np.full((128, 128), 1 / 128, f), sdn, sdn.T, edn, edn.T], 1)
    i = np.arange(128)[:, None]
    c = np.arange(192)[None, :]
    j = c - 64
    okq = (j <= i) & (i <= j + W)
    okq &= (np.floor_divide(j, W) >= i // W - 1)
    mq = np.where(okq, 0, NEG).astype(f)
    mq0 = np.where(okq & (j >= 0), 0, NEG).astype(f)
    jj, qq = np.arange(128)[:, None], np.arange(192)[None, :]
    okt = (jj <= qq) & (qq <= jj + W) & (jj // W >= qq // W - 1)
    mt = np.where(okt, 0, NEG).astype(f)
    mask = np.concatenate([mq, mq, mq0, mq0, mt, mt], 1)
    sel = np.zeros((8, 8, 128), f)
    for h in range(8):
        sel[h, h] = 1
    return {"c_f32": np.ascontiguousarray(cst), "c_mask": np.ascontiguousarray(mask), "c_sel": sel.reshape(8, 1024),
            "c_rope": rope_tables()}


_INS = ['L0_attn_a_x', 'L0_attn_b_qkv_w', 'L0_attn_b_c1', 'L0_attn_b_c2', 'L0_attn_b_conv1_w', 'L0_attn_b_gn_g',
        'L0_attn_b_gn_b', 'L0_attn_b_conv2_w', 'L0_attn_b_conv2_b', 'L0_attn_b_ch_w1', 'L0_attn_b_ch_b1',
        'L0_attn_b_ch_w2', 'L0_attn_b_ch_b2', 'L0_attn_b_proj_w', 'L0_attn_b_proj_b', 'L0_ffn_wqkv', 'L0_ffn_q_scale',
        'L0_ffn_k_scale', 'L0_ffn_wo', 'L0_ffn_ln_g', 'L0_ffn_ln_b', 'L0_ffn_w1', 'L0_ffn_b1', 'L0_ffn_w2', 'L0_ffn_b2']


def kernel(**inputs):
    import numpy as _np
    import concourse.bacc as _bacc
    from concourse import mybir as _mybir
    from concourse.bass_utils import run_bass_kernel_spmd as _run

    nc = _bacc.Bacc("TRN2", target_bir_lowering=False, num_devices=1)
    arrays, args = {}, {}
    given = {n: _np.ascontiguousarray(inputs[n]) for n in _INS}
    for n in ('L0_attn_b_c1', 'L0_attn_b_c2'):
        given[n] = given[n].reshape(1)
    given.update(constants())
    for name, v in given.items():
        arrays[f"in_{name}"] = v
        args[name] = nc.dram_tensor(f"in_{name}", v.shape, _mybir.dt.from_np(v.dtype), kind="ExternalInput").ap()
    out = nc.dram_tensor("out_x", (NB, N, D), F32, kind="ExternalOutput").ap()
    build(nc, args, out)
    r = _run(nc, [arrays], core_ids=[0])
    return r.results[0]["out_x"]
```

```python
from contextlib import ExitStack

import numpy as np

import concourse.bass as bass
from concourse import mybir

F32 = mybir.dt.float32
BF16 = mybir.dt.bfloat16
F32R = mybir.dt.float32r
ALU = mybir.AluOpType
ACT = mybir.ActivationFunctionType
AX = mybir.AxisListType

NB, N, D = 2, 2048, 128
NT = N // 128
NH, DH, W = 8, 64, 64
HID = 341
CW = [114, 114, 113]
C0 = [0, 114, 228]
CH = 512
NCH = NB * N // CH
EPS = 1e-5
NEG = -1e30


class Op:

    def __init__(self, eng, fn, waits):
        self.eng, self.fn, self.waits, self.mark, self.table = eng, fn, waits, None, False


class Load:

    def __init__(self, sem, value):
        self.sem, self.value = sem, value


class Queues:

    def __init__(self):
        self.q = {e: [] for e in ("sync", "tensor", "vector", "scalar", "gpsimd")}
        self.dma_sems = 0

    def op(self, eng, fn, *waits):
        flat = []
        todo = list(waits)
        while todo:
            w = todo.pop()
            if w is None:
                continue
            if isinstance(w, (list, tuple)):
                todo += w
            else:
                flat.append(w)
        o = Op(eng, fn, flat)
        self.q[eng].append(o)
        return o

    def last(self):
        return [[o for o in q if not o.table][-1:] for e, q in self.q.items() if e != "sync"]

    def emit(self, block, sems):
        for q in self.q.values():
            for o in q:
                for w in o.waits:
                    if isinstance(w, Op):
                        w.mark = 0
        for e, q in self.q.items():
            n = 0
            for o in q:
                if o.mark is not None and not isinstance(o.fn, Load):
                    n += 1
                    o.mark = n

        def run(eng, name):
            seen = {}
            for o in self.q[name]:
                for w in o.waits:
                    key, value = (w.eng, w.mark) if isinstance(w, Op) else (id(w.sem), w.value)
                    if seen.get(key, 0) >= value:
                        continue
                    seen[key] = value
                    eng.wait_ge(sems[w.eng] if isinstance(w, Op) else w.sem, value)
                ins = o.fn(eng)
                if o.mark is not None:
                    ins.then_inc(sems[name], 1)

        block.sync(lambda eng: run(eng, "sync"))
        block.tensor(lambda eng: run(eng, "tensor"))
        block.vector(lambda eng: run(eng, "vector"))
        block.scalar(lambda eng: run(eng, "scalar"))
        block.gpsimd(lambda eng: run(eng, "gpsimd"))


class Ring:

    def __init__(self, n, start=None):
        self.n, self.i, self.held = n, 0, [start] * n

    def take(self):
        k = self.i % self.n
        self.i += 1
        return k, self.held[k]

    def free(self, k, *ops):
        self.held[k] = list(ops)


def build(nc, a, out):
    ctx = ExitStack()
    with ctx:
        def sb(name, shape, dt=F32):
            return ctx.enter_context(nc.sbuf_tensor(name, shape, dt))

        def sem(name):
            return ctx.enter_context(nc.semaphore(name))

        sems = {e: sem("c_" + e) for e in ("sync", "tensor", "vector", "scalar", "gpsimd")}
        Q = Queues()

        def T(fn, *w):
            return Q.op("tensor", fn, *w)

        def V(fn, *w):
            return Q.op("vector", fn, *w)

        def A(fn, *w):
            return Q.op("scalar", fn, *w)

        def G(fn, *w):
            return Q.op("gpsimd", fn, *w)

        def tables():
            A(lambda e: e.preload_act_table_set("natural_log_exp_and_others")).table = True

        n_loads = [0]

        def load(pairs, *w):
            s = sem(f"d{n_loads[0]}")
            n_loads[0] += 1
            for dst, src in pairs:
                Q.op("sync", lambda e, dst=dst, src=src: e.dma_start(dst, src).then_inc(s, 16), *w)
                w = ()
            return Load(s, 16 * len(pairs))

        yT = sb("yT", [128, NB, N])
        HH = sb("HH", [128, NB, N + 4], F32R)
        HL = sb("HL", [128, NB, N + 4], F32R)
        TB = sb("TB", [128, 2, 2, NT, 2, DH])
        wqh = sb("wqh", [128, 3 * NH * DH], F32R)
        wql = sb("wql", [128, 3 * NH * DH], F32R)
        wo = sb("wo", [128, 4, D])
        w1 = sb("w1", [128, 2 * HID])
        w1h = sb("w1h", [128, 2 * HID], F32R)
        w1l = sb("w1l", [128, 2 * HID], F32R)
        w2 = sb("w2", [114, 3, D])
        w2h = sb("w2h", [114, 3, D], F32R)
        w2l = sb("w2l", [114, 3, D], F32R)
        wb = sb("wb", [128, 3 * D])
        wp = sb("wp", [128, D])
        cw1 = sb("cw1", [128, 32])
        cw2 = sb("cw2", [32, D])
        cst = sb("cst", [128, 7, 128])
        cenr = sb("cenr", [128, 128], F32R)
        mk = sb("mk", [128, 3, 384], BF16)
        idb = sb("idb", [128, 128], BF16)
        sel = sb("sel", [8, 8, 128], BF16)
        qks = sb("qks", [128, 2, 2, DH])
        b1c = sb("b1c", [114, 2, 6])
        b1r = sb("b1r", [114, 6])
        vec = sb("vec", [128, 64])
        cstv = sb("cstv", [128, 4])
        ident, cen, avg, sdn, sup, edn, eup = (cst[:, i, :] for i in range(7))
        PS = ctx.enter_context(nc.psum_tensor("PS", [128, 8, 512], F32))
        xsave = nc.dram_tensor("xsave", (128, NB * N), F32, kind="Internal").ap()

        scopes = []
        names = [0]

        def arena(n, shape, dt=F32, parts=128):
            names[0] += 1
            t = scopes[-1].enter_context(nc.sbuf_tensor(f"t{names[0]}", [parts] + list(shape), dt))
            return t[tuple(slice(None) for _ in range(len(shape) + 1))]

        def phase(f):
            def g(*args):
                scopes.append(ExitStack())
                with scopes[-1]:
                    r = f(*args)
                scopes.pop()
                return r
            return g

        def halves(out, a, b, w, more=(), last=True):
            (ah, al), (bh, bl) = a, b
            T(lambda e: e.matmul(out, ah, bh, start=not more, stop=False, skip_group_check=True), w)
            T(lambda e: e.matmul(out, ah, bl, start=False, stop=False, skip_group_check=True))
            return T(lambda e: e.matmul(out, al, bh, start=False, stop=last, skip_group_check=True))

        def split(hi, lo, src, e_hi, e_lo, *w):
            o = e_hi(lambda e: (e.copy if e_hi is A else e.tensor_copy)(hi, src), *w)
            return [o, e_lo(lambda e: e.tensor_tensor(lo, src, hi.bitcast(F32) if hi.dtype == F32R else hi,
                                                      ALU.subtract), o, *w)]

        xs = [ExitStack(), None]

        def take_x():
            names[0] += 1
            xs[1] = xs[0].enter_context(nc.sbuf_tensor(f"x{names[0]}", [128, NB, N], F32))

        take_x()
        scopes.append(ExitStack())
        xtok = arena(0, [NB * NT, D])
        mkf = arena(0, [1152])
        self32 = arena(0, [1024], F32, 8)
        wqs = arena(0, [1536])
        xd = a["L0_attn_a_x"].rearrange("b (t p) d -> p (b t) d", p=128)
        ld_cst = load([(cst[:, :, :], a["c_f32"])])
        ld_x = [load([(xtok[:, 8 * i:8 * i + 8, :], xd[:, 8 * i:8 * i + 8, :])]) for i in range(4)]
        ld_mk = load([(mkf, a["c_mask"]), (self32, a["c_sel"])])
        bc = lambda ap, n: ap.rearrange("(o n) -> o n", o=1).to_broadcast([128, n])
        ld_tb = load([(TB[:, 1, :, :, :, :].rearrange("p a b c d -> p (a b c d)"), a["c_rope"]),
                      (qks[:, :, 0, :], a["L0_ffn_q_scale"].rearrange("(o l) d -> o l d", o=1).to_broadcast([128, 2, DH])),
                      (qks[:, :, 1, :], a["L0_ffn_k_scale"].rearrange("(o l) d -> o l d", o=1).to_broadcast([128, 2, DH]))])
        col = lambda ap: ap.rearrange("(p o) -> p o", o=1)
        small = []
        for l in range(2):
            small += [(vec[:, l:l + 1], col(a["L0_ffn_ln_g"][l])), (vec[:, 2 + l:3 + l], col(a["L0_ffn_ln_b"][l])),
                      (vec[:, 4 + l:5 + l], col(a["L0_ffn_b2"][l]))]
            for g in range(2):
                for i in range(3):
                    s0 = HID * g + C0[i]
                    small.append((b1c[0:CW[i], l, 3 * g + i:3 * g + i + 1], col(a["L0_ffn_b1"][l, s0:s0 + CW[i]])))
        small += [(vec[:, 6:7], col(a["L0_attn_b_proj_b"])), (vec[:, 7:8], col(a["L0_attn_b_ch_b2"])),
                  (vec[0:32, 8:9], col(a["L0_attn_b_ch_b1"])),
                  (vec[:, 9:10], bc(a["L0_attn_b_c1"], 1)), (vec[:, 10:11], bc(a["L0_attn_b_c2"], 1)),
                  (vec[:, 12:24], bc(a["L0_attn_b_conv1_w"].rearrange("a b c -> (a b c)"), 12)),
                  (vec[:, 24:28], bc(a["L0_attn_b_gn_g"], 4)), (vec[:, 28:32], bc(a["L0_attn_b_gn_b"], 4)),
                  (vec[:, 32:44], bc(a["L0_attn_b_conv2_w"].rearrange("a b c -> (a b c)"), 12)),
                  (vec[:, 44:45], bc(a["L0_attn_b_conv2_b"], 1)),
                  (wb[:, :], a["L0_attn_b_qkv_w"]), (wp[:, :], a["L0_attn_b_proj_w"]),
                  (cw1[:, :], a["L0_attn_b_ch_w1"]), (cw2[:, :], a["L0_attn_b_ch_w2"])]
        ld_small = load(small)
        wait_attn_w = [None]
        wait_ffn_w = [None]

        def load_attn_w(l, stage, *w):
            ld = load([(stage, a["L0_ffn_wqkv"][l]),
                       (wo[:, :, :], a["L0_ffn_wo"][l].rearrange("(c p) d -> p c d", p=128))], *w)
            wait_attn_w[0] = [ld] + split(wqh[:, :], wql[:, :], stage, V, G, ld, *w)

        def load_ffn_w(l, *w):
            wait_ffn_w[0] = load([(w1[:, :], a["L0_ffn_w1"][l])] +
                                 [(w2[0:CW[i], i, :], a["L0_ffn_w2"][l, C0[i]:C0[i] + CW[i], :]) for i in range(3)], *w)

        load_attn_w(0, wqs)
        load_ffn_w(0)

        tables()
        t0 = V(lambda e: e.tensor_copy(mk[:, :, :].rearrange("p a b -> p (a b)"), mkf), ld_mk)
        t1 = V(lambda e: e.tensor_copy(idb[:, :], ident), ld_cst)
        t2 = V(lambda e: e.tensor_copy(sel[:, :, :].rearrange("p a b -> p (a b)"), self32), ld_mk)
        t3 = V(lambda e: e.memset(cstv[:, 0:1], EPS))
        t4 = V(lambda e: e.memset(cstv[:, 1:2], -64.0))
        t5 = V(lambda e: e.tensor_copy(cenr[:, :], cen), ld_cst)
        k_consts = [t0, t1, t2, t3, t4, t5]
        tb_ready = []
        for l in range(2):
            for c in range(2):
                dst = TB[:, l, c, :, :, :]
                src = TB[:, 1, c, :, :, :]
                sc = qks[:, l, :, :].rearrange("p a b -> p (a b)")[:, None, :].to_broadcast([128, NT, 2 * DH])
                d2 = dst.rearrange("p t a b -> p t (a b)")
                s2 = src.rearrange("p t a b -> p t (a b)")
                tb_ready.append(G(lambda e, d2=d2, s2=s2, sc=sc: e.tensor_tensor(d2, s2, sc, ALU.mult),
                                  ld_tb, tb_ready[-2:]))
        eps_ap = cstv[:, 0:1]

        def barrier():
            return Q.last()

        ring = Ring(8)
        x_parts = []
        for g in range(8):
            k, held = ring.take()
            for j in range(4):
                mm = T(lambda e, g=g, j=j, k=k: e.transpose(PS[:, k, j * 128:(j + 1) * 128], xtok[:, 4 * g + j, :], ident),
                       ld_cst, ld_x[g // 2], held)
            dst = xs[1][:, g // 4, (g % 4) * 512:(g % 4 + 1) * 512]
            x_parts.append(V(lambda e, k=k, dst=dst: e.tensor_copy(dst, PS[:, k, :]), mm))
        scopes.pop().close()

        def chunk(t, c):
            return t[:, c // 4, (c % 4) * CH:(c % 4 + 1) * CH]

        def layernorm(ready, free, put):
            sq = [arena(CH, [CH]) for _ in range(3)]
            rs = [arena(CH, [CH]) for _ in range(3)]
            ps, rsq, rrs = Ring(8, free), Ring(3, free), Ring(3, free)
            done = []
            held = []
            for c in range(NCH + 2):
                if c < NCH:
                    kc, h = ps.take()
                    T(lambda e, c=c, kc=kc: e.matmul(PS[:, kc, :], cenr[:, :], chunk(HH, c), start=True, stop=False),
                      ready[c], h, t5)
                    m1 = T(lambda e, c=c, kc=kc: e.matmul(PS[:, kc, :], cenr[:, :], chunk(HL, c), start=False, stop=True))
                    ks, h = rsq.take()
                    s1 = A(lambda e, kc=kc, ks=ks: e.activation(sq[ks], PS[:, kc, :], ACT.Square), m1, h)
                    held.append((c, kc, ks, s1))
                if c >= 2:
                    cc, kc, ks, s1 = held[c - 2]
                    kv, h = ps.take()
                    m2 = T(lambda e, kv=kv, ks=ks: e.matmul(PS[:, kv, :], avg, sq[ks], start=True, stop=True), s1, h)
                    rsq.free(ks, m2)
                    kr, h = rrs.take()
                    s2 = A(lambda e, kv=kv, kr=kr: e.activation(rs[kr], PS[:, kv, :], ACT.Ln, bias=eps_ap), m2, h, t3)
                    ps.free(kv, s2)
                    s3 = A(lambda e, kr=kr: e.activation(rs[kr], rs[kr], ACT.Exp, scale=-0.5), s2)
                    v, out = put(cc, PS[:, kc, :], rs[kr], s3)
                    ps.free(kc, v)
                    rrs.free(kr, v)
                    done.append(out)
            return done

        @phase
        def self_attention(ready):
            xT = xs[1]
            bar = barrier()
            ntok = arena(0, [NT, 128])
            nf = [arena(0, [128]) for _ in range(2)]
            nh = [arena(0, [128], F32R) for _ in range(2)]
            nl = [arena(0, [128], F32R) for _ in range(2)]
            E = [arena(0, [1024]) for _ in range(2)]
            Eh = [arena(0, [N], F32R) for _ in range(2)]
            El = [arena(0, [N], F32R) for _ in range(2)]
            zz = arena(0, [8])
            out_ops = []

            def sequence(b):
                tr = []
                before = out_ops[-4:]
                for g in range(4):
                    for j in range(4):
                        t = 4 * g + j
                        mm = T(lambda e, g=g, j=j, t=t: e.transpose(PS[:, 4 + g, j * 128:(j + 1) * 128],
                                                                 yT[:, b, t * 128:(t + 1) * 128], ident),
                               bar, ready[4 * b + g], before)
                    tr.append(V(lambda e, g=g: e.tensor_copy(ntok[:, 4 * g:4 * g + 4, :].rearrange("p a b -> p (a b)"),
                                                            PS[:, 4 + g, :]), mm, bar))
                ex, pv, scl, lows = {}, {}, {}, {}

                def scores(m):
                    for h in range(2):
                        for j in range(2):
                            o = PS[:, 2 * h + j, :]
                            ms = slice(m * 128, (m + 1) * 128)
                            ns = slice((2 * h + j) * 512, (2 * h + j + 1) * 512)
                            mm = halves(o, (HH[:, b, ms], HL[:, b, ms]), (HH[:, b, ns], HL[:, b, ns]),
                                        [ex.get((m - 1, h)), bar, ready])
                        ex[m, h] = A(lambda e, h=h: e.activation(
                            E[h], PS[:, 2 * h:2 * h + 2, :].rearrange("p a b -> p (a b)"),
                            ACT.Exp, bias=cstv[:, 1:2], accum_out=zz[:, 2 * (m % 2) + h:2 * (m % 2) + h + 1]),
                            mm, lows.get((m - 1, h)), scl.get(m - 2), t4, bar)
                        hs = slice(h * 1024, (h + 1) * 1024)
                        lows[m, h] = split(Eh[m % 2][:, hs], El[m % 2][:, hs], E[h], A, V, ex[m, h], pv.get(m - 2))
                    q = m % 2
                    s = V(lambda e: e.tensor_tensor(zz[:, 4 + q:5 + q], zz[:, 2 * q:2 * q + 1], zz[:, 2 * q + 1:2 * q + 2],
                                                    ALU.add), ex[m, 0], ex[m, 1], scl.get(m - 2))
                    r = V(lambda e: e.reciprocal(zz[:, 6 + q:7 + q], zz[:, 4 + q:5 + q]), s)
                    f = V(lambda e: e.tensor_scalar(nf[q], ntok[:, m, :], zz[:, 6 + q:7 + q], None, ALU.mult),
                          r, tr[m // 4], pv.get(m - 2), scl.get(m - 2))
                    scl[m] = split(nh[q], nl[q], nf[q], V, V, f)

                def weighted(m):
                    for j in range(4):
                        js = slice(j * 512, (j + 1) * 512)
                        (ah, al), (bh, bl) = (nh[m % 2], nl[m % 2]), (Eh[m % 2][:, js], El[m % 2][:, js])
                        o = PS[:, 4 + j, :]
                        w = [scl[m], lows[m, j // 2], tr]
                        T(lambda e, o=o, ah=ah, bh=bh: e.matmul(o, ah, bh, start=(m == 0), stop=False), w)
                        T(lambda e, o=o, ah=ah, bl=bl: e.matmul(o, ah, bl, start=False, stop=False))
                        mm = T(lambda e, o=o, al=al, bh=bh: e.matmul(o, al, bh, start=False, stop=(m == NT - 1)))
                    pv[m] = mm

                for m in range(NT + 1):
                    if m < NT:
                        scores(m)
                    if m >= 1:
                        weighted(m - 1)
                for j in range(4):
                    dst = xT[:, b, j * 512:(j + 1) * 512]
                    out_ops.append(V(lambda e, j=j, dst=dst: e.tensor_tensor(dst, PS[:, 4 + j, :], dst, ALU.add),
                                     pv[NT - 1]))

            for b in range(NB):
                sequence(b)
            return out_ops

        def shift(ready, free):
            done = []
            z = [V(lambda e, t=t: e.tensor_scalar(t[64:128, :, 0:1], vec[64:128, 0:NB].rearrange("p (b o) -> p b o", o=1),
                                                  0.0, None, ALU.mult), free, ld_small) for t in (HH, HL)]
            for c in range(NCH):
                b, n0 = c // 4, (c % 4) * CH
                o = split(HH[0:64, b, n0:n0 + CH], HL[0:64, b, n0:n0 + CH], yT[0:64, b, n0:n0 + CH], A, V, ready[c], free)
                o2 = split(HH[64:128, b, n0 + 1:n0 + 1 + CH], HL[64:128, b, n0 + 1:n0 + 1 + CH],
                           yT[64:128, b, n0:n0 + CH], A, V, ready[c], free)
                done.append([o, o2, z, done[-1][1] if c % 4 else None])
            return done

        def plain(src, ready, free):
            return [split(chunk(HH, c), chunk(HL, c), chunk(src, c), A, V if c % 2 else G, ready[c], free)
                    for c in range(NCH)]

        @phase
        def local_attention(l, ready, saved):
            bar = [barrier(), saved]
            h_ready = shift(ready, bar)
            sq = arena(1024, [NH * 2, DH])
            qn = arena(1024, [NH * 2, DH])
            ta = [arena(1024, [NH * 2, DH]) for _ in range(2)]
            tc = arena(1024, [NH * 2, DH])
            ss = arena(64, [2, 32])
            RQ = 8
            qH = arena(0, [4, RQ * 128 + 64], BF16)
            qL = arena(0, [4, RQ * 128 + 64], BF16)
            kH = arena(0, [4, RQ * 128 + 64], BF16)
            kL = [arena(0, [4, 128], BF16) for _ in range(4)]
            va = [arena(1024, [4, 256]) for _ in range(2)]
            PT = [arena(384, [2, 192]) for _ in range(3)]
            ND = [[arena(768, [2, 2, 192]) for _ in range(2)] for _ in range(2)]
            mx = [arena(8, [8]) for _ in range(2)]
            mT = arena((RQ * 128 + 64) // 2, [RQ * 128 + 64], BF16, 8)
            lnd = [arena(256, [2, 128]) for _ in range(2)]
            ot = [arena(512, [4, 128]) for _ in range(2)]
            ones = [V(lambda e, i=i: e.memset(va[i][:, :, 64:192], 1.0), bar) for i in range(2)]
            zk = V(lambda e: e.memset(kH[:, :, 0:64], 0.0), bar)
            ra, rm, rs, rv = Ring(3, bar), Ring(2, bar), Ring(2, bar), Ring(1, bar)
            rqn, rta, rtc, rsq, rss = Ring(1, bar), Ring(2, bar), Ring(1, bar), Ring(1, bar), Ring(2, bar)
            rkL, rva, rPT, rmx, rlnd, rot = (Ring(4, bar), Ring(2, bar), Ring(3, bar), Ring(2, bar), Ring(2, bar),
                                             Ring(2, bar))
            wait_w = wait_attn_w[0]
            R = {}
            tiles = [(b, t) for b in range(NB) for t in range(NT)]
            nt = len(tiles)

            def project(i):
                b, t = tiles[i]
                ops = []
                banks = []
                for x in range(2):
                    k, h = ra.take()
                    ts, xsl = slice(t * 128, (t + 1) * 128), slice(x * 512, (x + 1) * 512)
                    ops.append(halves(PS[:, k, :], (HH[:, b, ts], HL[:, b, ts]), (wqh[:, xsl], wql[:, xsl]),
                                      [h, h_ready[i // 4], wait_w, bar]))
                    banks.append(k)
                ks, h = rsq.take()
                a1 = [A(lambda e, x=x: e.activation(sq[:, 8 * x:8 * x + 8, :].rearrange("p a b -> p (a b)"),
                                                    PS[:, banks[x], :], ACT.Square), ops[x], h) for x in range(2)]
                R["p", i] = (ops, banks, ks, a1)

            def norms(i):
                ops, banks, ks, a1 = R["p", i]
                kss, h2 = rss.take()
                v1 = V(lambda e: e.tensor_reduce(ss[:, kss, 0:16], sq, AX.X, ALU.add), a1, h2)
                rsq.free(ks, v1)
                v2 = V(lambda e: e.tensor_scalar(ss[:, kss, 0:16], ss[:, kss, 0:16], 1e-24, None, ALU.max), v1)
                a2 = A(lambda e: e.activation(ss[:, kss, 16:32], ss[:, kss, 0:16], ACT.Ln), v2)
                a3 = A(lambda e: e.activation(ss[:, kss, 16:32], ss[:, kss, 16:32], ACT.Exp, scale=-0.5), a2)
                R["ss", i] = (kss, a3)

            def rope(i):
                b, t = tiles[i]
                ops, banks, _, _ = R.pop(("p", i))
                kss, a3 = R.pop(("ss", i))
                _, h = rqn.take()
                v3 = [V(lambda e, x=x: e.tensor_tensor(
                    qn[:, 8 * x:8 * x + 8, :], PS[:, banks[x], :].rearrange("p (a b) -> p a b", b=DH),
                    ss[:, kss, 16 + 8 * x:24 + 8 * x].rearrange("p (a o) -> p a o", o=1).to_broadcast([128, NH, DH]), ALU.mult),
                    a3, h) for x in range(2)]
                ra.free(banks[0], v3[0])
                ra.free(banks[1], v3[1])
                rss.free(kss, v3)
                ka, h = rta.take()
                kc, h2 = rtc.take()
                qv = qn.rearrange("p (x h) d -> p x h d", x=2)
                tab = lambda c: TB[:, l, c, t, :, :].rearrange("p x (o d) -> p x o d", o=1).to_broadcast([128, 2, NH, DH])
                v4 = V(lambda e: e.tensor_tensor(ta[ka].rearrange("p (x h) d -> p x h d", x=2), qv, tab(0), ALU.mult),
                       v3, h, tb_ready)
                g1 = G(lambda e: e.tensor_tensor(tc.rearrange("p (x h) d -> p x h d", x=2), qv, tab(1), ALU.mult),
                       v3, h2, tb_ready)
                rqn.free(0, v4, g1)
                tv = ta[ka]
                g2 = [G(lambda e, s=s: e.tensor_tensor(tv[:, :, 32 * s:32 * s + 32], tv[:, :, 32 * s:32 * s + 32],
                                                       tc[:, :, 32 * (1 - s):32 * (1 - s) + 32], ALU.add), v4, g1)
                      for s in range(2)]
                rtc.free(kc, g2)
                R["r", i] = (ka, g2)

            def turn(i, x):
                b, t = tiles[i]
                ka, g2 = R["r", i]
                k, h = ra.take()
                for j in range(4):
                    mm = T(lambda e, j=j: e.transpose(
                        PS[:, k, j * 128:(j + 1) * 128],
                        ta[ka][:, 8 * x + 2 * j:8 * x + 2 * j + 2, :].rearrange("p a b -> p (a b)"), ident), h, g2)
                src = PS[:, k, :].rearrange("p (a b) -> p a b", b=128)
                c0 = (i % RQ) * 128
                w = [bar, R.get(("S", i - RQ)), R.get(("S", i - RQ - 1)), R.get(("Mw", i - RQ)),
                     R.get(("Mw", i - RQ + 1))]
                if x == 0:
                    o = split(qH[:, :, c0:c0 + 128], qL[:, :, c0:c0 + 128], src, A, V, mm, w)
                    if i % RQ == 0 and i > 0:
                        ce = RQ * 128
                        o2 = A(lambda e: e.copy(qH[:, :, ce:ce + 64], src[:, :, 0:64]), mm, w, o)
                        o3 = V(lambda e: e.tensor_tensor(qL[:, :, ce:ce + 64], src[:, :, 0:64], qH[:, :, ce:ce + 64],
                                                         ALU.subtract), o2)
                        o += [o2, o3]
                    R["q", i] = o
                    ra.free(k, o)
                else:
                    kk, h = rkL.take()
                    o = split(kH[:, :, 64 + c0:192 + c0], kL[kk], src, A, V, mm, w, h)
                    if i % RQ == RQ - 1:
                        if t < NT - 1:
                            o.append(A(lambda e: e.copy(kH[:, :, 0:64], src[:, :, 64:128]), mm, w, o))
                        else:
                            o.append(V(lambda e: e.memset(kH[:, :, 0:64], 0.0), w, o))
                    R["k", i] = (kk, o)
                    ra.free(k, o)
                    rta.free(ka, mm)
                    del R["r", i]

            def maxima(i, n):
                g, s = divmod(n, 2)
                b, t = tiles[i]
                c0 = (i % RQ) * 128
                k, h = rm.take()
                need = [R["q", i], R["k", i][1], R["k", i - 1][1] if i else zk]
                T(lambda e: e.matmul(PS[:, 3 + k, 0:384], idb[:, :], mk[:, 0 if t else 1, :], start=True, stop=False,
                                     skip_group_check=True), h, k_consts)
                for c in range(2):
                    mm = T(lambda e, c=c: e.matmul(PS[:, 3 + k, 192 * c:192 * c + 192],
                                                   qH[64 * s:64 * s + 64, 2 * g + c, c0:c0 + 128],
                                                   kH[64 * s:64 * s + 64, 2 * g + c, c0:c0 + 192],
                                                   start=False, stop=True, skip_group_check=True), need)
                if n == 0:
                    R["mx", i] = [rmx.take(), []]
                (km, h), lst = R["mx", i]
                v = V(lambda e: e.tensor_reduce(mx[km][:, 4 * g + s:4 * g + s + 3:2],
                                                PS[:, 3 + k, 0:384].rearrange("p (a b) -> p a b", b=192), AX.X, ALU.max,
                                                negate=True), mm, h)
                rm.free(k, v)
                lst.append(v)
                if n == 3:
                    R["Mw", i] = mm

            def turn_maxima(i):
                (km, _), lst = R.pop(("mx", i))
                k, h = ra.take()
                mm = T(lambda e: e.transpose(PS[0:8, k, 0:128], mx[km], ident), lst, h)
                rmx.free(km, mm)
                c0 = (i % RQ) * 128
                w = [bar, R.get(("S", i - RQ)), R.get(("S", i - RQ - 1))]
                o = [A(lambda e: e.copy(mT[:, c0:c0 + 128], PS[0:8, k, 0:128]), mm, w)]
                if i % RQ == 0 and i > 0:
                    o.append(A(lambda e: e.copy(mT[:, RQ * 128:RQ * 128 + 64], PS[0:8, k, 0:64]), mm, w))
                ra.free(k, o)
                R["m", i] = o

            def values(i):
                b, t = tiles[i]
                k, h = ra.take()
                ts = slice(t * 128, (t + 1) * 128)
                mm = halves(PS[:, k, :], (HH[:, b, ts], HL[:, b, ts]), (wqh[:, 1024:1536], wql[:, 1024:1536]),
                            [h, h_ready[i // 4], wait_w, bar])
                kv, h = rva.take()
                src = PS[:, k, :].rearrange("p (a s d) -> p a s d", s=2, d=DH)
                o = [A(lambda e, s=s: e.copy(va[kv][:, :, 192 * s:192 * s + 64], src[:, :, s, :]), mm, h, ones)
                     for s in range(2)]
                ra.free(k, o)
                R["v", i] = (kv, o)

            def scores(i, n):
                g, s = divmod(n, 2)
                b, t = tiles[i]
                nq = 192 if t < NT - 1 else 128
                c0 = (i % RQ) * 128
                kk, okt = R["k", i]
                need = [R["q", i], R["m", i], okt]
                if nq == 192:
                    need += [R["q", i + 1], R["m", i + 1]]
                k, h = rs.take()
                T(lambda e: e.matmul(PS[:, 5 + k, 0:384], idb[:, :], mk[:, 2, :], start=True, stop=False,
                                     skip_group_check=True), h, k_consts)
                for c in range(2):
                    T(lambda e, c=c: e.matmul(PS[:, 5 + k, 192 * c:192 * c + nq], sel[:, 4 * g + 2 * c + s, :],
                                              mT[:, c0:c0 + nq], start=False, stop=False, skip_group_check=True), need)
                rows = slice(64 * s, 64 * s + 64)
                for c in range(2):
                    p = 2 * g + c
                    kh, kl = kH[rows, p, 64 + c0:192 + c0], kL[kk][rows, p, :]
                    qh, ql = qH[rows, p, c0:c0 + nq], qL[rows, p, c0:c0 + nq]
                    for x, y in ((kh, qh), (kh, ql), (kl, qh)):
                        mm = T(lambda e, c=c, x=x, y=y: e.matmul(PS[:, 5 + k, 192 * c:192 * c + nq], x, y, start=False,
                                                                 stop=True, skip_group_check=True), need)
                kp, h = rPT.take()
                src = PS[:, 5 + k, 0:384].rearrange("p (a b) -> p a b", b=192)[:, :, 0:nq]
                ae = A(lambda e: e.activation(PT[kp][:, :, 0:nq], src, ACT.Exp), mm, h)
                rs.free(k, ae)
                R["e", i, n] = (kp, ae)
                if n == 3:
                    rkL.free(kk, mm)
                    R["S", i] = mm

            def gather(i, n):
                g, s = divmod(n, 2)
                b, t = tiles[i]
                nq = 192 if t < NT - 1 else 128
                kv, ov = R["v", i]
                kp, ae = R.pop(("e", i, n))
                k, h = rv.take()
                for c in range(2):
                    mm = T(lambda e, c=c: e.matmul(PS[:, 7 + k, 192 * c:192 * c + nq],
                                                   va[kv][:, 2 * g + c, 128 * s:128 * s + 128],
                                                   PT[kp][:, c, 0:nq],
                                                   start=True, stop=True, skip_group_check=True), h, ae, ov)
                rPT.free(kp, mm)
                if n == 3:
                    rva.free(kv, mm)
                nd, old = ND[g][i % 2], ND[g][(i + 1) % 2]
                w = R.get(("nd", i - 1, g)), R.get(("nd", i - 2, g)), bar
                lo, hi = slice(64 * s, 64 * s + 64), slice(64 - 64 * s, 128 - 64 * s)
                src = PS[:, 7 + k, 0:384].rearrange("p (a b) -> p a b", b=192)[:, :, 0:nq]
                cp = [A(lambda e: e.copy(nd[lo, 0, :, 0:nq], src[lo, :, :]), mm, w),
                      A(lambda e: e.copy(nd[lo, 1, :, 0:nq], src[hi, :, :]), mm, w)]
                rv.free(k, cp)
                R["cp", i, n] = cp

            def finish(i, g):
                b, t = tiles[i]
                nd, old = ND[g][i % 2], ND[g][(i + 1) % 2]
                cp = R.pop(("cp", i, 2 * g)) + R.pop(("cp", i, 2 * g + 1))
                if t:
                    cp = [V(lambda e: e.tensor_tensor(nd[:, :, :, 0:64], nd[:, :, :, 0:64], old[:, :, :, 128:192], ALU.add),
                            cp)]
                kl, h = rlnd.take()
                a1 = A(lambda e: e.activation(lnd[kl], nd[:, 1, :, 0:128], ACT.Ln), cp, h)
                a2 = A(lambda e: e.activation(lnd[kl], lnd[kl], ACT.Exp, scale=-1.0), a1)
                if g == 0:
                    R["ot", i] = [rot.take(), []]
                (ko, h), lst = R["ot", i]
                o = V(lambda e: e.tensor_tensor(ot[ko][:, 2 * g:2 * g + 2, :], nd[:, 0, :, 0:128], lnd[kl], ALU.mult),
                      a2, cp, h)
                rlnd.free(kl, o)
                R["nd", i, g] = [o, cp]
                lst.append(o)

            def project_out(i):
                b, t = tiles[i]
                (ko, _), lst = R.pop(("ot", i))
                k, h = ra.take()
                for j in range(4):
                    mm = T(lambda e, j=j: e.matmul(PS[:, k, 0:128], wo[:, j, :], ot[ko][:, j, :],
                                                   start=(j == 0), stop=(j == 3)), h, lst, wait_w)
                rot.free(ko, mm)
                dst = yT[:, b, t * 128:(t + 1) * 128]
                o = V(lambda e: e.tensor_tensor(dst, PS[:, k, 0:128], dst, ALU.add), mm, bar)
                ra.free(k, o)
                R["out", i] = o

            for s in range(nt + 7):
                def on(lag):
                    return 0 <= s - lag < nt

                if on(0):
                    project(s)
                if on(2):
                    maxima(s - 2, 0)
                if on(3):
                    turn_maxima(s - 3)
                if on(5):
                    gather(s - 5, 3)
                if on(0):
                    norms(s)
                if on(2):
                    maxima(s - 2, 3)
                if on(4):
                    scores(s - 4, 0)
                if on(5):
                    finish(s - 5, 1)
                if on(2):
                    maxima(s - 2, 2)
                if on(4):
                    scores(s - 4, 1)
                    gather(s - 4, 0)
                    scores(s - 4, 2)
                if on(0):
                    rope(s)
                if on(4):
                    scores(s - 4, 3)
                if on(1):
                    turn(s - 1, 0)
                if on(4):
                    gather(s - 4, 1)
                if on(1):
                    turn(s - 1, 1)
                if on(3):
                    values(s - 3)
                if on(2):
                    maxima(s - 2, 1)
                if on(4):
                    gather(s - 4, 2)
                    finish(s - 4, 0)
                if on(5):
                    project_out(s - 5)
            return [[R["out", 4 * c + j] for j in range(4)] for c in range(NCH)], T_last(Q)

        def T_last(Q):
            return Q.q["tensor"][-1]

        @phase
        def feed_forward(l, ready, stage_next):
            bar = barrier()
            h_ready = shift(ready, bar)
            nf = [arena(0, [CH]) for _ in range(2)]
            rnf = Ring(2, bar)

            def put(c, ps, rs, w):
                k, h = rnf.take()
                v = V(lambda e: e.tensor_tensor(nf[k], ps, rs, ALU.mult), w, h)
                o = split(chunk(HH, c), chunk(HL, c), nf[k], A, G, v)
                rnf.free(k, o)
                return v, o

            hn = layernorm(h_ready, bar, put)
            bar2 = barrier()
            gl = [arena(CH, [CH]) for _ in range(3)]
            hf = [arena(CH, [CH]) for _ in range(3)]
            hh = [arena(CH, [CH], F32R) for _ in range(6)]
            hl = [arena(CH, [CH], F32R) for _ in range(6)]
            w1g = arena(0, [2 * HID])
            if stage_next is not None:
                stage = arena(0, [1536])
                load_attn_w(stage_next, stage, bar)
            f1 = V(lambda e: e.tensor_scalar(w1g, w1[:, :], vec[:, l:l + 1], None, ALU.mult), wait_ffn_w[0],
                   ld_small, bar)
            fold = split(w1h[:, :], w1l[:, :], w1g, V, V, f1) + \
                [o for i in range(3) for o in split(w2h[0:CW[i], i, :], w2l[0:CW[i], i, :], w2[0:CW[i], i, :], V, V,
                                                    wait_ffn_w[0], bar)]
            for i in range(6):
                s0 = HID * (i // 3) + C0[i % 3]
                wd = CW[i % 3]
                mm = T(lambda e, i=i, s0=s0, wd=wd: e.matmul(PS[0:wd, 0, i:i + 1], w1[:, s0:s0 + wd], vec[:, 2 + l:3 + l],
                                                            start=True, stop=True), wait_ffn_w[0], ld_small, bar2)
            bb = [V(lambda e, i=i: e.tensor_tensor(b1r[0:CW[i % 3], i:i + 1], PS[0:CW[i % 3], 0, i:i + 1],
                                                   b1c[0:CW[i % 3], l, i:i + 1], ALU.add), mm, bar) for i in range(6)]
            rf = Ring(3, bar2)
            r6, r2, rg, rh = Ring(6, [bb]), Ring(2, bar2), Ring(3, bar2), Ring(6, bar2)
            done = []
            pend = []

            def second(c, items):
                k, h = r2.take()
                for i, (kh, v) in enumerate(items):
                    mm = halves(PS[:, 6 + k, :], (w2h[0:CW[i], i, :], w2l[0:CW[i], i, :]),
                                (hh[kh][0:CW[i], :], hl[kh][0:CW[i], :]), [h, v, fold], more=i > 0, last=i == 2)
                    rh.free(kh, mm)
                dst = chunk(yT, c)
                o = V(lambda e: e.scalar_tensor_tensor(dst, PS[:, 6 + k, :], vec[:, 4 + l:5 + l], dst, ALU.add, ALU.add),
                      mm, bar2)
                r2.free(k, o)
                done.append(o)
                return mm

            lastT = None
            for c in range(NCH + 1):
                if c < NCH:
                    items = []
                    for i in range(3):
                        wd = CW[i]
                        kg, h = r6.take()
                        cs = slice(HID + C0[i], HID + C0[i] + wd)
                        m1 = halves(PS[0:wd, kg, :], (w1h[:, cs], w1l[:, cs]), (chunk(HH, c), chunk(HL, c)),
                                    [h, hn[c], fold, bar2])
                        ka, h = r6.take()
                        cs = slice(C0[i], C0[i] + wd)
                        m2 = halves(PS[0:wd, ka, :], (w1h[:, cs], w1l[:, cs]), (chunk(HH, c), chunk(HL, c)), [h])
                        q, h = rg.take()
                        g1 = A(lambda e, i=i, kg=kg, wd=wd, q=q: e.activation(gl[q][0:wd, :], PS[0:wd, kg, :], ACT.Gelu,
                                                                              bias=b1r[0:wd, 3 + i:4 + i]), m1, h, bb)
                        r6.free(kg, g1)
                        kf, h = rf.take()
                        v = V(lambda e, i=i, ka=ka, wd=wd, q=q, kf=kf: e.scalar_tensor_tensor(
                            hf[kf][0:wd, :], PS[0:wd, ka, :], b1r[0:wd, i:i + 1], gl[q][0:wd, :], ALU.add, ALU.mult),
                            m2, g1, h, bb)
                        r6.free(ka, v)
                        rg.free(q, v)
                        kh, h = rh.take()
                        o = split(hh[kh][0:wd, :], hl[kh][0:wd, :], hf[kf][0:wd, :], A, V, v, h)
                        rf.free(kf, o)
                        items.append((kh, o))
                    pend.append(items)
                if c >= 1:
                    lastT = second(c - 1, pend[c - 1])
            return done, lastT

        n_saved = [0]

        def ffn(ready, last):
            s = sem(f"save{n_saved[0]}")
            n_saved[0] += 1
            xT = xs[1]
            Q.op("sync", lambda e: e.dma_start(xsave, xT[:, :, :].rearrange("p b n -> p (b n)")).then_inc(s, 16), barrier())
            saved = Load(s, 16)
            xs[0].close()
            for l in range(2):
                ready, lt = local_attention(l, ready, saved)
                end = last and l == 1
                if l == 1:
                    take_x()
                    xT2 = xs[1]
                    back = load([(xT2[:, :, :].rearrange("p b n -> p (b n)"), xsave)], saved, barrier())
                ready, lt = feed_forward(l, ready, None if end else 1 - l)
                if not end:
                    load_ffn_w(1 - l, lt)
                tables()
            res = []
            for c in range(NCH):
                xc = chunk(xs[1], c)
                res.append(V(lambda e, c=c, xc=xc: e.tensor_tensor(xc, xc, chunk(yT, c), ALU.add),
                             ready[c], back))
            return res

        @phase
        def weighted_values(ready):
            xT = xs[1]
            bar = barrier()
            TT = NB * NT
            st = arena(5 * TT, [5, TT])
            dd = [arena(512, [4, 128]) for _ in range(2)]
            d2 = [arena(512, [4, 128]) for _ in range(2)]
            dm = [arena(256, [2, 128]) for _ in range(2)]
            w = arena(16 * TT, [16, TT])
            h4 = arena(4 * TT, [4, TT])
            h5 = arena(4 * TT, [4, TT])
            sm = arena(32, [32])
            wbr = [arena(128, [128]) for _ in range(4)]
            wbs = [arena(512, [512]) for _ in range(2)]
            vs = [arena(512, [512]) for _ in range(2)]
            rp, rd = Ring(3, bar), Ring(2, bar)
            seq = []
            for j in range(TT // 2):
                b = j // (NT // 2)
                k, h = rp.take()
                for s in range(2):
                    n0 = (2 * j + s) % NT * 128
                    mm = T(lambda e, s=s, n0=n0, b=b, k=k: e.matmul(PS[:, k, 256 * s:256 * s + 256], yT[:, b, n0:n0 + 128],
                                                                    wb[:, 0:256], start=True, stop=True,
                                                                    skip_group_check=True), h, ready, bar, ld_small)
                q, h = rd.take()
                p4 = PS[:, k, :].rearrange("p (a b) -> p a b", b=128)
                mu = st[:, 0:2, 2 * j:2 * j + 2].rearrange("p a b -> p b a")
                v1 = V(lambda e, p4=p4, mu=mu: e.tensor_reduce(mu, p4.rearrange("p (a c) b -> p a c b", c=2), AX.X, ALU.add),
                       mm, bar)
                v2 = V(lambda e, mu=mu: e.tensor_scalar(mu, mu, 1.0 / 128, None, ALU.mult), v1)
                v3 = V(lambda e, p4=p4, mu=mu, q=q: e.tensor_tensor(
                    dd[q].rearrange("p (a c) b -> p a c b", c=2), p4.rearrange("p (a c) b -> p a c b", c=2),
                    mu.rearrange("p a (c o) -> p a c o", o=1).to_broadcast([128, 2, 2, 128]), ALU.subtract), v2, h)
                rp.free(k, v3)
                a1 = A(lambda e, q=q: e.activation(d2[q], dd[q], ACT.Square), v3, h)
                dv = dd[q].rearrange("p (a c) b -> p a c b", c=2)
                g1 = G(lambda e, q=q, dv=dv: e.tensor_tensor(dm[q], dv[:, :, 0, :], dv[:, :, 1, :], ALU.mult), v3, h)
                sg = st[:, 2:4, 2 * j:2 * j + 2].rearrange("p a b -> p b a")
                v4 = V(lambda e, q=q, sg=sg: e.tensor_reduce(sg, d2[q].rearrange("p (a c) b -> p a c b", c=2), AX.X, ALU.add), a1)
                v5 = V(lambda e, q=q, j=j: e.tensor_reduce(st[:, 4, 2 * j:2 * j + 2], dm[q], AX.X, ALU.add), g1)
                rd.free(q, v4, v5)
                seq += [v4, v5]
            c1, c2 = vec[:, 9:10], vec[:, 10:11]
            prev = [seq + [bar]]

            def V1(fn, *more):
                prev[0] = V(fn, prev[0], *more)
                return prev[0]

            mq, mkk, sq2, sk2, sqk = (st[:, i, :] for i in range(5))
            i127 = 1.0 / 127
            V1(lambda e: e.tensor_tensor(w[:, 0, :], mq, mkk, ALU.mult))
            V1(lambda e: e.tensor_scalar(w[:, 0, :], w[:, 0, :], 2.0, c1, ALU.mult, ALU.add))
            V1(lambda e: e.tensor_scalar(w[:, 1, :], sqk, 2.0 * i127, c2, ALU.mult, ALU.add))
            V1(lambda e: e.tensor_tensor(w[:, 0, :], w[:, 0, :], w[:, 1, :], ALU.mult))
            V1(lambda e: e.tensor_tensor(w[:, 1, :], mq, mq, ALU.mult))
            V1(lambda e: e.tensor_tensor(w[:, 2, :], mkk, mkk, ALU.mult))
            V1(lambda e: e.scalar_tensor_tensor(w[:, 1, :], w[:, 1, :], c1, w[:, 2, :], ALU.add, ALU.add))
            V1(lambda e: e.tensor_tensor(w[:, 2, :], sq2, sk2, ALU.add))
            V1(lambda e: e.tensor_scalar(w[:, 2, :], w[:, 2, :], i127, c2, ALU.mult, ALU.add))
            V1(lambda e: e.tensor_tensor(w[:, 1, :], w[:, 1, :], w[:, 2, :], ALU.mult))
            V1(lambda e: e.tensor_scalar(w[:, 1, :], w[:, 1, :], 1e-7, None, ALU.add))
            V1(lambda e: e.reciprocal(w[:, 2, :], w[:, 1, :]))
            V1(lambda e: e.tensor_tensor(w[:, 0, :], w[:, 0, :], w[:, 2, :], ALU.mult))
            va_ = V1(lambda e: e.tensor_tensor(w[:, 3, :], w[:, 0, :], w[:, 0, :], ALU.mult))

            def neighbours(src, nch, bank, *wait):
                view = lambda ap: ap.rearrange("p (c b t) -> p c b t", b=NB, t=NT)
                s = view(src)
                ops = []
                for d, (m, ed) in enumerate(((sdn, edn), (sup, eup))):
                    o = PS[:, bank + d, 0:nch * TT]
                    ov = view(o)
                    T(lambda e, o=o, m=m: e.matmul(o, m, src, start=True, stop=False, skip_group_check=True), wait)
                    for c in range(nch):
                        for b in range(NB):
                            do = ov[:, c, b, 1:NT] if d == 0 else ov[:, c, b, 0:NT - 1]
                            di = s[:, c, b, 0:NT - 1] if d == 0 else s[:, c, b, 1:NT]
                            mm = T(lambda e, do=do, di=di, ed=ed: e.matmul(do, ed, di, start=False, stop=True,
                                                                          skip_group_check=True))
                    ops.append(mm)
                return ops

            nb = neighbours(w[:, 3, :], 1, 3, va_, bar)
            for c in range(4):
                wc = lambda k: vec[:, 12 + 3 * c + k:13 + 3 * c + k]
                V1(lambda e, c=c: e.tensor_scalar(h4[:, c, :], w[:, 3, :], vec[:, 13 + 3 * c:14 + 3 * c], None, ALU.mult))
                for k, d in ((0, 0), (2, 1)):
                    V1(lambda e, c=c, k=k, d=d: e.scalar_tensor_tensor(
                        h4[:, c, :], PS[:, 3 + d, 0:TT], vec[:, 12 + 3 * c + k:13 + 3 * c + k], h4[:, c, :],
                        ALU.mult, ALU.add), nb)
            g5 = lambda ap: ap.rearrange("p (g c) (b t) -> p g c b t", g=2, b=NB)

            def group_mean(src, bank, *more):
                for g in range(2):
                    for b in range(NB):
                        V1(lambda e, g=g, b=b: e.tensor_reduce(sm[:, 2 * g + b:2 * g + b + 1], g5(src)[:, g, :, b, :],
                                                               AX.XY, ALU.add), *more)
                m = T(lambda e: e.matmul(PS[:, bank, 0:4], avg, sm[:, 0:4], start=True, stop=True), prev[0])
                return V1(lambda e: e.tensor_scalar(sm[:, 4:8], PS[:, bank, 0:4], 1.0 / 32, None, ALU.mult), m)

            group_mean(h4, 5)
            for g in range(2):
                for b in range(NB):
                    hv = g5(h4)[:, g, :, b, :]
                    V1(lambda e, g=g, b=b, hv=hv: e.tensor_scalar(hv, hv, sm[:, 4 + 2 * g + b:5 + 2 * g + b], None,
                                                                  ALU.subtract))
            V1(lambda e: e.tensor_tensor(h5, h4, h4, ALU.mult))
            v = group_mean(h5, 6)
            a1 = A(lambda e: e.activation(sm[:, 8:12], sm[:, 4:8], ACT.Ln, bias=eps_ap), v)
            a2 = A(lambda e: e.activation(sm[:, 12:16], sm[:, 8:12], ACT.Exp, scale=-0.5), a1)
            for g in range(2):
                for b in range(NB):
                    hv = g5(h4)[:, g, :, b, :]
                    V1(lambda e, g=g, b=b, hv=hv: e.tensor_scalar(hv, hv, sm[:, 12 + 2 * g + b:13 + 2 * g + b], None,
                                                                  ALU.mult), a2)
            for c in range(4):
                V1(lambda e, c=c: e.tensor_scalar(h4[:, c, :], h4[:, c, :], vec[:, 24 + c:25 + c], vec[:, 28 + c:29 + c],
                                                  ALU.mult, ALU.add))
            vh = V1(lambda e: e.tensor_scalar(h4, h4, 0.0, None, ALU.max))
            nb = neighbours(h4.rearrange("p a b -> p (a b)"), 4, 3, vh)
            for c in range(4):
                V1(lambda e, c=c: e.scalar_tensor_tensor(w[:, 3, :], h4[:, c, :], vec[:, 33 + 3 * c:34 + 3 * c], w[:, 3, :],
                                                         ALU.mult, ALU.add))
                for k, d in ((0, 0), (2, 1)):
                    V1(lambda e, c=c, k=k, d=d: e.scalar_tensor_tensor(
                        w[:, 3, :], PS[:, 3 + d, c * TT:(c + 1) * TT], vec[:, 32 + 3 * c + k:33 + 3 * c + k], w[:, 3, :],
                        ALU.mult, ALU.add), nb)
            v = V1(lambda e: e.tensor_reduce(sm[:, 16:18], yT[:, :, :], AX.X, ALU.add))
            v = V1(lambda e: e.tensor_scalar(sm[:, 16:18], sm[:, 16:18], 1.0 / N, None, ALU.mult))
            m = T(lambda e: e.matmul(PS[0:32, 5, 0:2], cw1[:, :], sm[:, 16:18], start=True, stop=True), v)
            v = V1(lambda e: e.tensor_scalar(sm[0:32, 18:20], PS[0:32, 5, 0:2], vec[0:32, 8:9], 0.0, ALU.add, ALU.max), m)
            m = T(lambda e: e.matmul(PS[:, 6, 0:2], cw2[:, :], sm[0:32, 18:20], start=True, stop=True), v)
            a0 = A(lambda e: e.activation(sm[:, 20:22], PS[:, 6, 0:2], ACT.Sigmoid, bias=vec[:, 7:8]), m)
            a1 = A(lambda e: e.activation(w[:, 4, :], w[:, 3, :], ACT.Sigmoid, bias=vec[:, 44:45]), prev[0])
            tables()
            a2 = A(lambda e: e.activation(w[:, 5, :], w[:, 4, :], ACT.Exp), a1)
            v = V1(lambda e: e.tensor_reduce(sm[:, 22:24], w[:, 5, :].rearrange("p (b t) -> p b t", b=NB), AX.X, ALU.add), a2)
            m = T(lambda e: e.matmul(PS[:, 5, 0:2], avg, sm[:, 22:24], start=True, stop=True), v)
            v = V1(lambda e: e.tensor_scalar(sm[:, 24:26], PS[:, 5, 0:2], 128.0, None, ALU.mult), m)
            v = V1(lambda e: e.reciprocal(sm[:, 26:28], sm[:, 24:26]))
            for b in range(NB):
                v = V1(lambda e, b=b: e.tensor_scalar(w[:, 6, NT * b:NT * (b + 1)], w[:, 5, NT * b:NT * (b + 1)],
                                                      sm[:, 26 + b:27 + b], None, ALU.mult))
            bar2 = [barrier()]
            rb, rwb, rv3, rws, rvs, ro = Ring(2, bar2), Ring(4, bar2), Ring(2, bar2), Ring(2, bar2), Ring(2, bar2), Ring(2, bar2)
            done = []
            for c in range(NCH):
                b = c // 4
                kv, h = rv3.take()
                mv = T(lambda e, c=c, kv=kv: e.matmul(PS[:, kv, :], wb[:, 256:384], chunk(yT, c), start=True, stop=True), h)
                kb, h = rb.take()
                for j in range(4):
                    t = 4 * c + j
                    kw, h2 = rwb.take()
                    v1 = V(lambda e, t=t, kw=kw: e.tensor_copy(wbr[kw], w[:, 6, t:t + 1].to_broadcast([128, 128])), v, h2)
                    mm = T(lambda e, j=j, kw=kw, kb=kb: e.matmul(PS[:, 2 + kb, 128 * j:128 * j + 128], wbr[kw], ident,
                                                                start=True, stop=True, skip_group_check=True), v1, h)
                    rwb.free(kw, mm)
                ks, h = rws.take()
                a1 = A(lambda e, kb=kb, ks=ks: e.copy(wbs[ks], PS[:, 2 + kb, :]), mm, h)
                rb.free(kb, a1)
                kz, h = rvs.take()
                v2 = V(lambda e, kv=kv, ks=ks, kz=kz, b=b: e.scalar_tensor_tensor(
                    vs[kz], PS[:, kv, :], sm[:, 20 + b:21 + b], wbs[ks], ALU.mult, ALU.mult), mv, a1, a0, h)
                rv3.free(kv, v2)
                rws.free(ks, v2)
                ko, h = ro.take()
                mo = T(lambda e, ko=ko, kz=kz: e.matmul(PS[:, 4 + ko, :], wp[:, :], vs[kz], start=True, stop=True), v2, h)
                rvs.free(kz, mo)
                o = V(lambda e, c=c, ko=ko: e.scalar_tensor_tensor(chunk(xT, c), PS[:, 4 + ko, :], vec[:, 6:7], chunk(xT, c),
                                                                   ALU.add, ALU.add), mo)
                ro.free(ko, o)
                done.append(o)
            return done

        @phase
        def normed(ready, twice=False):
            bar = barrier()

            def put(c, ps, rs, w):
                v = V(lambda e: e.tensor_tensor(chunk(yT, c), ps, rs, ALU.mult), w, bar)
                o = split(chunk(HH, c), chunk(HL, c), chunk(yT, c), A, G, v) if twice else None
                return v, [v, o]

            return layernorm(plain(xs[1], ready, bar), bar, put)

        r = normed(x_parts, True)
        r = self_attention(r)
        r = ffn(normed(r), False)
        r = weighted_values(normed(r))
        r = ffn(normed(r), True)

        bar = barrier()
        scopes.append(ExitStack())
        ob = [arena(512, [4, 128]) for _ in range(8)]
        od = out.rearrange("b (t p) d -> p (b t) d", p=128)
        s_out = sem("s_out")
        for g in range(8):
            for j in range(4):
                mm = T(lambda e, g=g, j=j: e.transpose(PS[:, g, j * 128:(j + 1) * 128],
                                                       chunk(xs[1], g)[:, j * 128:(j + 1) * 128], ident), r[g], bar)
            o = (V if g % 2 else A)(lambda e, g=g: (e.tensor_copy if g % 2 else e.copy)(
                ob[g].rearrange("p a b -> p (a b)"), PS[:, g, :]), mm, bar)
            Q.op("sync", lambda e, g=g: e.dma_start(od[:, 4 * g:4 * g + 4, :], ob[g]).then_inc(s_out, 16), o)
        Q.op("sync", lambda e: e.wait_ge(s_out, 128))

        scopes.pop().close()
        xs[0].close()
        block = ctx.enter_context(nc.Block())
        Q.emit(block, sems)


def rope_tables():
    f = np.float32
    half = np.arange(0, DH, 2, dtype=f)
    inv = (f(1.0) / np.power(f(10000.0), half / f(DH))).astype(f)
    t = np.arange(N, dtype=f)
    fr = (t[:, None] * inv[None, :]).astype(f).astype(np.float64)
    base = ((half + f(0.4 * DH)) / f(1.4 * DH)).astype(f).astype(np.float64)
    sc = base[None, :] ** ((t.astype(np.float64) - N // 2) / (W // 2))[:, None]
    c, s = np.cos(fr), np.sin(fr)
    dup = lambda x: np.concatenate([x, x], -1)
    sgn = lambda x: np.concatenate([x, -x], -1)
    C = np.stack([dup(8 * c * sc), dup(c / sc)], 1)
    S = np.stack([sgn(8 * s * sc), sgn(s / sc)], 1)
    tab = np.stack([C, S], 0).astype(f).reshape(2, NT, 128, 2, DH)
    return np.ascontiguousarray(tab.transpose(2, 0, 1, 3, 4)).reshape(128, -1)


def constants():
    f = np.float32
    I = np.eye(128, dtype=f)
    sdn = np.zeros((128, 128), f)
    sdn[np.arange(127), np.arange(1, 128)] = 1
    edn = np.zeros((128, 128), f)
    edn[127, 0] = 1
    cst = np.stack([I, I - f(1 / 128), np.full((128, 128), 1 / 128, f), sdn, sdn.T, edn, edn.T], 1)
    i = np.arange(128)[:, None]
    c = np.arange(192)[None, :]
    j = c - 64
    okq = (j <= i) & (i <= j + W)
    okq &= (np.floor_divide(j, W) >= i // W - 1)
    mq = np.where(okq, 0, NEG).astype(f)
    mq0 = np.where(okq & (j >= 0), 0, NEG).astype(f)
    jj, qq = np.arange(128)[:, None], np.arange(192)[None, :]
    okt = (jj <= qq) & (qq <= jj + W) & (jj // W >= qq // W - 1)
    mt = np.where(okt, 0, NEG).astype(f)
    mask = np.concatenate([mq, mq, mq0, mq0, mt, mt], 1)
    sel = np.zeros((8, 8, 128), f)
    for h in range(8):
        sel[h, h] = 1
    return {"c_f32": np.ascontiguousarray(cst), "c_mask": np.ascontiguousarray(mask), "c_sel": sel.reshape(8, 1024),
            "c_rope": rope_tables()}


_INS = ['L0_attn_a_x', 'L0_attn_b_qkv_w', 'L0_attn_b_c1', 'L0_attn_b_c2', 'L0_attn_b_conv1_w', 'L0_attn_b_gn_g',
        'L0_attn_b_gn_b', 'L0_attn_b_conv2_w', 'L0_attn_b_conv2_b', 'L0_attn_b_ch_w1', 'L0_attn_b_ch_b1',
        'L0_attn_b_ch_w2', 'L0_attn_b_ch_b2', 'L0_attn_b_proj_w', 'L0_attn_b_proj_b', 'L0_ffn_wqkv', 'L0_ffn_q_scale',
        'L0_ffn_k_scale', 'L0_ffn_wo', 'L0_ffn_ln_g', 'L0_ffn_ln_b', 'L0_ffn_w1', 'L0_ffn_b1', 'L0_ffn_w2', 'L0_ffn_b2']


def kernel(**inputs):
    import numpy as _np
    import concourse.bacc as _bacc
    from concourse import mybir as _mybir
    from concourse.bass_utils import run_bass_kernel_spmd as _run

    nc = _bacc.Bacc("TRN2", target_bir_lowering=False, num_devices=1)
    arrays, args = {}, {}
    given = {n: _np.ascontiguousarray(inputs[n]) for n in _INS}
    for n in ('L0_attn_b_c1', 'L0_attn_b_c2'):
        given[n] = given[n].reshape(1)
    given.update(constants())
    for name, v in given.items():
        arrays[f"in_{name}"] = v
        args[name] = nc.dram_tensor(f"in_{name}", v.shape, _mybir.dt.from_np(v.dtype), kind="ExternalInput").ap()
    out = nc.dram_tensor("out_x", (NB, N, D), F32, kind="ExternalOutput").ap()
    build(nc, args, out)
    r = _run(nc, [arrays], core_ids=[0])
    return r.results[0]["out_x"]
```

```python
from contextlib import ExitStack

import numpy as np

import concourse.bass as bass
from concourse import mybir

F32 = mybir.dt.float32
BF16 = mybir.dt.bfloat16
F32R = mybir.dt.float32r
ALU = mybir.AluOpType
ACT = mybir.ActivationFunctionType
AX = mybir.AxisListType

NB, N, D = 2, 2048, 128
NT = N // 128
NH, DH, W = 8, 64, 64
HID = 341
CW = [114, 114, 113]
C0 = [0, 114, 228]
CH = 512
NCH = NB * N // CH
EPS = 1e-5
NF = 3
NEG = -1e30


class Op:

    def __init__(self, eng, fn, waits):
        self.eng, self.fn, self.waits, self.mark, self.table = eng, fn, waits, None, False


class Load:

    def __init__(self, sem, value):
        self.sem, self.value = sem, value


class Queues:

    def __init__(self):
        self.q = {e: [] for e in ("sync", "tensor", "vector", "scalar", "gpsimd")}
        self.dma_sems = 0

    def op(self, eng, fn, *waits):
        flat = []
        todo = list(waits)
        while todo:
            w = todo.pop()
            if w is None:
                continue
            if isinstance(w, (list, tuple)):
                todo += w
            else:
                flat.append(w)
        o = Op(eng, fn, flat)
        self.q[eng].append(o)
        return o

    def last(self):
        return [[o for o in q if not o.table][-1:] for e, q in self.q.items() if e != "sync"]

    def emit(self, block, sems):
        for q in self.q.values():
            for o in q:
                for w in o.waits:
                    if isinstance(w, Op):
                        w.mark = 0
        for e, q in self.q.items():
            n = 0
            for o in q:
                if o.mark is not None and not isinstance(o.fn, Load):
                    n += 1
                    o.mark = n

        def run(eng, name):
            seen = {}
            for o in self.q[name]:
                for w in o.waits:
                    key, value = (w.eng, w.mark) if isinstance(w, Op) else (id(w.sem), w.value)
                    if seen.get(key, 0) >= value:
                        continue
                    seen[key] = value
                    eng.wait_ge(sems[w.eng] if isinstance(w, Op) else w.sem, value)
                ins = o.fn(eng)
                if o.mark is not None:
                    ins.then_inc(sems[name], 1)

        block.sync(lambda eng: run(eng, "sync"))
        block.tensor(lambda eng: run(eng, "tensor"))
        block.vector(lambda eng: run(eng, "vector"))
        block.scalar(lambda eng: run(eng, "scalar"))
        block.gpsimd(lambda eng: run(eng, "gpsimd"))


class Ring:

    def __init__(self, n, start=None):
        self.n, self.i, self.held = n, 0, [start] * n

    def take(self):
        k = self.i % self.n
        self.i += 1
        return k, self.held[k]

    def free(self, k, *ops):
        self.held[k] = list(ops)


def build(nc, a, out):
    ctx = ExitStack()
    with ctx:
        def sb(name, shape, dt=F32):
            return ctx.enter_context(nc.sbuf_tensor(name, shape, dt))

        def sem(name):
            return ctx.enter_context(nc.semaphore(name))

        sems = {e: sem("c_" + e) for e in ("sync", "tensor", "vector", "scalar", "gpsimd")}
        Q = Queues()

        def T(fn, *w):
            return Q.op("tensor", fn, *w)

        def V(fn, *w):
            return Q.op("vector", fn, *w)

        def A(fn, *w):
            return Q.op("scalar", fn, *w)

        def G(fn, *w):
            return Q.op("gpsimd", fn, *w)

        def tables():
            A(lambda e: e.preload_act_table_set("natural_log_exp_and_others")).table = True

        n_loads = [0]

        def load(pairs, *w):
            s = sem(f"d{n_loads[0]}")
            n_loads[0] += 1
            for dst, src in pairs:
                Q.op("sync", lambda e, dst=dst, src=src: e.dma_start(dst, src).then_inc(s, 16), *w)
                w = ()
            return Load(s, 16 * len(pairs))

        yT = sb("yT", [128, NB, N])
        HH = sb("HH", [128, NB, N + 4], F32R)
        HL = sb("HL", [128, NB, N + 4], F32R)
        TB = sb("TB", [128, 2, 2, NT, 2, DH])
        wqh = sb("wqh", [128, 3 * NH * DH], F32R)
        wql = sb("wql", [128, 3 * NH * DH], F32R)
        wo = sb("wo", [128, 4, D])
        w1 = sb("w1", [128, 2 * HID])
        w2 = sb("w2", [114, 3, D])
        wb = sb("wb", [128, 3 * D])
        wp = sb("wp", [128, D])
        cw1 = sb("cw1", [128, 32])
        cw2 = sb("cw2", [32, D])
        cst = sb("cst", [128, 7, 128])
        cenr = sb("cenr", [128, 128], F32R)
        mk = sb("mk", [128, 2, 384], BF16)
        idb = sb("idb", [128, 128], BF16)
        sel = sb("sel", [74, 8, 128], BF16)
        mwin = sb("mwin", [74, 192], BF16)
        mid = sb("mid", [128, 256], BF16)
        qks = sb("qks", [128, 2, 2, DH])
        b1c = sb("b1c", [114, 2, 6])
        b1r = sb("b1r", [114, 6])
        vec = sb("vec", [128, 64])
        cstv = sb("cstv", [128, 4])
        ident, cen, avg, sdn, sup, edn, eup = (cst[:, i, :] for i in range(7))
        PS = ctx.enter_context(nc.psum_tensor("PS", [128, 8, 512], F32))
        xsave = nc.dram_tensor("xsave", (128, NB * N), F32, kind="Internal").ap()

        scopes = []
        names = [0]

        def arena(n, shape, dt=F32, parts=128):
            names[0] += 1
            t = scopes[-1].enter_context(nc.sbuf_tensor(f"t{names[0]}", [parts] + list(shape), dt))
            return t[tuple(slice(None) for _ in range(len(shape) + 1))]

        def phase(f):
            def g(*args):
                scopes.append(ExitStack())
                with scopes[-1]:
                    r = f(*args)
                scopes.pop()
                return r
            return g

        def halves(out, a, b, w, more=(), last=True):
            (ah, al), (bh, bl) = a, b
            T(lambda e: e.matmul(out, ah, bh, start=not more, stop=False, skip_group_check=True), w)
            T(lambda e: e.matmul(out, ah, bl, start=False, stop=False, skip_group_check=True))
            return T(lambda e: e.matmul(out, al, bh, start=False, stop=last, skip_group_check=True))

        def split(hi, lo, src, e_hi, e_lo, *w):
            o = e_hi(lambda e: (e.copy if e_hi is A else e.tensor_copy)(hi, src), *w)
            return [o, e_lo(lambda e: e.tensor_tensor(lo, src, hi.bitcast(F32) if hi.dtype == F32R else hi,
                                                      ALU.subtract), o, *w)]

        xs = [ExitStack(), None]

        def take_x():
            names[0] += 1
            xs[1] = xs[0].enter_context(nc.sbuf_tensor(f"x{names[0]}", [128, NB, N], F32))

        take_x()
        scopes.append(ExitStack())
        xtok = arena(0, [NB * NT, D])
        mkf = arena(0, [768])
        self32 = arena(0, [1024 + 192], F32, 74)
        mid32 = arena(0, [256])
        xd = a["L0_attn_a_x"].rearrange("b (t p) d -> p (b t) d", p=128)
        ld_cst = load([(cst[:, :, :], a["c_f32"])])
        ld_x = [load([(xtok[:, 8 * i:8 * i + 8, :], xd[:, 8 * i:8 * i + 8, :])]) for i in range(4)]
        ld_mk = load([(mkf, a["c_mask"]), (self32, a["c_sel"]), (mid32, a["c_mid"])])
        bc = lambda ap, n: ap.rearrange("(o n) -> o n", o=1).to_broadcast([128, n])
        ld_tb = load([(TB[:, 1, :, :, :, :].rearrange("p a b c d -> p (a b c d)"), a["c_rope"]),
                      (qks[:, :, 0, :], a["L0_ffn_q_scale"].rearrange("(o l) d -> o l d", o=1).to_broadcast([128, 2, DH])),
                      (qks[:, :, 1, :], a["L0_ffn_k_scale"].rearrange("(o l) d -> o l d", o=1).to_broadcast([128, 2, DH]))])
        col = lambda ap: ap.rearrange("(p o) -> p o", o=1)
        small = []
        for l in range(2):
            small += [(vec[:, l:l + 1], col(a["L0_ffn_ln_g"][l])), (vec[:, 2 + l:3 + l], col(a["L0_ffn_ln_b"][l])),
                      (vec[:, 4 + l:5 + l], col(a["L0_ffn_b2"][l]))]
            for g in range(2):
                for i in range(3):
                    s0 = HID * g + C0[i]
                    small.append((b1c[0:CW[i], l, 3 * g + i:3 * g + i + 1], col(a["L0_ffn_b1"][l, s0:s0 + CW[i]])))
        small += [(vec[:, 6:7], col(a["L0_attn_b_proj_b"])), (vec[:, 7:8], col(a["L0_attn_b_ch_b2"])),
                  (vec[0:32, 8:9], col(a["L0_attn_b_ch_b1"])),
                  (vec[:, 9:10], bc(a["L0_attn_b_c1"], 1)), (vec[:, 10:11], bc(a["L0_attn_b_c2"], 1)),
                  (vec[:, 12:24], bc(a["L0_attn_b_conv1_w"].rearrange("a b c -> (a b c)"), 12)),
                  (vec[:, 24:28], bc(a["L0_attn_b_gn_g"], 4)), (vec[:, 28:32], bc(a["L0_attn_b_gn_b"], 4)),
                  (vec[:, 32:44], bc(a["L0_attn_b_conv2_w"].rearrange("a b c -> (a b c)"), 12)),
                  (vec[:, 44:45], bc(a["L0_attn_b_conv2_b"], 1)),
                  (wb[:, :], a["L0_attn_b_qkv_w"]), (wp[:, :], a["L0_attn_b_proj_w"]),
                  (cw1[:, :], a["L0_attn_b_ch_w1"]), (cw2[:, :], a["L0_attn_b_ch_w2"])]
        ld_small = load(small)
        wait_attn_w = [None]
        wait_ffn_w = [None]

        def load_attn_w(l, stage, *w):
            ld = load([(stage, a["L0_ffn_wqkv"][l]),
                       (wo[:, :, :], a["L0_ffn_wo"][l].rearrange("(c p) d -> p c d", p=128))], *w)
            wait_attn_w[0] = [ld] + split(wqh[:, :], wql[:, :], stage, V, G, ld, *w)

        def load_ffn_w(l, *w):
            wait_ffn_w[0] = load([(w1[:, :], a["L0_ffn_w1"][l])] +
                                 [(w2[0:CW[i], i, :], a["L0_ffn_w2"][l, C0[i]:C0[i] + CW[i], :]) for i in range(3)], *w)

        load_ffn_w(0)

        tables()
        t1 = V(lambda e: e.tensor_copy(idb[:, :], ident), ld_cst)
        t3 = V(lambda e: e.memset(cstv[:, 0:1], EPS))
        t4 = V(lambda e: e.memset(cstv[:, 1:2], -64.0))
        t5 = V(lambda e: e.tensor_copy(cenr[:, :], cen), ld_cst)
        eps_ap = cstv[:, 0:1]

        def barrier():
            return Q.last()

        ring = Ring(8)
        x_parts = []
        for g in range(8):
            k, held = ring.take()
            for j in range(4):
                mm = T(lambda e, g=g, j=j, k=k: e.transpose(PS[:, k, j * 128:(j + 1) * 128], xtok[:, 4 * g + j, :], ident),
                       ld_cst, ld_x[g // 2], held)
            dst = xs[1][:, g // 4, (g % 4) * 512:(g % 4 + 1) * 512]
            x_parts.append(V(lambda e, k=k, dst=dst: e.tensor_copy(dst, PS[:, k, :]), mm))
        t0 = V(lambda e: e.tensor_copy(mk[:, :, :].rearrange("p a b -> p (a b)"), mkf), ld_mk)
        t2 = V(lambda e: e.tensor_copy(sel[:, :, :].rearrange("p a b -> p (a b)"), self32[:, 0:1024]), ld_mk)
        t6 = V(lambda e: e.tensor_copy(mwin[:, :], self32[:, 1024:1216]), ld_mk)
        t7 = V(lambda e: e.tensor_copy(mid[:, :], mid32), ld_mk)
        k_consts = [t0, t1, t2, t3, t4, t5, t6, t7]
        scopes.pop().close()

        def chunk(t, c):
            return t[:, c // 4, (c % 4) * CH:(c % 4 + 1) * CH]

        def layernorm(ready, banks, put, more=lambda: None):
            sq = [arena(CH, [CH]) for _ in range(3)]
            rs = [arena(CH, [CH]) for _ in range(3)]
            free = banks.held[1]
            ps, rsq, rrs = banks, Ring(3, free), Ring(3, free)
            done = []
            held = []
            late = []
            for c in range(NCH + 3):
                if c < NCH:
                    more()
                    kc, h = ps.take()
                    T(lambda e, c=c, kc=kc: e.matmul(PS[:, kc, :], cenr[:, :], chunk(HH, c), start=True, stop=False),
                      ready[c], h, t5)
                    m1 = T(lambda e, c=c, kc=kc: e.matmul(PS[:, kc, :], cenr[:, :], chunk(HL, c), start=False, stop=True))
                    ks, h = rsq.take()
                    s1 = A(lambda e, kc=kc, ks=ks: e.activation(sq[ks], PS[:, kc, :], ACT.Square), m1, h)
                    held.append((c, kc, ks, s1))
                if late:
                    done.append(late.pop()())
                if 2 <= c < NCH + 2:
                    cc, kc, ks, s1 = held[c - 2]
                    kv, h = ps.take()
                    m2 = T(lambda e, kv=kv, ks=ks: e.matmul(PS[:, kv, :], avg, sq[ks], start=True, stop=True), s1, h)
                    rsq.free(ks, m2)
                    kr, h = rrs.take()
                    s2 = A(lambda e, kv=kv, kr=kr: e.activation(rs[kr], PS[:, kv, :], ACT.Ln, bias=eps_ap), m2, h, t3)
                    ps.free(kv, s2)
                    s3 = A(lambda e, kr=kr: e.activation(rs[kr], rs[kr], ACT.Exp, scale=-0.5), s2)
                    v, rest = put(cc, PS[:, kc, :], rs[kr], s3)
                    ps.free(kc, v)
                    rrs.free(kr, v)
                    late.append(rest)
            return done

        @phase
        def self_attention(ready):
            xT = xs[1]
            bar = barrier()
            ntok = arena(0, [NT, 128])
            nf = [arena(0, [128]) for _ in range(3)]
            nh = [arena(0, [128], F32R) for _ in range(3)]
            nl = [arena(0, [128], F32R) for _ in range(3)]
            E = [arena(0, [1024]) for _ in range(2)]
            Eh = [arena(0, [N], F32R) for _ in range(3)]
            El = [arena(0, [N], F32R) for _ in range(3)]
            zz = arena(0, [12])
            stage = arena(0, [1536])
            out_ops = []

            def sequence(b):
                tr = []
                before = out_ops[-4:]
                for g in range(4):
                    for j in range(4):
                        t = 4 * g + j
                        mm = T(lambda e, g=g, j=j, t=t: e.transpose(PS[:, 4 + g, j * 128:(j + 1) * 128],
                                                                 yT[:, b, t * 128:(t + 1) * 128], ident),
                               bar, ready[4 * b + g], before)
                    tr.append(V(lambda e, g=g: e.tensor_copy(ntok[:, 4 * g:4 * g + 4, :].rearrange("p a b -> p (a b)"),
                                                            PS[:, 4 + g, :]), mm, bar))
                ex, pv, scl, lows = {}, {}, {}, {}

                def scores(m, h):
                    for j in range(2):
                        o = PS[:, 2 * h + j, :]
                        ms = slice(m * 128, (m + 1) * 128)
                        ns = slice((2 * h + j) * 512, (2 * h + j + 1) * 512)
                        mm = halves(o, (HH[:, b, ms], HL[:, b, ms]), (HH[:, b, ns], HL[:, b, ns]),
                                    [ex.get((m - 1, h)), bar, ready])
                    ex[m, h] = A(lambda e: e.activation(
                        E[h], PS[:, 2 * h:2 * h + 2, :].rearrange("p a b -> p (a b)"),
                        ACT.Exp, bias=cstv[:, 1:2], accum_out=zz[:, 2 * (m % 3) + h:2 * (m % 3) + h + 1]),
                        mm, lows.get((m - 1, h)), scl.get(m - 3), t4, bar)
                    hs = slice(h * 1024, (h + 1) * 1024)
                    lows[m, h] = split(Eh[m % 3][:, hs], El[m % 3][:, hs], E[h], A, V, ex[m, h], pv.get(m - 3))

                def normalise(m):
                    q = m % 3
                    s = V(lambda e: e.tensor_tensor(zz[:, 6 + q:7 + q], zz[:, 2 * q:2 * q + 1], zz[:, 2 * q + 1:2 * q + 2],
                                                    ALU.add), ex[m, 0], ex[m, 1], scl.get(m - 3))
                    r = V(lambda e: e.reciprocal(zz[:, 9 + q:10 + q], zz[:, 6 + q:7 + q]), s)
                    f = V(lambda e: e.tensor_scalar(nf[q], ntok[:, m, :], zz[:, 9 + q:10 + q], None, ALU.mult),
                          r, tr[m // 4], pv.get(m - 3), scl.get(m - 3))
                    scl[m] = split(nh[q], nl[q], nf[q], V, V, f)

                def weighted(m, h):
                    for j in (2 * h, 2 * h + 1):
                        js = slice(j * 512, (j + 1) * 512)
                        (ah, al), (bh, bl) = (nh[m % 3], nl[m % 3]), (Eh[m % 3][:, js], El[m % 3][:, js])
                        o = PS[:, 4 + j, :]
                        w = [scl[m], lows[m, j // 2], tr]
                        T(lambda e, o=o, ah=ah, bh=bh: e.matmul(o, ah, bh, start=(m == 0), stop=False), w)
                        T(lambda e, o=o, ah=ah, bl=bl: e.matmul(o, ah, bl, start=False, stop=False))
                        mm = T(lambda e, o=o, al=al, bh=bh: e.matmul(o, al, bh, start=False, stop=(m == NT - 1)))
                    pv[m] = mm

                for m in range(NT + 2):
                    for h in range(2):
                        if m < NT:
                            scores(m, h)
                        if m >= 2:
                            weighted(m - 2, h)
                    if m < NT:
                        normalise(m)
                for j in range(4):
                    dst = xT[:, b, j * 512:(j + 1) * 512]
                    out_ops.append(V(lambda e, j=j, dst=dst: e.tensor_tensor(dst, PS[:, 4 + j, :], dst, ALU.add),
                                     pv[NT - 1]))

            ld_w = load([(stage, a["L0_ffn_wqkv"][0]),
                         (wo[:, :, :], a["L0_ffn_wo"][0].rearrange("(c p) d -> p c d", p=128))], bar)
            sequence(0)
            wait_attn_w[0] = [ld_w] + split(wqh[:, :], wql[:, :], stage, V, G, ld_w, bar)
            sequence(1)
            return out_ops

        def shift(ready, done, n):
            for c in range(len(done), min(NCH, len(done) + n)):
                b, n0 = c // 4, (c % 4) * CH
                w = ready[c:c + 2]
                z = [V(lambda e, t=t, b=b: e.tensor_scalar(t[64:128, b, 0:1], vec[64:128, 0:1], 0.0, None, ALU.mult),
                       w, ld_small) for t in (HH, HL)] if n0 == 0 else None
                o = split(HH[0:64, b, n0:n0 + CH], HL[0:64, b, n0:n0 + CH], yT[0:64, b, n0:n0 + CH], V, V, w)
                o2 = split(HH[64:128, b, n0 + 1:n0 + 1 + CH], HL[64:128, b, n0 + 1:n0 + 1 + CH],
                           yT[64:128, b, n0:n0 + CH], V if c % 2 else A, V, w)
                done.append([o, o2, z, done[-1][1:] if c % 4 else None])

        def plain(src, ready, free):
            return [split(chunk(HH, c), chunk(HL, c), chunk(src, c), A, V if c % 2 else G, ready[c], free)
                    for c in range(NCH)]

        @phase
        def local_attention(l, ready, saved):
            bar = [barrier(), saved]
            h_ready = []
            shift(ready, h_ready, 2)
            sq = arena(1024, [NH * 2, DH])
            qn = arena(1024, [NH * 2, DH])
            ta = [arena(1024, [NH * 2, DH]) for _ in range(2)]
            tc = arena(1024, [NH * 2, DH])
            ss = arena(64, [2, 32])
            RQ = 8
            qH = arena(0, [4, RQ * 128 + 64], BF16)
            qL = arena(0, [4, RQ * 128 + 64], BF16)
            kH = arena(0, [4, RQ * 128 + 64], BF16)
            kL = [arena(0, [4, 128], BF16) for _ in range(4)]
            va = [arena(1024, [4, 256]) for _ in range(2)]
            PT = [arena(384, [2, 192]) for _ in range(5)]
            ND = [[arena(768, [2, 2, 192]) for _ in range(2)] for _ in range(2)]
            mx = [arena(8, [8]) for _ in range(2)]
            mT = arena(0, [RQ, 192], BF16, 74)
            mT_rest = V(lambda e: e.tensor_copy(mT, mwin[:, 0:192].rearrange("p (o n) -> p o n", o=1)
                                                .to_broadcast([74, RQ, 192])), bar)
            lnd = [arena(256, [2, 128]) for _ in range(2)]
            ot = [arena(512, [4, 128]) for _ in range(2)]
            ones = [V(lambda e, i=i: e.memset(va[i][:, :, 64:192], 1.0), bar) for i in range(2)]
            zk = V(lambda e: e.memset(kH[:, :, 0:64], 0.0), bar)
            ra, rm, rs, rv = Ring(3, bar), Ring(2, bar), Ring(2, bar), Ring(1, bar)
            rqn, rta, rtc, rsq, rss = Ring(1, bar), Ring(2, bar), Ring(1, bar), Ring(1, bar), Ring(2, bar)
            rkL, rva, rPT, rmx, rlnd, rot = (Ring(4, bar), Ring(2, bar), Ring(5, bar), Ring(2, bar), Ring(2, bar),
                                             Ring(2, bar))
            wait_w = wait_attn_w[0]
            R = {}
            tiles = [(b, t) for b in range(NB) for t in range(NT)]
            nt = len(tiles)

            def project(i):
                b, t = tiles[i]
                ops = []
                banks = []
                for x in range(2):
                    k, h = ra.take()
                    ts, xsl = slice(t * 128, (t + 1) * 128), slice(x * 512, (x + 1) * 512)
                    ops.append(halves(PS[:, k, :], (HH[:, b, ts], HL[:, b, ts]), (wqh[:, xsl], wql[:, xsl]),
                                      [h, h_ready[i // 4], wait_w, bar]))
                    banks.append(k)
                ks, h = rsq.take()
                a1 = [A(lambda e, x=x: e.activation(sq[:, 8 * x:8 * x + 8, :].rearrange("p a b -> p (a b)"),
                                                    PS[:, banks[x], :], ACT.Square), ops[x], h) for x in range(2)]
                R["p", i] = (ops, banks, ks, a1)

            def norms(i):
                ops, banks, ks, a1 = R["p", i]
                kss, h2 = rss.take()
                v1 = V(lambda e: e.tensor_reduce(ss[:, kss, 0:16], sq, AX.X, ALU.add), a1, h2)
                rsq.free(ks, v1)
                v2 = V(lambda e: e.tensor_scalar(ss[:, kss, 0:16], ss[:, kss, 0:16], 1e-24, None, ALU.max), v1)
                a2 = A(lambda e: e.activation(ss[:, kss, 16:32], ss[:, kss, 0:16], ACT.Ln), v2)
                a3 = A(lambda e: e.activation(ss[:, kss, 16:32], ss[:, kss, 16:32], ACT.Exp, scale=-0.5), a2)
                R["ss", i] = (kss, a3)

            def rope(i):
                b, t = tiles[i]
                ops, banks, _, _ = R.pop(("p", i))
                kss, a3 = R.pop(("ss", i))
                _, h = rqn.take()
                v3 = [V(lambda e, x=x: e.tensor_tensor(
                    qn[:, 8 * x:8 * x + 8, :], PS[:, banks[x], :].rearrange("p (a b) -> p a b", b=DH),
                    ss[:, kss, 16 + 8 * x:24 + 8 * x].rearrange("p (a o) -> p a o", o=1).to_broadcast([128, NH, DH]), ALU.mult),
                    a3, h) for x in range(2)]
                ra.free(banks[0], v3[0])
                ra.free(banks[1], v3[1])
                rss.free(kss, v3)
                ka, h = rta.take()
                kc, h2 = rtc.take()
                qv = qn.rearrange("p (x h) d -> p x h d", x=2)
                tab = lambda c: TB[:, l, c, t, :, :].rearrange("p x (o d) -> p x o d", o=1).to_broadcast([128, 2, NH, DH])
                v4 = V(lambda e: e.tensor_tensor(ta[ka].rearrange("p (x h) d -> p x h d", x=2), qv, tab(0), ALU.mult),
                       v3, h, tb_ready)
                g1 = G(lambda e: e.tensor_tensor(tc.rearrange("p (x h) d -> p x h d", x=2), qv, tab(1), ALU.mult),
                       v3, h2, tb_ready)
                rqn.free(0, v4, g1)
                tv = ta[ka]
                g2 = [G(lambda e, s=s: e.tensor_tensor(tv[:, :, 32 * s:32 * s + 32], tv[:, :, 32 * s:32 * s + 32],
                                                       tc[:, :, 32 * (1 - s):32 * (1 - s) + 32], ALU.add), v4, g1)
                      for s in range(2)]
                rtc.free(kc, g2)
                R["r", i] = (ka, g2)

            def turn(i, x):
                b, t = tiles[i]
                ka, g2 = R["r", i]
                k, h = ra.take()
                for j in range(4):
                    mm = T(lambda e, j=j: e.transpose(
                        PS[:, k, j * 128:(j + 1) * 128],
                        ta[ka][:, 8 * x + 2 * j:8 * x + 2 * j + 2, :].rearrange("p a b -> p (a b)"), ident), h, g2)
                src = PS[:, k, :].rearrange("p (a b) -> p a b", b=128)
                c0 = (i % RQ) * 128
                w = [bar, R.get(("S", i - RQ)), R.get(("S", i - RQ - 1)), R.get(("Mw", i - RQ)),
                     R.get(("Mw", i - RQ + 1))]
                if x == 0:
                    o = split(qH[:, :, c0:c0 + 128], qL[:, :, c0:c0 + 128], src, A, V, mm, w)
                    if i % RQ == 0 and i > 0:
                        ce = RQ * 128
                        o2 = A(lambda e: e.copy(qH[:, :, ce:ce + 64], src[:, :, 0:64]), mm, w, o)
                        o3 = V(lambda e: e.tensor_tensor(qL[:, :, ce:ce + 64], src[:, :, 0:64], qH[:, :, ce:ce + 64],
                                                         ALU.subtract), o2)
                        o += [o2, o3]
                    R["q", i] = o
                    ra.free(k, o)
                else:
                    kk, h = rkL.take()
                    o = split(kH[:, :, 64 + c0:192 + c0], kL[kk], src, A, V, mm, w, h)
                    if i % RQ == RQ - 1:
                        if t < NT - 1:
                            o.append(A(lambda e: e.copy(kH[:, :, 0:64], src[:, :, 64:128]), mm, w, o))
                        else:
                            o.append(V(lambda e: e.memset(kH[:, :, 0:64], 0.0), w, o))
                    R["k", i] = (kk, o)
                    ra.free(k, o)
                    rta.free(ka, mm)
                    del R["r", i]

            def maxima(i, n):
                g, s = divmod(n, 2)
                b, t = tiles[i]
                c0 = (i % RQ) * 128
                k, h = rm.take()
                need = [R["q", i], R["k", i][1], R["k", i - 1][1] if i else zk]
                T(lambda e: e.matmul(PS[:, 3 + k, 0:384], idb[:, :], mk[:, 0 if t else 1, :], start=True, stop=False,
                                     skip_group_check=True), h, k_consts)
                for c in range(2):
                    mm = T(lambda e, c=c: e.matmul(PS[:, 3 + k, 192 * c:192 * c + 192],
                                                   qH[64 * s:64 * s + 64, 2 * g + c, c0:c0 + 128],
                                                   kH[64 * s:64 * s + 64, 2 * g + c, c0:c0 + 192],
                                                   start=False, stop=True, skip_group_check=True), need)
                if n == 0:
                    R["mx", i] = [rmx.take(), []]
                (km, h), lst = R["mx", i]
                v = V(lambda e: e.tensor_reduce(mx[km][:, 4 * g + s:4 * g + s + 3:2],
                                                PS[:, 3 + k, 0:384].rearrange("p (a b) -> p a b", b=192), AX.X, ALU.max,
                                                negate=True), mm, h)
                rm.free(k, v)
                lst.append(v)
                if n == 3:
                    R["Mw", i] = mm

            def turn_maxima(i):
                (km, _), lst = R.pop(("mx", i))
                k, h = ra.take()
                mm = T(lambda e: e.transpose(PS[0:8, k, 0:128], mx[km], ident), lst, h)
                rmx.free(km, mm)
                c0 = (i % RQ) * 128
                w = [bar, R.get(("S", i - RQ)), R.get(("S", i - RQ - 1))]
                o = [A(lambda e: e.copy(mT[0:8, i % RQ, 0:128], PS[0:8, k, 0:128]), mm, w, mT_rest)]
                if i > 0:
                    o.append(A(lambda e: e.copy(mT[0:8, (i - 1) % RQ, 128:192], PS[0:8, k, 0:64]), mm, w, mT_rest))
                ra.free(k, o)
                R["m", i] = o

            def values(i):
                b, t = tiles[i]
                k, h = ra.take()
                ts = slice(t * 128, (t + 1) * 128)
                mm = halves(PS[:, k, :], (HH[:, b, ts], HL[:, b, ts]), (wqh[:, 1024:1536], wql[:, 1024:1536]),
                            [h, h_ready[i // 4], wait_w, bar])
                kv, h = rva.take()
                src = PS[:, k, :].rearrange("p (a s d) -> p a s d", s=2, d=DH)
                o = [A(lambda e, s=s: e.copy(va[kv][:, :, 192 * s:192 * s + 64], src[:, :, s, :]), mm, h, ones)
                     for s in range(2)]
                ra.free(k, o)
                R["v", i] = (kv, o)

            def scores(i, n):
                g, s = divmod(n, 2)
                b, t = tiles[i]
                nq = 192 if t < NT - 1 else 128
                c0 = (i % RQ) * 128
                kk, okt = R["k", i]
                need = [R["q", i], R["m", i], okt]
                if nq == 192:
                    need += [R["q", i + 1], R["m", i + 1]]
                k, h = rs.take()
                rows = slice(64 * s, 64 * s + 64)
                for c in range(2):
                    T(lambda e, c=c: e.matmul(PS[:, 5 + k, 192 * c:192 * c + nq], sel[:, 4 * g + 2 * c + s, :],
                                              mT[:, i % RQ, 0:nq], start=c == 0, stop=False, skip_group_check=True),
                      need, h, k_consts)
                T(lambda e: e.matmul(PS[:, 5 + k, 0:384].rearrange("p (a b) -> p a b", b=192)[:, :, 64:128],
                                     mid[rows, 0:128], mid[rows, 128:256].rearrange("p (a b) -> p a b", b=64),
                                     start=False, stop=False, skip_group_check=True))
                for c in range(2):
                    p = 2 * g + c
                    kh, kl = kH[rows, p, 64 + c0:192 + c0], kL[kk][rows, p, :]
                    qh, ql = qH[rows, p, c0:c0 + nq], qL[rows, p, c0:c0 + nq]
                    for x, y in ((kh, qh), (kh, ql), (kl, qh)):
                        mm = T(lambda e, c=c, x=x, y=y: e.matmul(PS[:, 5 + k, 192 * c:192 * c + nq], x, y, start=False,
                                                                 stop=True, skip_group_check=True), need)
                kp, h = rPT.take()
                src = PS[:, 5 + k, 0:384].rearrange("p (a b) -> p a b", b=192)[:, :, 0:nq]
                ae = A(lambda e: e.activation(PT[kp][:, :, 0:nq], src, ACT.Exp), mm, h)
                rs.free(k, ae)
                R["e", i, n] = (kp, ae)
                if n == 3:
                    rkL.free(kk, mm)
                    R["S", i] = mm

            def gather(i, n):
                g, s = divmod(n, 2)
                b, t = tiles[i]
                nq = 192 if t < NT - 1 else 128
                kv, ov = R["v", i]
                kp, ae = R.pop(("e", i, n))
                k, h = rv.take()
                for c in range(2):
                    mm = T(lambda e, c=c: e.matmul(PS[:, 7 + k, 192 * c:192 * c + nq],
                                                   va[kv][:, 2 * g + c, 128 * s:128 * s + 128],
                                                   PT[kp][:, c, 0:nq],
                                                   start=True, stop=True, skip_group_check=True), h, ae, ov)
                rPT.free(kp, mm)
                if n == 3:
                    rva.free(kv, mm)
                nd, old = ND[g][i % 2], ND[g][(i + 1) % 2]
                w = R.get(("nd", i - 1, g)), R.get(("nd", i - 2, g)), bar
                lo, hi = slice(64 * s, 64 * s + 64), slice(64 - 64 * s, 128 - 64 * s)
                src = PS[:, 7 + k, 0:384].rearrange("p (a b) -> p a b", b=192)[:, :, 0:nq]
                cp = [A(lambda e: e.copy(nd[lo, 0, :, 0:nq], src[lo, :, :]), mm, w),
                      A(lambda e: e.copy(nd[lo, 1, :, 0:nq], src[hi, :, :]), mm, w)]
                rv.free(k, cp)
                R["cp", i, n] = cp

            def finish(i, g):
                b, t = tiles[i]
                nd, old = ND[g][i % 2], ND[g][(i + 1) % 2]
                cp = R.pop(("cp", i, 2 * g)) + R.pop(("cp", i, 2 * g + 1))
                if t:
                    cp = [V(lambda e: e.tensor_tensor(nd[:, :, :, 0:64], nd[:, :, :, 0:64], old[:, :, :, 128:192], ALU.add),
                            cp)]
                kl, h = rlnd.take()
                a1 = A(lambda e: e.activation(lnd[kl], nd[:, 1, :, 0:128], ACT.Ln), cp, h)
                a2 = A(lambda e: e.activation(lnd[kl], lnd[kl], ACT.Exp, scale=-1.0), a1)
                if g == 0:
                    R["ot", i] = [rot.take(), []]
                (ko, h), lst = R["ot", i]
                o = V(lambda e: e.tensor_tensor(ot[ko][:, 2 * g:2 * g + 2, :], nd[:, 0, :, 0:128], lnd[kl], ALU.mult),
                      a2, cp, h)
                rlnd.free(kl, o)
                R["nd", i, g] = [o, cp]
                lst.append(o)

            def project_out(i):
                b, t = tiles[i]
                (ko, _), lst = R.pop(("ot", i))
                k, h = ra.take()
                for j in range(4):
                    mm = T(lambda e, j=j: e.matmul(PS[:, k, 0:128], wo[:, j, :], ot[ko][:, j, :],
                                                   start=(j == 0), stop=(j == 3)), h, lst, wait_w)
                rot.free(ko, mm)
                dst = yT[:, b, t * 128:(t + 1) * 128]
                o = V(lambda e: e.tensor_tensor(dst, PS[:, k, 0:128], dst, ALU.add), mm, bar)
                ra.free(k, o)
                R["out", i] = o

            for s in range(nt + 7):
                shift(ready, h_ready, 1)

                def on(lag):
                    return 0 <= s - lag < nt

                if on(0):
                    project(s)
                if on(2):
                    maxima(s - 2, 0)
                if on(3):
                    turn_maxima(s - 3)
                if on(5):
                    gather(s - 5, 3)
                if on(4):
                    scores(s - 4, 0)
                if on(0):
                    norms(s)
                if on(2):
                    maxima(s - 2, 3)
                if on(5):
                    finish(s - 5, 1)
                if on(2):
                    maxima(s - 2, 2)
                if on(4):
                    scores(s - 4, 1)
                    gather(s - 4, 0)
                    scores(s - 4, 2)
                if on(0):
                    rope(s)
                if on(4):
                    scores(s - 4, 3)
                if on(2):
                    maxima(s - 2, 1)
                if on(4):
                    gather(s - 4, 1)
                if on(1):
                    turn(s - 1, 0)
                    turn(s - 1, 1)
                if on(4):
                    gather(s - 4, 2)
                if on(3):
                    values(s - 3)
                if on(4):
                    finish(s - 4, 0)
                if on(5):
                    project_out(s - 5)
            return [[R["out", 4 * c + j] for j in range(4)] for c in range(NCH)], T_last(Q)

        def T_last(Q):
            return Q.q["tensor"][-1]

        @phase
        def feed_forward(l, ready, stage_next):
            bar = barrier()
            h_ready = []
            shift(ready, h_ready, 1)
            w1g = arena(0, [2 * HID])
            w1h, w1l = arena(0, [2 * HID], F32R), arena(0, [2 * HID], F32R)
            w2h, w2l = arena(0, [3, D], F32R, 114), arena(0, [3, D], F32R, 114)
            f1 = V(lambda e: e.tensor_scalar(w1g, w1[:, :], vec[:, l:l + 1], None, ALU.mult), wait_ffn_w[0],
                   ld_small, bar)
            fold = split(w1h, w1l, w1g, V, G, f1, bar) + \
                [o for i in range(3) for o in split(w2h[0:CW[i], i, :], w2l[0:CW[i], i, :], w2[0:CW[i], i, :], V, G,
                                                    wait_ffn_w[0], bar)]
            for i in range(6):
                s0 = HID * (i // 3) + C0[i % 3]
                wd = CW[i % 3]
                mm = T(lambda e, i=i, s0=s0, wd=wd: e.matmul(PS[0:wd, 0, i:i + 1], w1[:, s0:s0 + wd], vec[:, 2 + l:3 + l],
                                                            start=True, stop=True), wait_ffn_w[0], ld_small, bar)
            bb = [V(lambda e, i=i: e.tensor_tensor(b1r[0:CW[i % 3], i:i + 1], PS[0:CW[i % 3], 0, i:i + 1],
                                                   b1c[0:CW[i % 3], l, i:i + 1], ALU.add), mm, bar) for i in range(6)]
            nf = [arena(0, [CH]) for _ in range(3)]
            rnf = Ring(3, bar)

            def put(c, ps, rs, w):
                k, h = rnf.take()
                v = V(lambda e: e.tensor_tensor(nf[k], ps, rs, ALU.mult), w, h)

                def rest():
                    o = split(chunk(HH, c), chunk(HL, c), nf[k], A, G, v)
                    rnf.free(k, o)
                    return o

                return v, rest

            banks = Ring(8, bar)
            banks.held[0] = [bar, bb]
            hn = layernorm(h_ready, banks, put, lambda: shift(ready, h_ready, 1))
            gl = [arena(CH, [CH]) for _ in range(NF)]
            hf = [arena(CH, [CH]) for _ in range(NF)]
            hh = [arena(CH, [CH], F32R) for _ in range(6)]
            hl = [arena(CH, [CH], F32R) for _ in range(6)]
            if stage_next is not None:
                stage = arena(0, [1536])
                load_attn_w(stage_next, stage, bar)
            rf, rg, rh = Ring(NF, bar), Ring(NF, bar), Ring(6, bar)
            r6, r2 = Ring(6), Ring(2)
            r6.held, r2.held = banks.held[0:6], banks.held[6:8]
            done = []
            pend = []

            def second(c, items):
                k, h = r2.take()
                for i, (kh, v) in enumerate(items):
                    mm = halves(PS[:, 6 + k, :], (w2h[0:CW[i], i, :], w2l[0:CW[i], i, :]),
                                (hh[kh][0:CW[i], :], hl[kh][0:CW[i], :]), [h, v, fold], more=i > 0, last=i == 2)
                    rh.free(kh, mm)
                dst = chunk(yT, c)
                o = V(lambda e: e.scalar_tensor_tensor(dst, PS[:, 6 + k, :], vec[:, 4 + l:5 + l], dst, ALU.add, ALU.add),
                      mm)
                r2.free(k, o)
                done.append(o)
                return mm

            lastT = None
            waiting = []
            for c in range(NCH + 1):
                if c < NCH:
                    items = []
                    for i in range(3):
                        wd = CW[i]
                        kg, h = r6.take()
                        cs = slice(HID + C0[i], HID + C0[i] + wd)
                        m1 = halves(PS[0:wd, kg, :], (w1h[:, cs], w1l[:, cs]), (chunk(HH, c), chunk(HL, c)),
                                    [h, hn[c], fold])
                        ka, h = r6.take()
                        cs = slice(C0[i], C0[i] + wd)
                        m2 = halves(PS[0:wd, ka, :], (w1h[:, cs], w1l[:, cs]), (chunk(HH, c), chunk(HL, c)), [h])
                        q, h = rg.take()
                        g1 = A(lambda e, i=i, kg=kg, wd=wd, q=q: e.activation(gl[q][0:wd, :], PS[0:wd, kg, :], ACT.Gelu,
                                                                              bias=b1r[0:wd, 3 + i:4 + i]), m1, h, bb)
                        r6.free(kg, g1)
                        kf, h = rf.take()
                        v = V(lambda e, i=i, ka=ka, wd=wd, q=q, kf=kf: e.scalar_tensor_tensor(
                            hf[kf][0:wd, :], PS[0:wd, ka, :], b1r[0:wd, i:i + 1], gl[q][0:wd, :], ALU.add, ALU.mult),
                            m2, g1, h, bb)
                        r6.free(ka, v)
                        rg.free(q, v)
                        if waiting:
                            waiting.pop()()

                        def parts(kf=kf, wd=wd, v=v, items=items):
                            kh, h = rh.take()
                            o = split(hh[kh][0:wd, :], hl[kh][0:wd, :], hf[kf][0:wd, :], A, V, v, h)
                            rf.free(kf, o)
                            items.append((kh, o))

                        waiting.append(parts)
                    pend.append(items)
                if c >= 1:
                    if c == NCH:
                        waiting.pop()()
                    lastT = second(c - 1, pend[c - 1])
            return done, lastT

        n_saved = [0]

        def ffn(x_ready, last):
            s = sem(f"save{n_saved[0]}")
            n_saved[0] += 1
            xT = xs[1]
            Q.op("sync", lambda e: e.dma_start(xsave, xT[:, :, :].rearrange("p b n -> p (b n)")).then_inc(s, 16), x_ready)
            saved = Load(s, 16)
            ready = normed(x_ready)
            xs[0].close()
            for l in range(2):
                ready, lt = local_attention(l, ready, saved)
                end = last and l == 1
                if l == 1:
                    take_x()
                    xT2 = xs[1]
                    back = load([(xT2[:, :, :].rearrange("p b n -> p (b n)"), xsave)], saved, barrier())
                ready, lt = feed_forward(l, ready, None if end else 1 - l)
                if not end:
                    load_ffn_w(1 - l, lt)
                tables()
            res = []
            for c in range(NCH):
                xc = chunk(xs[1], c)
                res.append(V(lambda e, c=c, xc=xc: e.tensor_tensor(xc, xc, chunk(yT, c), ALU.add),
                             ready[c], back))
            return res

        @phase
        def weighted_values(ready):
            xT = xs[1]
            bar = barrier()
            TT = NB * NT
            st = arena(5 * TT, [5, TT])
            dd = [arena(512, [4, 128]) for _ in range(3)]
            d2 = [arena(512, [4, 128]) for _ in range(3)]
            dm = [arena(256, [2, 128]) for _ in range(3)]
            ysum = arena(0, [NCH])
            w = arena(16 * TT, [16, TT])
            h4 = arena(4 * TT, [4, TT])
            h5 = arena(4 * TT, [4, TT])
            sm = arena(32, [32])
            wbr = [arena(512, [4, 128]) for _ in range(2)]
            wbs = [arena(512, [512]) for _ in range(2)]
            vs = [arena(512, [512]) for _ in range(2)]
            wce, wm = arena(0, [2, 128]), arena(0, [2])
            wb2 = wb[:, 0:256].rearrange("p (a b) -> p a b", b=128)
            o = V(lambda e: e.tensor_reduce(wm, wb2, AX.X, ALU.add), ld_small, bar)
            o = V(lambda e: e.tensor_scalar(wm, wm, 1.0 / 128, None, ALU.mult), o)
            o = V(lambda e: e.tensor_tensor(wce, wb2, wm.rearrange("p (a o) -> p a o", o=1).to_broadcast([128, 2, 128]),
                                            ALU.subtract), o)
            rp, rd = Ring(4, bar), Ring(3, bar)
            seq = []
            late = []
            for j in range(TT // 2 + 1):
                if j < TT // 2:
                    b = j // (NT // 2)
                    k, h = rp.take()
                    for s in range(2):
                        n0 = (2 * j + s) % NT * 128
                        T(lambda e, s=s, n0=n0, b=b, k=k: e.matmul(PS[:, k, 256 * s:256 * s + 256], yT[:, b, n0:n0 + 128],
                                                                  wce.rearrange("p a b -> p (a b)"), start=True, stop=True,
                                                                  skip_group_check=True), h, ready, bar, o)
                        mm = T(lambda e, s=s, n0=n0, b=b, j=j: e.matmul(
                            PS[:, 7, 4 * j + 2 * s:4 * j + 2 * s + 2], yT[:, b, n0:n0 + 128], wm, start=True, stop=True,
                            skip_group_check=True))
                    q, h = rd.take()
                    p4 = PS[:, k, :].rearrange("p (a c b) -> p a c b", c=2, b=128)
                    a1 = A(lambda e, q=q, k=k: e.copy(dd[q].rearrange("p a b -> p (a b)"), PS[:, k, :]), mm, h)
                    rp.free(k, a1)
                    dv = dd[q].rearrange("p (a c) b -> p a c b", c=2)
                    a2 = A(lambda e, q=q: e.activation(d2[q], dd[q], ACT.Square), a1, h)
                    g1 = G(lambda e, q=q, dv=dv: e.tensor_tensor(dm[q], dv[:, :, 0, :], dv[:, :, 1, :], ALU.mult), a1, h)
                if late:
                    i, p, a0_, g0_ = late.pop()
                    sg = st[:, 2:4, 2 * i:2 * i + 2].rearrange("p a b -> p b a")
                    v4 = V(lambda e, p=p, sg=sg: e.tensor_reduce(sg, d2[p].rearrange("p (a c) b -> p a c b", c=2), AX.X,
                                                                 ALU.add), a0_, bar)
                    v5 = V(lambda e, p=p, i=i: e.tensor_reduce(st[:, 4, 2 * i:2 * i + 2], dm[p], AX.X, ALU.add), g0_, bar)
                    rd.free(p, v4, v5)
                    seq += [v4, v5]
                late.append((j, q, a2, g1))
            seq.append(V(lambda e: e.tensor_copy(st[:, 0:2, :].rearrange("p a b -> p b a"),
                                                 PS[:, 7, 0:2 * TT].rearrange("p (t a) -> p t a", a=2)), mm, bar))
            sums = []
            for c in range(NCH):
                sums.append(A(lambda e, c=c: e.activation(vs[c % 2], chunk(yT, c), ACT.Copy, accum_out=ysum[:, c:c + 1]),
                              ready[c], bar, sums[-2:]))
            c1, c2 = vec[:, 9:10], vec[:, 10:11]
            prev = [seq + [bar]]

            def V1(fn, *more):
                prev[0] = V(fn, prev[0], *more)
                return prev[0]

            mq, mkk, sq2, sk2, sqk = (st[:, i, :] for i in range(5))
            i127 = 1.0 / 127
            V1(lambda e: e.tensor_tensor(w[:, 0, :], mq, mkk, ALU.mult))
            V1(lambda e: e.tensor_scalar(w[:, 0, :], w[:, 0, :], 2.0, c1, ALU.mult, ALU.add))
            V1(lambda e: e.tensor_scalar(w[:, 1, :], sqk, 2.0 * i127, c2, ALU.mult, ALU.add))
            V1(lambda e: e.tensor_tensor(w[:, 0, :], w[:, 0, :], w[:, 1, :], ALU.mult))
            V1(lambda e: e.tensor_tensor(w[:, 1, :], mq, mq, ALU.mult))
            V1(lambda e: e.tensor_tensor(w[:, 2, :], mkk, mkk, ALU.mult))
            V1(lambda e: e.scalar_tensor_tensor(w[:, 1, :], w[:, 1, :], c1, w[:, 2, :], ALU.add, ALU.add))
            V1(lambda e: e.tensor_tensor(w[:, 2, :], sq2, sk2, ALU.add))
            V1(lambda e: e.tensor_scalar(w[:, 2, :], w[:, 2, :], i127, c2, ALU.mult, ALU.add))
            V1(lambda e: e.tensor_tensor(w[:, 1, :], w[:, 1, :], w[:, 2, :], ALU.mult))
            V1(lambda e: e.tensor_scalar(w[:, 1, :], w[:, 1, :], 1e-7, None, ALU.add))
            V1(lambda e: e.reciprocal(w[:, 2, :], w[:, 1, :]))
            V1(lambda e: e.tensor_tensor(w[:, 0, :], w[:, 0, :], w[:, 2, :], ALU.mult))
            va_ = V1(lambda e: e.tensor_tensor(w[:, 3, :], w[:, 0, :], w[:, 0, :], ALU.mult))

            def neighbours(src, nch, bank, *wait):
                view = lambda ap: ap.rearrange("p (c b t) -> p c b t", b=NB, t=NT)
                s = view(src)
                ops = []
                for d, (m, ed) in enumerate(((sdn, edn), (sup, eup))):
                    o = PS[:, bank + d, 0:nch * TT]
                    ov = view(o)
                    T(lambda e, o=o, m=m: e.matmul(o, m, src, start=True, stop=False, skip_group_check=True), wait)
                    do = ov[:, :, :, 1:NT] if d == 0 else ov[:, :, :, 0:NT - 1]
                    di = s[:, :, :, 0:NT - 1] if d == 0 else s[:, :, :, 1:NT]
                    mm = T(lambda e, do=do, di=di, ed=ed: e.matmul(do, ed, di, start=False, stop=True,
                                                                  skip_group_check=True))
                    ops.append(mm)
                return ops

            nb = neighbours(w[:, 3, :], 1, 3, va_, bar)
            for c in range(4):
                wc = lambda k: vec[:, 12 + 3 * c + k:13 + 3 * c + k]
                V1(lambda e, c=c: e.tensor_scalar(h4[:, c, :], w[:, 3, :], vec[:, 13 + 3 * c:14 + 3 * c], None, ALU.mult))
                for k, d in ((0, 0), (2, 1)):
                    V1(lambda e, c=c, k=k, d=d: e.scalar_tensor_tensor(
                        h4[:, c, :], PS[:, 3 + d, 0:TT], vec[:, 12 + 3 * c + k:13 + 3 * c + k], h4[:, c, :],
                        ALU.mult, ALU.add), nb)
            g5 = lambda ap: ap.rearrange("p (g c) (b t) -> p g c b t", g=2, b=NB)

            def group_mean(src, bank, *more):
                for g in range(2):
                    for b in range(NB):
                        V1(lambda e, g=g, b=b: e.tensor_reduce(sm[:, 2 * g + b:2 * g + b + 1], g5(src)[:, g, :, b, :],
                                                               AX.XY, ALU.add), *more)
                m = T(lambda e: e.matmul(PS[:, bank, 0:4], avg, sm[:, 0:4], start=True, stop=True), prev[0])
                return V1(lambda e: e.tensor_scalar(sm[:, 4:8], PS[:, bank, 0:4], 1.0 / 32, None, ALU.mult), m)

            group_mean(h4, 5)
            for g in range(2):
                for b in range(NB):
                    hv = g5(h4)[:, g, :, b, :]
                    V1(lambda e, g=g, b=b, hv=hv: e.tensor_scalar(hv, hv, sm[:, 4 + 2 * g + b:5 + 2 * g + b], None,
                                                                  ALU.subtract))
            V1(lambda e: e.tensor_tensor(h5, h4, h4, ALU.mult))
            v = group_mean(h5, 6)
            a1 = A(lambda e: e.activation(sm[:, 8:12], sm[:, 4:8], ACT.Ln, bias=eps_ap), v)
            a2 = A(lambda e: e.activation(sm[:, 12:16], sm[:, 8:12], ACT.Exp, scale=-0.5), a1)
            for g in range(2):
                for b in range(NB):
                    hv = g5(h4)[:, g, :, b, :]
                    V1(lambda e, g=g, b=b, hv=hv: e.tensor_scalar(hv, hv, sm[:, 12 + 2 * g + b:13 + 2 * g + b], None,
                                                                  ALU.mult), a2)
            for c in range(4):
                V1(lambda e, c=c: e.tensor_scalar(h4[:, c, :], h4[:, c, :], vec[:, 24 + c:25 + c], vec[:, 28 + c:29 + c],
                                                  ALU.mult, ALU.add))
            vh = V1(lambda e: e.tensor_scalar(h4, h4, 0.0, None, ALU.max))
            nb = neighbours(h4.rearrange("p a b -> p (a b)"), 4, 3, vh)
            for c in range(4):
                V1(lambda e, c=c: e.scalar_tensor_tensor(w[:, 3, :], h4[:, c, :], vec[:, 33 + 3 * c:34 + 3 * c], w[:, 3, :],
                                                         ALU.mult, ALU.add))
                for k, d in ((0, 0), (2, 1)):
                    V1(lambda e, c=c, k=k, d=d: e.scalar_tensor_tensor(
                        w[:, 3, :], PS[:, 3 + d, c * TT:(c + 1) * TT], vec[:, 32 + 3 * c + k:33 + 3 * c + k], w[:, 3, :],
                        ALU.mult, ALU.add), nb)
            v = V1(lambda e: e.tensor_reduce(sm[:, 16:18], ysum.rearrange("p (b c) -> p b c", b=NB), AX.X, ALU.add), sums)
            v = V1(lambda e: e.tensor_scalar(sm[:, 16:18], sm[:, 16:18], 1.0 / N, None, ALU.mult))
            m = T(lambda e: e.matmul(PS[0:32, 5, 0:2], cw1[:, :], sm[:, 16:18], start=True, stop=True), v)
            v = V1(lambda e: e.tensor_scalar(sm[0:32, 18:20], PS[0:32, 5, 0:2], vec[0:32, 8:9], 0.0, ALU.add, ALU.max), m)
            m = T(lambda e: e.matmul(PS[:, 6, 0:2], cw2[:, :], sm[0:32, 18:20], start=True, stop=True), v)
            a0 = A(lambda e: e.activation(sm[:, 20:22], PS[:, 6, 0:2], ACT.Sigmoid, bias=vec[:, 7:8]), m)
            a1 = A(lambda e: e.activation(w[:, 4, :], w[:, 3, :], ACT.Sigmoid, bias=vec[:, 44:45]), prev[0])
            tables()
            a2 = A(lambda e: e.activation(w[:, 5, :], w[:, 4, :], ACT.Exp), a1)
            v = V1(lambda e: e.tensor_reduce(sm[:, 22:24], w[:, 5, :].rearrange("p (b t) -> p b t", b=NB), AX.X, ALU.add), a2)
            m = T(lambda e: e.matmul(PS[:, 5, 0:2], avg, sm[:, 22:24], start=True, stop=True), v)
            v = V1(lambda e: e.tensor_scalar(sm[:, 24:26], PS[:, 5, 0:2], 128.0, None, ALU.mult), m)
            v = V1(lambda e: e.reciprocal(sm[:, 26:28], sm[:, 24:26]))
            for b in range(NB):
                v = V1(lambda e, b=b: e.tensor_scalar(w[:, 6, NT * b:NT * (b + 1)], w[:, 5, NT * b:NT * (b + 1)],
                                                      sm[:, 26 + b:27 + b], None, ALU.mult))
            bar2 = [barrier()]
            rb, rwb, rv3, rws, rvs, ro = (Ring(2, bar2) for _ in range(6))
            done = []
            H = {}
            for c in range(NCH + 2):
                if c < NCH:
                    kv, h = rv3.take()
                    mv = T(lambda e, c=c, kv=kv: e.matmul(PS[:, kv, :], wb[:, 256:384], chunk(yT, c), start=True, stop=True), h)
                    kb, h = rb.take()
                    kw, h2 = rwb.take()
                    v1 = V(lambda e, c=c, kw=kw: e.tensor_copy(
                        wbr[kw], w[:, 6, 4 * c:4 * c + 4].rearrange("p (a o) -> p a o", o=1).to_broadcast([128, 4, 128])),
                        v, h2)
                    for j in range(4):
                        mm = T(lambda e, j=j, kw=kw, kb=kb: e.matmul(PS[:, 2 + kb, 128 * j:128 * j + 128], wbr[kw][:, j, :],
                                                                    ident, start=True, stop=True, skip_group_check=True),
                               v1, h)
                    rwb.free(kw, mm)
                    ks, h = rws.take()
                    a1 = A(lambda e, kb=kb, ks=ks: e.copy(wbs[ks], PS[:, 2 + kb, :]), mm, h)
                    rb.free(kb, a1)
                    H[c] = kv, mv, ks, a1
                if 1 <= c <= NCH:
                    kv, mv, ks, a1 = H[c - 1]
                    b = (c - 1) // 4
                    kz, h = rvs.take()
                    v2 = V(lambda e, kv=kv, ks=ks, kz=kz, b=b: e.scalar_tensor_tensor(
                        vs[kz], PS[:, kv, :], sm[:, 20 + b:21 + b], wbs[ks], ALU.mult, ALU.mult), mv, a1, a0, h)
                    rv3.free(kv, v2)
                    rws.free(ks, v2)
                    ko, h = ro.take()
                    mo = T(lambda e, ko=ko, kz=kz: e.matmul(PS[:, 4 + ko, :], wp[:, :], vs[kz], start=True, stop=True), v2, h)
                    rvs.free(kz, mo)
                    H["o", c - 1] = ko, mo
                if c >= 2:
                    ko, mo = H["o", c - 2]
                    o = V(lambda e, c=c, ko=ko: e.scalar_tensor_tensor(chunk(xT, c - 2), PS[:, 4 + ko, :], vec[:, 6:7],
                                                                       chunk(xT, c - 2), ALU.add, ALU.add), mo)
                    ro.free(ko, o)
                    done.append(o)
            return done

        @phase
        def normed(ready, twice=False):
            bar = barrier()

            def put(c, ps, rs, w):
                v = V(lambda e: e.tensor_tensor(chunk(yT, c), ps, rs, ALU.mult), w, bar)
                return v, lambda: [v, split(chunk(HH, c), chunk(HL, c), chunk(yT, c), A, G, v) if twice else None]

            return layernorm(plain(xs[1], ready, bar), Ring(8, bar), put)

        r = normed(x_parts, True)
        r = self_attention(r)
        tb_ready = []
        for l in range(2):
            for c in range(2):
                dst = TB[:, l, c, :, :, :]
                src = TB[:, 1, c, :, :, :]
                sc = qks[:, l, :, :].rearrange("p a b -> p (a b)")[:, None, :].to_broadcast([128, NT, 2 * DH])
                d2 = dst.rearrange("p t a b -> p t (a b)")
                s2 = src.rearrange("p t a b -> p t (a b)")
                tb_ready.append(G(lambda e, d2=d2, s2=s2, sc=sc: e.tensor_tensor(d2, s2, sc, ALU.mult),
                                  ld_tb, tb_ready[-2:]))
        r = ffn(r, False)
        r = weighted_values(normed(r))
        r = ffn(r, True)

        bar = barrier()
        scopes.append(ExitStack())
        ob = [arena(512, [4, 128]) for _ in range(8)]
        od = out.rearrange("b (t p) d -> p (b t) d", p=128)
        s_out = sem("s_out")
        for g in range(8):
            for j in range(4):
                mm = T(lambda e, g=g, j=j: e.transpose(PS[:, g, j * 128:(j + 1) * 128],
                                                       chunk(xs[1], g)[:, j * 128:(j + 1) * 128], ident), r[g], bar)
            o = (V if g % 2 else A)(lambda e, g=g: (e.tensor_copy if g % 2 else e.copy)(
                ob[g].rearrange("p a b -> p (a b)"), PS[:, g, :]), mm, bar)
            Q.op("sync", lambda e, g=g: e.dma_start(od[:, 4 * g:4 * g + 4, :], ob[g]).then_inc(s_out, 16), o)
        Q.op("sync", lambda e: e.wait_ge(s_out, 128))

        scopes.pop().close()
        xs[0].close()
        block = ctx.enter_context(nc.Block())
        Q.emit(block, sems)


def rope_tables():
    f = np.float32
    half = np.arange(0, DH, 2, dtype=f)
    inv = (f(1.0) / np.power(f(10000.0), half / f(DH))).astype(f)
    t = np.arange(N, dtype=f)
    fr = (t[:, None] * inv[None, :]).astype(f).astype(np.float64)
    base = ((half + f(0.4 * DH)) / f(1.4 * DH)).astype(f).astype(np.float64)
    sc = base[None, :] ** ((t.astype(np.float64) - N // 2) / (W // 2))[:, None]
    c, s = np.cos(fr), np.sin(fr)
    dup = lambda x: np.concatenate([x, x], -1)
    sgn = lambda x: np.concatenate([x, -x], -1)
    C = np.stack([dup(8 * c * sc), dup(c / sc)], 1)
    S = np.stack([sgn(8 * s * sc), sgn(s / sc)], 1)
    tab = np.stack([C, S], 0).astype(f).reshape(2, NT, 128, 2, DH)
    return np.ascontiguousarray(tab.transpose(2, 0, 1, 3, 4)).reshape(128, -1)


def constants():
    f = np.float32
    I = np.eye(128, dtype=f)
    sdn = np.zeros((128, 128), f)
    sdn[np.arange(127), np.arange(1, 128)] = 1
    edn = np.zeros((128, 128), f)
    edn[127, 0] = 1
    cst = np.stack([I, I - f(1 / 128), np.full((128, 128), 1 / 128, f), sdn, sdn.T, edn, edn.T], 1)
    i = np.arange(128)[:, None]
    c = np.arange(192)[None, :]
    j = c - 64
    okq = (j <= i) & (i <= j + W)
    okq &= (np.floor_divide(j, W) >= i // W - 1)
    mq = np.where(okq, 0, NEG).astype(f)
    mq0 = np.where(okq & (j >= 0), 0, NEG).astype(f)
    mask = np.concatenate([mq, mq, mq0, mq0], 1)
    late, early = np.tril(np.ones((64, 64), f), -1), np.triu(np.ones((64, 64), f), 1)
    sel = np.zeros((74, 8, 128), f)
    for h in range(8):
        sel[h, h] = 1
    sel[8:72, :, 0:64] = early[:, None, :]
    sel[8:72, :, 64:128] = late[:, None, :]
    sel[72, :, 64:128] = 1
    sel[73, :, 0:64] = 1
    mwin = np.zeros((74, 192), f)
    mwin[8:72, 0:64] = mwin[8:72, 128:192] = NEG * np.eye(64, dtype=f)
    mwin[72, 0:64] = mwin[73, 128:192] = NEG
    eye = (NEG * np.eye(64)).astype(f)
    mid = np.tile(np.concatenate([late, early, eye, eye], 1), (2, 1))
    sel = np.concatenate([sel.reshape(74, 1024), mwin], 1)
    return {"c_f32": np.ascontiguousarray(cst), "c_mask": np.ascontiguousarray(mask), "c_sel": sel, "c_mid": mid,
            "c_rope": rope_tables()}


_INS = ['L0_attn_a_x', 'L0_attn_b_qkv_w', 'L0_attn_b_c1', 'L0_attn_b_c2', 'L0_attn_b_conv1_w', 'L0_attn_b_gn_g',
        'L0_attn_b_gn_b', 'L0_attn_b_conv2_w', 'L0_attn_b_conv2_b', 'L0_attn_b_ch_w1', 'L0_attn_b_ch_b1',
        'L0_attn_b_ch_w2', 'L0_attn_b_ch_b2', 'L0_attn_b_proj_w', 'L0_attn_b_proj_b', 'L0_ffn_wqkv', 'L0_ffn_q_scale',
        'L0_ffn_k_scale', 'L0_ffn_wo', 'L0_ffn_ln_g', 'L0_ffn_ln_b', 'L0_ffn_w1', 'L0_ffn_b1', 'L0_ffn_w2', 'L0_ffn_b2']


def kernel(**inputs):
    import numpy as _np
    import concourse.bacc as _bacc
    from concourse import mybir as _mybir
    from concourse.bass_utils import run_bass_kernel_spmd as _run

    nc = _bacc.Bacc("TRN2", target_bir_lowering=False, num_devices=1)
    arrays, args = {}, {}
    given = {n: _np.ascontiguousarray(inputs[n]) for n in _INS}
    for n in ('L0_attn_b_c1', 'L0_attn_b_c2'):
        given[n] = given[n].reshape(1)
    given.update(constants())
    for name, v in given.items():
        arrays[f"in_{name}"] = v
        args[name] = nc.dram_tensor(f"in_{name}", v.shape, _mybir.dt.from_np(v.dtype), kind="ExternalInput").ap()
    out = nc.dram_tensor("out_x", (NB, N, D), F32, kind="ExternalOutput").ap()
    build(nc, args, out)
    r = _run(nc, [arrays], core_ids=[0])
    return r.results[0]["out_x"]
```
